# Optimizing a Trainium2 kernel written in Bass

```python
import numpy as np
import jax
import jax.numpy as jnp

def _softmax(x, axis=-1):
    return jax.nn.softmax(x, axis=axis)

def _gelu(x):
    return jax.nn.gelu(x, approximate=True)

def _silu(x):
    return jax.nn.silu(x)

def _sigmoid(x):
    return jax.nn.sigmoid(x)

def _layernorm(x, axis=-1, eps=1e-05):
    m = jnp.mean(x, axis=axis, keepdims=True)
    v = jnp.var(x, axis=axis, keepdims=True)
    return (x - m) / jnp.sqrt(v + eps)

def _scatter_add(tgt, idx, src, axis=0):
    return tgt.at[idx].add(src)

def _segment_sum(src, seg, n):
    return jax.ops.segment_sum(src, seg, n)
kernel_name = 'mk_seq_postln_d2_jaxref_r4_707a5c'

def setup_inputs(seed: int=0):
    np.random.seed(seed)
    _w = jnp.asarray

    def _L0_attn_setup():
        import jax, jax.numpy as jnp
        import numpy as np
        B, S, HID = (4, 256, 256)
        H = 8
        HD = HID // H
        NQ = 8
        RATIO = 0.5
        FF = 4 * HID
        EPS_COS = 1e-08
        LN_EPS = 1e-05

        def _layernorm(x, g, b):
            m = jnp.mean(x, axis=-1, keepdims=True)
            v = jnp.var(x, axis=-1, keepdims=True)
            return (x - m) * jax.lax.rsqrt(v + LN_EPS) * g + b
        key = jax.random.key(seed)
        ks = jax.random.split(key, 24)
        sc = 0.02
        inp = {'x': jax.random.normal(ks[0], (B, S, HID), jnp.float32), 'Wq': jax.random.normal(ks[1], (H, HID, HD)) * sc, 'bq': jnp.zeros((H, HD)), 'Wk': jax.random.normal(ks[2], (H, HID, HD)) * sc, 'bk': jnp.zeros((H, HD)), 'Wv': jax.random.normal(ks[3], (H, HID, HD)) * sc, 'bv': jnp.zeros((H, HD)), 'Wc2q': jax.random.normal(ks[4], (H, HD, NQ)) * sc, 'bc2q': jnp.zeros((H, NQ)), 'Wo': jax.random.normal(ks[5], (HID, HID)) * sc, 'bo': jnp.zeros((HID,)), 'g1': jnp.ones((HID,)), 'beta1': jnp.zeros((HID,)), 'g2': jnp.ones((HID,)), 'beta2': jnp.zeros((HID,)), 'W1': jax.random.normal(ks[6], (HID, FF)) * sc, 'b1': jnp.zeros((FF,)), 'Wm': jax.random.normal(ks[7], (FF, NQ)) * sc, 'bm': jnp.zeros((NQ,)), 'Wqo': jax.random.normal(ks[8], (NQ, FF)) * sc, 'bqo': jnp.zeros((FF,)), 'W2': jax.random.normal(ks[9], (FF, HID)) * sc, 'b2': jnp.zeros((HID,))}
        return inp
    _L0_attn_in = _L0_attn_setup()

    def _L0_ffn_setup():
        import jax, jax.numpy as jnp
        import numpy as np
        DIM = 256
        HIDDEN = 768
        SCALE = 1.0 / 127.0

        def _dequant(w_int, dtype):
            return w_int.astype(dtype) * jnp.asarray(SCALE, dtype)
        key = jax.random.key(seed)
        k_x, k_g, k_u, k_d = jax.random.split(key, 4)
        x = jax.random.normal(k_x, (4, 512, DIM), dtype=jnp.float32)
        w_gate = jax.random.randint(k_g, (HIDDEN, DIM), -127, 128, dtype=jnp.int32)
        w_up = jax.random.randint(k_u, (HIDDEN, DIM), -127, 128, dtype=jnp.int32)
        w_down = jax.random.randint(k_d, (DIM, HIDDEN), -127, 128, dtype=jnp.int32)
        return {'x': x, 'w_gate': w_gate, 'w_up': w_up, 'w_down': w_down}
    _L0_ffn_in = _L0_ffn_setup()

    def _L1_attn_setup():
        import jax, jax.numpy as jnp
        import numpy as np
        from jax import lax
        B, L, D, K = (4, 1024, 256, 3)
        H = 512

        def _layernorm(h, g, b):
            m = jnp.mean(h, axis=-1, keepdims=True)
            v = jnp.mean((h - m) ** 2, axis=-1, keepdims=True)
            return (h - m) / jnp.sqrt(v + 1e-05) * g + b
        key = jax.random.key(seed)
        ks = jax.random.split(key, 16)
        s = 0.02
        return {'x': jax.random.normal(ks[0], (B, L, D), jnp.float32), 'ln1_g': jnp.ones((D,), jnp.float32), 'ln1_b': jnp.zeros((D,), jnp.float32), 'in_W': jax.random.normal(ks[1], (D, 2 * D), jnp.float32) * s, 'in_b': jnp.zeros((2 * D,), jnp.float32), 'dw_W': jax.random.normal(ks[2], (D, 1, K), jnp.float32) * s, 'dw_b': jnp.zeros((D,), jnp.float32), 'dt_W': jax.random.normal(ks[3], (D, D), jnp.float32) * s, 'dt_b': jnp.zeros((D,), jnp.float32), 'b_W': jax.random.normal(ks[4], (D, D), jnp.float32) * s, 'b_b': jnp.zeros((D,), jnp.float32), 'c_W': jax.random.normal(ks[5], (D, D), jnp.float32) * s, 'c_b': jnp.zeros((D,), jnp.float32), 'a_log': jnp.zeros((D,), jnp.float32), 'd_skip': jnp.ones((D,), jnp.float32), 'out_W': jax.random.normal(ks[6], (D, D), jnp.float32) * s, 'out_b': jnp.zeros((D,), jnp.float32), 'ln2_g': jnp.ones((D,), jnp.float32), 'ln2_b': jnp.zeros((D,), jnp.float32), 'f1_W': jax.random.normal(ks[7], (D, H), jnp.float32) * s, 'f1_b': jnp.zeros((H,), jnp.float32), 'f2_W': jax.random.normal(ks[8], (H, D), jnp.float32) * s, 'f2_b': jnp.zeros((D,), jnp.float32)}
    _L1_attn_in = _L1_attn_setup()

    def _L1_ffn_setup():
        import jax, jax.numpy as jnp
        import numpy as np
        B, T = (2, 512)
        D_MODEL, D_HIDDEN = (256, 512)
        N_EXPERTS, TOP_K = (8, 2)
        N_TOKENS = B * T
        CAPACITY = 2 * N_TOKENS * TOP_K // N_EXPERTS
        key = jax.random.key(seed)
        k_x, k_rw, k_w, k_v, k_o = jax.random.split(key, 5)
        x = jax.random.normal(k_x, (B, T, D_MODEL), jnp.float32)
        router_w = jax.random.normal(k_rw, (N_EXPERTS, D_MODEL), jnp.float32) * D_MODEL ** (-0.5)
        router_b = jnp.zeros((N_EXPERTS,), jnp.float32)
        W = jax.random.normal(k_w, (N_EXPERTS, D_MODEL, D_HIDDEN), jnp.float32) * D_MODEL ** (-0.5)
        V = jax.random.normal(k_v, (N_EXPERTS, D_MODEL, D_HIDDEN), jnp.float32) * D_MODEL ** (-0.5)
        W_out = jax.random.normal(k_o, (N_EXPERTS, D_HIDDEN, D_MODEL), jnp.float32) * D_HIDDEN ** (-0.5)
        return {'x': x, 'router_w': router_w, 'router_b': router_b, 'W': W, 'V': V, 'W_out': W_out}
    _L1_ffn_in = _L1_ffn_setup()
    _d = {'L0_attn_x': _L0_attn_in['x'], 'L0_attn_Wq': _L0_attn_in['Wq'], 'L0_attn_bq': _L0_attn_in['bq'], 'L0_attn_Wk': _L0_attn_in['Wk'], 'L0_attn_bk': _L0_attn_in['bk'], 'L0_attn_Wv': _L0_attn_in['Wv'], 'L0_attn_bv': _L0_attn_in['bv'], 'L0_attn_Wc2q': _L0_attn_in['Wc2q'], 'L0_attn_bc2q': _L0_attn_in['bc2q'], 'L0_attn_Wo': _L0_attn_in['Wo'], 'L0_attn_bo': _L0_attn_in['bo'], 'L0_attn_g1': _L0_attn_in['g1'], 'L0_attn_beta1': _L0_attn_in['beta1'], 'L0_attn_g2': _L0_attn_in['g2'], 'L0_attn_beta2': _L0_attn_in['beta2'], 'L0_attn_W1': _L0_attn_in['W1'], 'L0_attn_b1': _L0_attn_in['b1'], 'L0_attn_Wm': _L0_attn_in['Wm'], 'L0_attn_bm': _L0_attn_in['bm'], 'L0_attn_Wqo': _L0_attn_in['Wqo'], 'L0_attn_bqo': _L0_attn_in['bqo'], 'L0_attn_W2': _L0_attn_in['W2'], 'L0_attn_b2': _L0_attn_in['b2'], 'L0_ffn_w_gate': _L0_ffn_in['w_gate'], 'L0_ffn_w_up': _L0_ffn_in['w_up'], 'L0_ffn_w_down': _L0_ffn_in['w_down'], 'L1_attn_ln1_g': _L1_attn_in['ln1_g'], 'L1_attn_ln1_b': _L1_attn_in['ln1_b'], 'L1_attn_in_W': _L1_attn_in['in_W'], 'L1_attn_in_b': _L1_attn_in['in_b'], 'L1_attn_dw_W': _L1_attn_in['dw_W'], 'L1_attn_dw_b': _L1_attn_in['dw_b'], 'L1_attn_dt_W': _L1_attn_in['dt_W'], 'L1_attn_dt_b': _L1_attn_in['dt_b'], 'L1_attn_b_W': _L1_attn_in['b_W'], 'L1_attn_b_b': _L1_attn_in['b_b'], 'L1_attn_c_W': _L1_attn_in['c_W'], 'L1_attn_c_b': _L1_attn_in['c_b'], 'L1_attn_a_log': _L1_attn_in['a_log'], 'L1_attn_d_skip': _L1_attn_in['d_skip'], 'L1_attn_out_W': _L1_attn_in['out_W'], 'L1_attn_out_b': _L1_attn_in['out_b'], 'L1_attn_ln2_g': _L1_attn_in['ln2_g'], 'L1_attn_ln2_b': _L1_attn_in['ln2_b'], 'L1_attn_f1_W': _L1_attn_in['f1_W'], 'L1_attn_f1_b': _L1_attn_in['f1_b'], 'L1_attn_f2_W': _L1_attn_in['f2_W'], 'L1_attn_f2_b': _L1_attn_in['f2_b'], 'L1_ffn_router_w': _L1_ffn_in['router_w'], 'L1_ffn_router_b': _L1_ffn_in['router_b'], 'L1_ffn_W': _L1_ffn_in['W'], 'L1_ffn_V': _L1_ffn_in['V'], 'L1_ffn_W_out': _L1_ffn_in['W_out']}
    _x0 = _d['L0_attn_x']
    _d['L0_attn_x'] = jax.random.normal(jax.random.fold_in(jax.random.key(seed), 1), (4, 1024, 256), dtype=_x0.dtype)
    del _x0
    return _d

def reference(L0_attn_x, L0_attn_Wq, L0_attn_bq, L0_attn_Wk, L0_attn_bk, L0_attn_Wv, L0_attn_bv, L0_attn_Wc2q, L0_attn_bc2q, L0_attn_Wo, L0_attn_bo, L0_attn_g1, L0_attn_beta1, L0_attn_g2, L0_attn_beta2, L0_attn_W1, L0_attn_b1, L0_attn_Wm, L0_attn_bm, L0_attn_Wqo, L0_attn_bqo, L0_attn_W2, L0_attn_b2, L0_ffn_w_gate, L0_ffn_w_up, L0_ffn_w_down, L1_attn_ln1_g, L1_attn_ln1_b, L1_attn_in_W, L1_attn_in_b, L1_attn_dw_W, L1_attn_dw_b, L1_attn_dt_W, L1_attn_dt_b, L1_attn_b_W, L1_attn_b_b, L1_attn_c_W, L1_attn_c_b, L1_attn_a_log, L1_attn_d_skip, L1_attn_out_W, L1_attn_out_b, L1_attn_ln2_g, L1_attn_ln2_b, L1_attn_f1_W, L1_attn_f1_b, L1_attn_f2_W, L1_attn_f2_b, L1_ffn_router_w, L1_ffn_router_b, L1_ffn_W, L1_ffn_V, L1_ffn_W_out):

    def _L0_attn_ref(x, Wq, bq, Wk, bk, Wv, bv, Wc2q, bc2q, Wo, bo, g1, beta1, g2, beta2, W1, b1, Wm, bm, Wqo, bqo, W2, b2):
        import jax, jax.numpy as jnp
        import numpy as np
        B, S, HID = (4, 256, 256)
        H = 8
        HD = HID // H
        NQ = 8
        RATIO = 0.5
        FF = 4 * HID
        EPS_COS = 1e-08
        LN_EPS = 1e-05

        def _layernorm(x, g, b):
            m = jnp.mean(x, axis=-1, keepdims=True)
            v = jnp.var(x, axis=-1, keepdims=True)
            return (x - m) * jax.lax.rsqrt(v + LN_EPS) * g + b
        Q = jnp.einsum('bsh,nhd->bnsd', x, Wq) + bq[None, :, None, :]
        K = jnp.einsum('bsh,nhd->bnsd', x, Wk) + bk[None, :, None, :]
        V = jnp.einsum('bsh,nhd->bnsd', x, Wv) + bv[None, :, None, :]
        qq = jnp.einsum('bnsd,ndq->bnsq', Q, Wc2q) + bc2q[None, :, None, :]
        kq = jnp.einsum('bnsd,ndq->bnsq', K, Wc2q) + bc2q[None, :, None, :]
        qn = jnp.linalg.norm(qq, axis=-1)
        kn = jnp.linalg.norm(kq, axis=-1)
        dots = jnp.einsum('bnsq,bntq->bnst', qq, kq)
        fid = dots / jnp.maximum(qn[..., :, None] * kn[..., None, :], EPS_COS)
        qw = fid * (1.0 + 0.1 * jnp.sin(fid * jnp.pi))
        cw = jnp.einsum('bnsd,bntd->bnst', Q, K) / np.sqrt(HD).astype(np.float32)
        aw = RATIO * qw + (1.0 - RATIO) * cw
        probs = jax.nn.softmax(aw, axis=-1)
        heads = jnp.einsum('bnst,bntd->bnsd', probs, V)
        attn = heads.transpose(0, 2, 1, 3).reshape(x.shape[0], x.shape[1], HID)
        attn = attn @ Wo + bo
        x1 = _layernorm(x + attn, g1, beta1)
        h = x1 @ W1 + b1
        qm = h @ Wm + bm
        qe = jnp.tanh(qm) * jnp.cos(qm * (jnp.pi / 4))
        ha = qe @ Wqo + bqo
        ff = ha @ W2 + b2
        out = _layernorm(x1 + ff, g2, beta2)
        return out

    def _L0_ffn_ref(x, w_gate, w_up, w_down):
        import jax, jax.numpy as jnp
        import numpy as np
        DIM = 256
        HIDDEN = 768
        SCALE = 1.0 / 127.0

        def _dequant(w_int, dtype):
            return w_int.astype(dtype) * jnp.asarray(SCALE, dtype)
        wg = _dequant(w_gate, x.dtype)
        wu = _dequant(w_up, x.dtype)
        wd = _dequant(w_down, x.dtype)
        gate = jnp.einsum('bsd,hd->bsh', x, wg)
        up = jnp.einsum('bsd,hd->bsh', x, wu)
        h = jax.nn.silu(gate) * up
        return jnp.einsum('bsh,dh->bsd', h, wd)

    def _L1_attn_ref(x, ln1_g, ln1_b, in_W, in_b, dw_W, dw_b, dt_W, dt_b, b_W, b_b, c_W, c_b, a_log, d_skip, out_W, out_b, ln2_g, ln2_b, f1_W, f1_b, f2_W, f2_b):
        import jax, jax.numpy as jnp
        import numpy as np
        from jax import lax
        B, L, D, K = (4, 1024, 256, 3)
        H = 512

        def _layernorm(h, g, b):
            m = jnp.mean(h, axis=-1, keepdims=True)
            v = jnp.mean((h - m) ** 2, axis=-1, keepdims=True)
            return (h - m) / jnp.sqrt(v + 1e-05) * g + b
        nx = _layernorm(x, ln1_g, ln1_b)
        proj = nx @ in_W + in_b
        x_proj, gate = jnp.split(proj, 2, axis=-1)
        xt = jnp.transpose(x_proj, (0, 2, 1))
        mixed = lax.conv_general_dilated(xt, dw_W, window_strides=(1,), padding=[(K // 2, K // 2)], dimension_numbers=('NCH', 'OIH', 'NCH'), feature_group_count=D)
        mixed = jnp.transpose(mixed + dw_b[None, :, None], (0, 2, 1))
        dt = jax.nn.softplus(mixed @ dt_W + dt_b)
        bt = jnp.tanh(mixed @ b_W + b_b)
        ct = jnp.tanh(mixed @ c_W + c_b)
        a = -jnp.exp(a_log)

        def step(state, inp):
            dt_t, b_t, c_t, m_t, g_t = inp
            decay = jnp.exp(dt_t * a)
            state = decay * state + dt_t * b_t * m_t
            y_t = c_t * state + d_skip * m_t
            return (state, y_t * jax.nn.sigmoid(g_t))
        seqs = tuple((jnp.transpose(t, (1, 0, 2)) for t in (dt, bt, ct, mixed, gate)))
        state0 = jnp.zeros((x.shape[0], x.shape[2]), x.dtype)
        _, ys = lax.scan(step, state0, seqs)
        y = jnp.transpose(ys, (1, 0, 2))
        x2 = x + y @ out_W + out_b
        h = _layernorm(x2, ln2_g, ln2_b)
        ffn = jax.nn.gelu(h @ f1_W + f1_b, approximate=False) @ f2_W + f2_b
        return x2 + ffn

    def _L1_ffn_ref(x, router_w, router_b, W, V, W_out):
        import jax, jax.numpy as jnp
        import numpy as np
        B, T = (2, 512)
        D_MODEL, D_HIDDEN = (256, 512)
        N_EXPERTS, TOP_K = (8, 2)
        N_TOKENS = B * T
        CAPACITY = 2 * N_TOKENS * TOP_K // N_EXPERTS
        Bq, Tq, D = x.shape
        N = Bq * Tq
        x_flat = x.reshape(N, D)
        router_logits = x_flat @ router_w.T + router_b
        top_vals, top_ids = jax.lax.top_k(router_logits, TOP_K)
        top_probs = jax.nn.softmax(top_vals, axis=-1)
        x_pad = jnp.concatenate([x_flat, jnp.zeros((1, D), x_flat.dtype)], axis=0)
        probs_pad = jnp.concatenate([top_probs, jnp.zeros((1, TOP_K), top_probs.dtype)], axis=0)
        out = jnp.zeros((N + 1, D), x_flat.dtype)
        for e in range(N_EXPERTS):
            tok, slot = jnp.nonzero(top_ids == e, size=CAPACITY, fill_value=(N, 0))
            w = probs_pad[tok, slot][:, None]
            xin = x_pad[tok]
            a = xin @ W[e]
            b = xin @ V[e]
            y = a * (b * jax.nn.sigmoid(b)) @ W_out[e]
            out = out.at[tok].add(y * w)
        return out[:N].reshape(Bq, Tq, D)
    x = L0_attn_x
    x = _layernorm(x + _L0_attn_ref(x, L0_attn_Wq, L0_attn_bq, L0_attn_Wk, L0_attn_bk, L0_attn_Wv, L0_attn_bv, L0_attn_Wc2q, L0_attn_bc2q, L0_attn_Wo, L0_attn_bo, L0_attn_g1, L0_attn_beta1, L0_attn_g2, L0_attn_beta2, L0_attn_W1, L0_attn_b1, L0_attn_Wm, L0_attn_bm, L0_attn_Wqo, L0_attn_bqo, L0_attn_W2, L0_attn_b2), axis=-1)
    x = _layernorm(x + _L0_ffn_ref(x, L0_ffn_w_gate, L0_ffn_w_up, L0_ffn_w_down), axis=-1)
    x = _layernorm(x + _L1_attn_ref(x, L1_attn_ln1_g, L1_attn_ln1_b, L1_attn_in_W, L1_attn_in_b, L1_attn_dw_W, L1_attn_dw_b, L1_attn_dt_W, L1_attn_dt_b, L1_attn_b_W, L1_attn_b_b, L1_attn_c_W, L1_attn_c_b, L1_attn_a_log, L1_attn_d_skip, L1_attn_out_W, L1_attn_out_b, L1_attn_ln2_g, L1_attn_ln2_b, L1_attn_f1_W, L1_attn_f1_b, L1_attn_f2_W, L1_attn_f2_b), axis=-1)
    x = _layernorm(x + _L1_ffn_ref(x, L1_ffn_router_w, L1_ffn_router_b, L1_ffn_W, L1_ffn_V, L1_ffn_W_out), axis=-1)
    return x

_drawn_inputs = setup_inputs


def setup_inputs(seed=0):
    import zlib

    import numpy as np

    out = dict(_drawn_inputs(seed))
    spreads = {'L0_attn_bq': (0.0, 0.8),
     'L0_attn_bk': (0.0, 2.0),
     'L0_attn_bv': (0.0, 0.1),
     'L0_attn_bc2q': (0.0, 2.0),
     'L0_attn_bo': (0.0, 0.1),
     'L0_attn_g1': (1.0, 0.2),
     'L0_attn_beta1': (0.0, 0.1),
     'L0_attn_g2': (1.0, 0.2),
     'L0_attn_beta2': (0.0, 0.1),
     'L0_attn_b1': (0.0, 0.496),
     'L0_attn_bm': (0.0, 2.0),
     'L0_attn_bqo': (0.0, 0.1),
     'L0_attn_b2': (0.0, 0.1),
     'L1_attn_ln1_g': (1.0, 0.6),
     'L1_attn_ln1_b': (0.0, 0.8),
     'L1_attn_in_b': (0.0, 0.8),
     'L1_attn_dw_b': (0.0, 0.1),
     'L1_attn_dt_b': (0.0, 0.8),
     'L1_attn_b_b': (0.0, 0.8),
     'L1_attn_c_b': (0.0, 0.8),
     'L1_attn_a_log': (0.0, 0.8),
     'L1_attn_d_skip': (1.0, 0.6),
     'L1_attn_out_b': (0.0, 0.1),
     'L1_attn_ln2_g': (1.0, 0.6),
     'L1_attn_ln2_b': (0.0, 0.375),
     'L1_attn_f1_b': (0.0, 0.1),
     'L1_attn_f2_b': (0.0, 0.1),
     'L1_ffn_router_b': (0.0, 0.1)}
    factors = {'L0_attn_Wq': 8.0,
     'L0_attn_Wk': 6.306,
     'L0_attn_Wv': 3.717,
     'L0_attn_Wc2q': 21.949,
     'L0_attn_Wm': 2.824,
     'L1_attn_in_W': 4.516,
     'L1_attn_dw_W': 5.559,
     'L1_attn_dt_W': 8.0,
     'L1_attn_b_W': 8.0,
     'L1_attn_c_W': 8.0}
    for name, (base, spread) in spreads.items():
        noise = np.random.default_rng([zlib.crc32(name.encode()), seed]).standard_normal(out[name].shape)
        drawn = base * np.exp(spread * noise) if base else spread * noise
        out[name] = jnp.asarray(drawn.astype(out[name].dtype))
    for name, factor in factors.items():
        out[name] = (out[name] * factor).astype(out[name].dtype)
    return out
```

```python
import concourse.bass as bass
from concourse import mybir
from concourse.alu_op_type import AluOpType as ALU
from contextlib import ExitStack

ACT = mybir.ActivationFunctionType
AX = mybir.AxisListType
F32 = mybir.dt.float32
BF16 = mybir.dt.bfloat16
I32 = mybir.dt.int32
U32 = mybir.dt.uint32

P = 128
B, S, D = 4, 1024, 256
N = B * S
TILES = N // P
H, HD, NQ = 8, 32, 8
KD = D // P
CH = 512
TPC = CH // P
ST = S // P
PAIRS = B * H // 2
UNITS = 2 * ST
FID_SCALE = 0.05
SIN_SCALE = float(-3.14159265 / FID_SCALE * (1.0 - 4e-7))
SCORE_SCALE = float(-0.5 / (HD ** 0.5))
TINY = 1e-37
FF, FK, HID, HT = 1024, 8, 768, 6
LN_EPS = 1e-5
ROUND = 12582912.0
PI = 3.141592653589793
W3_IN = 16 * (15 + 16)
E, CAP = 8, 512
TOP_STEPS_E = 15
W5_IN = 16 * (15 + 8 + 2 * 7)
W_DMAS = 6 + 4 + 1 + 2 + 8


def now(per, n, k):
    return per * (n + 1) + k


def before(per, n, k):
    return per * n + k


def build_program(nc, t, out):
    ctx = ExitStack()
    with ctx:
        def sem(name):
            return ctx.enter_context(nc.semaphore(name))

        arena = ctx.enter_context(nc.sbuf_tensor("arena", [P, 51200], F32))
        banks = ctx.enter_context(nc.psum_tensor("banks", [P, 8 * 512], F32))

        def fp(at, n):
            return arena[:, at:at + n]

        def bank(i, n=1):
            return banks[:, i * 512:(i + n) * 512]

        q_planes = nc.dram_tensor("q_planes", [3, B * H, HD, S], BF16, kind="Internal").ap()
        k_planes = nc.dram_tensor("k_planes", [3, B * H, HD, S], BF16, kind="Internal").ap()
        fq_planes = nc.dram_tensor("fq_planes", [3, B * H, NQ, S], BF16, kind="Internal").ap()
        fk_planes = nc.dram_tensor("fk_planes", [3, B * H, NQ, S], BF16, kind="Internal").ap()

        ident = fp(0, 128)
        fscale = fp(128, 1)
        rsum = fp(136, UNITS)
        rinv = fp(152, UNITS)
        nmax = fp(168, UNITS)
        V = fp(2048, 8192).rearrange("p (t n) -> p t n", n=D)
        att = fp(10240, 8192).rearrange("p (t n) -> p t n", n=D)
        R3 = 18432

        o = R3
        def take(n):
            nonlocal o
            o += n
            return fp(o - n, n)
        wq = take(KD * D).rearrange("p (k n) -> p k n", k=KD)
        wk = take(KD * D).rearrange("p (k n) -> p k n", k=KD)
        wv = take(KD * D).rearrange("p (k n) -> p k n", k=KD)
        wc = take(KD * H * NQ).rearrange("p (k n) -> p k n", k=KD)
        bqk = take(4)
        bvb = take(D)
        bcb = take(2 * H * NQ)
        half = fp(256, 64)
        xin = [take(TPC * D).rearrange("p (j n) -> p j n", j=TPC) for _ in range(2)]
        xT = take(KD * CH).rearrange("p (k n) -> p k n", k=KD)
        feat = take(5 * CH).rearrange("p (f n) -> p f n", f=5)
        rest = take(5 * CH).rearrange("p (f n) -> p f n", f=5)
        planes = [take(5 * 3 * CH // 2).bitcast(BF16).rearrange("p (f l n) -> p f l n", f=5, l=3) for _ in range(2)]
        qk = take(TPC * P).rearrange("p (j n) -> p j n", j=TPC)
        qk2 = take(TPC * P).rearrange("p (j n) -> p j n", j=TPC)
        ss = take(TPC * 2 * H)
        rn = take(TPC * 2 * H)
        assert o <= 51200

        o = R3
        logits = take(UNITS * S).rearrange("p (u n) -> p u n", u=UNITS)
        fq = [take(S // 2).bitcast(BF16) for _ in range(2)]
        fk = [take(S // 2).bitcast(BF16) for _ in range(2)]
        qs = [take(S).bitcast(BF16).rearrange("p (a n) -> p a n", a=2) for _ in range(2)]
        ks = [take(S).bitcast(BF16).rearrange("p (a n) -> p a n", a=2) for _ in range(2)]
        sn = [take(S) for _ in range(2)]
        pr = [take(S) for _ in range(2)]
        pT = [take(S).rearrange("p (t n) -> p t n", t=ST) for _ in range(2)]
        assert o <= 51200

        o = 2048
        wo = take(KD * D).rearrange("p (k n) -> p k n", k=KD)
        wgT = take(KD * HID).rearrange("p (k n) -> p k n", k=KD)
        wuT = take(KD * HID).rearrange("p (k n) -> p k n", k=KD)
        wdT = take(HT * D).rearrange("p (k n) -> p k n", k=HT)
        w1m = take(KD * NQ).rearrange("p (k n) -> p k n", k=KD)
        qm_row = take(NQ)
        w2q = take(D)
        ones = take(P)
        last_row = take(NQ + 1)
        bo_b, g1_b, be1_b, g2_b, be2_b = (take(D) for _ in range(5))
        assert o <= 10240
        o = R3
        tiles = lambda a: a.rearrange("p (j n) -> p j n", n=D)
        attc = [tiles(take(TPC * D)) for _ in range(2)]
        xc = [tiles(take(TPC * D)) for _ in range(2)]
        overlay = o
        w1 = take(KD * FF).rearrange("p (k n) -> p k n", k=KD)
        w1T = take(FK * D).rearrange("p (k n) -> p k n", k=FK)
        w2 = take(FK * D).rearrange("p (k n) -> p k n", k=FK)
        wm = take(FK * NQ).rearrange("p (k n) -> p k n", k=FK)
        b1c = take(FK)
        wqo = take(FF)
        wqoT = take(FK * (NQ + 1)).rearrange("p (k n) -> p k n", k=FK)
        bm = take(NQ)
        b2 = take(D)
        ints = take(3 * HT * D).bitcast(I32)
        floats = take(3 * HT * D)
        assert o <= 51200
        o = overlay
        xbo, xb2, r1, n1, m1, x1, r2, n2, m2, r3, r4 = (tiles(take(TPC * D)) for _ in range(11))
        xp = [tiles(take(TPC * D)) for _ in range(2)]
        xo = [tiles(take(TPC * D)) for _ in range(2)]
        aT = take(KD * CH).rearrange("p (k n) -> p k n", k=KD)
        x1T = take(KD * CH).rearrange("p (k n) -> p k n", k=KD)
        xpT = [take(KD * CH).rearrange("p (k n) -> p k n", k=KD) for _ in range(2)]
        sg = [take(CH) for _ in range(2)]
        hT = take(HT * CH).rearrange("p (k n) -> p k n", k=HT)
        turns, th, cs = (take(TPC * NQ) for _ in range(3))
        qe = take(TPC * (NQ + 1)).rearrange("p (j q) -> p j q", j=TPC)
        qeT = take(CH)
        stats = take(8 * 6).rearrange("p (j s) -> p j s", s=6)
        stats_f = take(8 * 6).rearrange("p (j s) -> p j s", s=6)
        moments = take(8 * 2).rearrange("p (j s) -> p j s", s=2)
        moments_f = take(8 * 2).rearrange("p (j s) -> p j s", s=2)
        var = take(8)
        var_f = take(8)
        rstd = take(8)
        rstd_f = take(8)
        assert o <= 51200
        x_mid = nc.dram_tensor("x_mid", [N, D], F32, kind="Internal").ap()
        x_mid_c = x_mid.rearrange("(c j p) n -> c p j n", j=TPC, p=P)
        rows = lambda w: w.rearrange("(k p) n -> p k n", p=P)

        o = 320
        ln1g_b, ln1b_b, ln2g_b, ln2b_b, outb_b, f2b_b = (take(D) for _ in range(6))
        assert o <= 2048
        x_all = tiles(fp(2048, TILES * D))
        o = 10240
        kn = lambda a, k: a.rearrange("p (k n) -> p k n", k=k)
        in_w = kn(take(KD * 2 * D), KD)
        dt_w, b_w, c_w, out_w = (kn(take(KD * D), KD) for _ in range(4))
        f1_w = kn(take(KD * 2 * D), KD)
        f2_w = kn(take(2 * KD * D), 2 * KD)
        rt_w = take(D)
        rt_wT = kn(take(KD * E), KD)
        rt_b = take(E)
        in_b = take(4)
        taps = kn(take(KD * 3), KD)
        tap_b, dt_b, b_b, c_b, a_neg, skip = (take(KD) for _ in range(6))
        f1_b = take(4)
        lg_all = take(TILES * E).rearrange("p (t e) -> p t e", e=E)
        xr, n5, m5, h5, x2, xob = (tiles(take(ST * D)) for _ in range(6))
        T5, gate, mixed = (kn(take(KD * S), KD) for _ in range(3))
        gl = kn(fp(o, 2 * KD * S), 2 * KD)
        z, l, v, ct, dt, state = (kn(take(KD * S), KD) for _ in range(6))
        xpad = kn(take(KD * (S + 2)), KD)
        decay = z
        wide_x = state.rearrange("p k n -> p (k n)").rearrange("p (j n) -> p j n", n=D)
        stats5 = take(ST * 6).rearrange("p (j s) -> p j s", s=6)
        mom5 = take(ST * 2).rearrange("p (j s) -> p j s", s=2)
        var5, rstd5 = take(ST), take(ST)
        ones4 = take(P)
        assert o <= 51200, o
        x_mid_b = x_mid.rearrange("(b j p) n -> b p j n", j=ST, p=P)
        xe = nc.dram_tensor("x_by_expert", [E * CAP, D], F32, kind="Internal").ap()
        ye = nc.dram_tensor("y_by_expert", [E * CAP + 1, D], F32, kind="Internal").ap()

        o = 26624
        lg6 = take(TILES * E).rearrange("p (t e) -> p t e", e=E)
        rev, eq, mask1, mask2, both, rest6, tot, pos = (take(TILES * E).rearrange("p (t e) -> p t e", e=E) for _ in range(8))
        top1, top2, s1, s2, p1, p2, slot, fits = (take(TILES) for _ in range(8))
        idx = [take(TILES).bitcast(U32) for _ in range(2)]
        below, ones6 = take(P), take(P)
        xe_s = [tiles(take(TPC * D)) for _ in range(2)]
        we = [kn(take(KD * CAP), KD) for _ in range(2)]
        ve = [kn(take(KD * CAP), KD) for _ in range(2)]
        woe = [kn(take(4 * D), 4) for _ in range(2)]
        XT = kn(take(KD * CAP), KD)
        sg6 = [take(CAP) for _ in range(2)]
        h6 = kn(take(4 * CAP), 4)
        ye_s = [tiles(take(TPC * D)) for _ in range(2)]
        y_g = [tiles(fp(10240 + s * TILES * D, TILES * D)) for s in range(2)]
        acc = [tiles(take(TPC * D)) for _ in range(2)]
        fin = [tiles(take(TPC * D)) for _ in range(2)]
        stats6 = take(TPC * 6).rearrange("p (j s) -> p j s", s=6)
        mom6 = take(TPC * 2).rearrange("p (j s) -> p j s", s=2)
        var6, rstd6 = take(TPC), take(TPC)
        assert o <= 51200, o
        got6 = [sem(f"got6_{c}") for c in range(TILES // TPC)]
        out_c = out.rearrange("b (c j p) n -> (b c) p j n", j=TPC, p=P)

        qe_one = sem("qe_one")
        c3_in = [sem("c3_in0"), sem("c3_in1")]
        x_out = [sem("x_out0"), sem("x_out1")]
        w3_in = sem("w3_in")
        prep_pe = sem("prep_pe")
        prep_act = sem("prep_act")
        prep_dve = sem("prep_dve")
        prep_c = sem("prep_c")
        pre_pe = sem("pre_pe")
        ffn_pe = sem("ffn_pe")
        act_pre = sem("act_pre")
        act_silu = sem("act_silu")
        dve_pre = sem("dve_pre")
        h_made = sem("h_made")
        dve_out = sem("dve_out")
        pool_pre = sem("pool_pre")
        pool_ffn = sem("pool_ffn")
        x5_in = sem("x5_in")
        w5_in = sem("w5_in")
        zero_in = sem("zero_in")
        x3_out = sem("x3_out")
        pe5 = sem("pe5")
        act5 = sem("act5")
        dve5 = sem("dve5")
        pool5 = sem("pool5")
        prep5_pe = sem("prep5_pe")
        prep5_act = sem("prep5_act")
        prep5 = sem("prep5")
        const5 = sem("const5")
        e_in = [sem("e_in0"), sem("e_in1")]
        y_out = [sem("y_out0"), sem("y_out1")]
        const6 = sem("const6")
        rank_made = sem("rank_made")
        count_pe = sem("count_pe")
        top6 = sem("top6")
        exp6 = sem("exp6")
        idx6 = sem("idx6")
        sent6 = sem("sent6")
        pe6 = sem("pe6")
        act6 = sem("act6")
        dve6 = sem("dve6")
        lg_in = sem("lg_in")
        fin6 = sem("fin6")
        pow6 = sem("pow6")
        fin_out = [sem("fin_out0"), sem("fin_out1")]
        s_const = sem("s_const")
        s_w = sem("s_w")
        s_fscale = sem("s_fscale")
        passed = sem("passed")
        s_x = [sem("s_x0"), sem("s_x1")]
        s_xT = sem("s_xT")
        s_xTs = sem("s_xTs")
        s_proj = sem("s_proj")
        s_feat = sem("s_feat")
        s_v = sem("s_v")
        s_qq = sem("s_qq")
        s_qkb = sem("s_qkb")
        s_sq = sem("s_sq")
        s_ss = sem("s_ss")
        s_rn = sem("s_rn")
        s_qn = sem("s_qn")
        s_fT = sem("s_fT")
        s_hi = sem("s_hi")
        s_rest = sem("s_rest")
        s_mid = sem("s_mid")
        s_lo = sem("s_lo")
        s_st = [sem("s_st0"), sem("s_st1")]
        stage = sem("stage")

        score_made = sem("score_made")
        score_used = sem("score_used")
        sin_made = sem("sin_made")
        exp_made = sem("exp_made")
        tr_made = sem("tr_made")
        ev_a = sem("ev_a")
        ev_d = sem("ev_d")
        pv_made = sem("pv_made")
        att_made = sem("att_made")
        rinv_made = sem("rinv_made")
        f_in = [sem("f_in0"), sem("f_in1")]
        c_in = [sem("c_in0"), sem("c_in1")]

        block = ctx.enter_context(nc.Block())

        def meet(eng, k):
            eng.drain().then_inc(stage, 1)
            eng.wait_ge(stage, 5 * k)

        x_tok = t["L0_attn_x"].rearrange("b (c j p) n -> (b c) p j n", j=TPC, p=P)
        wview = lambda w: w.rearrange("h (k p) d -> p k h d", p=P)
        FQR = 9 * NQ


        def load_f(sp, g, hh):
            gh = 2 * g + hh
            for rep in range(3):
                sp.dma_start(fq[hh][rep * 24:rep * 24 + 24, :],
                             fq_planes[:, bass.ds(gh, 1), :, :].rearrange("l o d n -> l (o d) n")).then_inc(f_in[hh], 16)
                sp.dma_start(fk[hh][rep * 24:rep * 24 + 24, :],
                             fk_planes[rep, bass.ds(gh, 1), :, :].rearrange("o d n -> (o d) n").partition_broadcast(3)).then_inc(f_in[hh], 16)

        def load_c(sp, g, hh):
            gh = 2 * g + hh
            q = lambda a, z: q_planes[a:z, bass.ds(gh, 1), :, :].rearrange("l o d n -> l (o d) n")
            k = lambda l, n: k_planes[l, bass.ds(gh, 1), :, :].rearrange("o d n -> (o d) n").partition_broadcast(n)
            for dst, src in ((qs[hh][0:96, 0, :], q(0, 3)), (qs[hh][96:128, 0, :], q(0, 1)),
                             (qs[hh][0:64, 1, :], q(1, 3)), (qs[hh][64:128, 1, :], q(0, 2)),
                             (ks[hh][0:96, 0, :], k(0, 3)), (ks[hh][96:128, 0, :], k(1, 1)),
                             (ks[hh][0:64, 1, :], k(1, 2)), (ks[hh][64:128, 1, :], k(2, 2))):
                sp.dma_start(dst, src).then_inc(c_in[hh], 16)

        F_IN, C_IN = 6 * 16, 8 * 16

        @block.sync
        def _(sp):
            for k in range(KD):
                for dst, src in ((wq, "L0_attn_Wq"), (wk, "L0_attn_Wk"), (wv, "L0_attn_Wv")):
                    sp.dma_start(dst[:, k, :].rearrange("p (h d) -> p h d", h=H),
                                 t[src][:, k * P:(k + 1) * P, :].rearrange("h p d -> p h d")).then_inc(s_w, 16)
            for i, n in enumerate(("L0_attn_bq", "L0_attn_bk")):
                for k in range(KD):
                    sp.dma_start(bqk[:, 2 * i + k:2 * i + k + 1],
                                 t[n].rearrange("(k h) d -> k (h d)", k=KD)[k].rearrange("(p o) -> p o", o=1)).then_inc(s_w, 16)
            sp.dma_start(bvb, t["L0_attn_bv"].rearrange("h d -> (h d)").partition_broadcast(P)).then_inc(s_w, 16)
            for i in range(2):
                sp.dma_start(bcb[:, i * 64:(i + 1) * 64], t["L0_attn_bc2q"].rearrange("h d -> (h d)").partition_broadcast(P)).then_inc(s_w, 16)
            sp.wait_ge(s_const, 4)
            for h in range(H):
                sp.dma_start(wc[(h % 4) * 32:(h % 4 + 1) * 32, h // 4, h * NQ:(h + 1) * NQ], t["L0_attn_Wc2q"][h]).then_inc(s_w, 16)
            for r in range(2):
                sp.dma_start(xin[r], x_tok[r]).then_inc(s_x[r], 16)

            def store(b):
                for r in range(2):
                    sp.wait_ge(s_lo, 5 * (2 * b + r + 1))
                    for f, dst in enumerate((q_planes, q_planes, k_planes, k_planes)):
                        d = dst[:, bass.ds(b * H + 4 * (f % 2), 4), :, r * CH:(r + 1) * CH].rearrange("l h d n -> (h d) l n")
                        sp.dma_start(d, planes[r][:, f]).then_inc(s_st[r], 16)
                    for i, dst in enumerate((fq_planes, fk_planes)):
                        d = dst[:, bass.ds(b * H, H), :, r * CH:(r + 1) * CH].rearrange("l h d n -> (h d) l n")
                        sp.dma_start(d, planes[r][64 * i:64 * i + 64, 4]).then_inc(s_st[r], 16)

            with sp.Fori(0, B - 1) as b:
                for r in range(2):
                    sp.wait_ge(s_xT, 2 * b + r + 1)
                    sp.dma_start(xin[r], x_tok[bass.ds(2 * b + (2 + r), 1)].rearrange("o p j n -> p (o j) n")).then_inc(s_x[r], 16)
                store(b)
            store(B - 1)
            for r in range(2):
                sp.wait_ge(s_st[r], 96 * B)
            meet(sp, 1)

            for hh in range(2):
                load_f(sp, 0, hh)
            for hh in range(2):
                load_c(sp, 0, hh)
            with sp.Fori(0, PAIRS - 1) as g:
                for hh in range(2):
                    sp.wait_ge(score_made, 32 * g + 8 * (hh + 1))
                    load_f(sp, g + 1, hh)
                for hh in range(2):
                    sp.wait_ge(score_made, 32 * g + 16 + 8 * (hh + 1))
                    load_c(sp, g + 1, hh)
            meet(sp, 2)

            for dst, src in ((wo, rows(t["L0_attn_Wo"])), (w1, rows(t["L0_attn_W1"])), (w2, rows(t["L0_attn_W2"])),
                             (wm, rows(t["L0_attn_Wm"])), (wqo[0:NQ], t["L0_attn_Wqo"]),
                             (bm[0:1], t["L0_attn_bm"].unsqueeze(0)), (b2[0:1], t["L0_attn_b2"].unsqueeze(0)),
                             (bo_b, t["L0_attn_bo"].partition_broadcast(P)),
                             (g1_b, t["L0_attn_g1"].partition_broadcast(P)), (be1_b, t["L0_attn_beta1"].partition_broadcast(P)),
                             (g2_b, t["L0_attn_g2"].partition_broadcast(P)), (be2_b, t["L0_attn_beta2"].partition_broadcast(P)),
                             (tiles(ints[:, 0:HT * D]), rows(t["L0_ffn_w_gate"])), (tiles(ints[:, HT * D:2 * HT * D]), rows(t["L0_ffn_w_up"])),
                             (ints[:, 2 * HT * D:].rearrange("p (k n) -> p k n", k=KD), rows(t["L0_ffn_w_down"]))):
                sp.dma_start(dst, src).then_inc(w3_in, 16)
            for k in range(FK):
                sp.dma_start(b1c[:, k:k + 1], t["L0_attn_b1"][k * P:(k + 1) * P].unsqueeze(1)).then_inc(w3_in, 16)
                sp.dma_start(wqoT[:, k, NQ:NQ + 1], t["L0_attn_bqo"][k * P:(k + 1) * P].unsqueeze(1)).then_inc(w3_in, 16)

            def load3(n, r):
                sp.dma_start(attc[r], att[:, bass.ds(TPC * n, TPC), :]).then_inc(c3_in[r], 16)
                sp.dma_start(xc[r], x_tok[bass.ds(n, 1)].rearrange("o p j n -> p (o j) n")).then_inc(c3_in[r], 16)

            def store3(n, r):
                sp.wait_ge(dve_out, now(5, n, 5))
                sp.dma_start(x_mid_c[bass.ds(n, 1)].rearrange("o p j n -> p (o j) n"), xo[r]).then_inc(x_out[r], 16)

            for r in range(2):
                load3(r, r)
            with sp.Fori(0, B - 1) as i:
                for r in range(2):
                    sp.wait_ge(pre_pe, now(7, 2 * i + r, 1))
                    sp.wait_ge(pool_pre, now(8, 2 * i + r, 2))
                    load3(2 * i + (r + 2), r)
                for r in range(2):
                    store3(2 * i + r, r)
            for r in range(2):
                store3(2 * (B - 1) + r, r)
            for r in range(2):
                sp.wait_ge(x_out[r], 16 * B)
            meet(sp, 3)

            col = lambda w, k: w.rearrange("(k p) -> k p", p=P)[k].unsqueeze(1)
            for dst, src in ((in_w, rows(t["L1_attn_in_W"])), (dt_w, rows(t["L1_attn_dt_W"])), (b_w, rows(t["L1_attn_b_W"])),
                             (c_w, rows(t["L1_attn_c_W"])), (out_w, rows(t["L1_attn_out_W"])), (f1_w, rows(t["L1_attn_f1_W"])),
                             (f2_w, rows(t["L1_attn_f2_W"])), (rt_w[0:E], t["L1_ffn_router_w"]),
                             (rt_b[0:1], t["L1_ffn_router_b"].unsqueeze(0)),
                             (ln1g_b, t["L1_attn_ln1_g"].partition_broadcast(P)), (ln1b_b, t["L1_attn_ln1_b"].partition_broadcast(P)),
                             (ln2g_b, t["L1_attn_ln2_g"].partition_broadcast(P)), (ln2b_b, t["L1_attn_ln2_b"].partition_broadcast(P)),
                             (outb_b, t["L1_attn_out_b"].partition_broadcast(P)), (f2b_b, t["L1_attn_f2_b"].partition_broadcast(P))):
                sp.dma_start(dst, src).then_inc(w5_in, 16)
            for k in range(4):
                sp.dma_start(in_b[:, k:k + 1], col(t["L1_attn_in_b"], k)).then_inc(w5_in, 16)
                sp.dma_start(f1_b[:, k:k + 1], col(t["L1_attn_f1_b"], k)).then_inc(w5_in, 16)
            for k in range(KD):
                sp.dma_start(taps[:, k, :], t["L1_attn_dw_W"][k * P:(k + 1) * P].rearrange("p o q -> p (o q)")).then_inc(w5_in, 16)
                for dst, src in ((tap_b, "dw_b"), (dt_b, "dt_b"), (b_b, "b_b"), (c_b, "c_b"), (a_neg, "a_log"), (skip, "d_skip")):
                    sp.dma_start(dst[:, k:k + 1], col(t["L1_attn_" + src], k)).then_inc(w5_in, 16)
            sp.dma_start(xr, x_mid_b[0]).then_inc(x5_in, 16)
            sp.wait_ge(const5, 2)
            for q in range(E):
                sp.dma_start(xe[q * CAP:(q + 1) * CAP].rearrange("(p r) n -> p (r n)", p=P),
                             wide_x.rearrange("p j n -> p (j n)")[:, 0:TPC * D]).then_inc(zero_in, 16)
            sp.dma_start(ye[E * CAP:E * CAP + 1], wide_x[0:1, 0, :]).then_inc(zero_in, 16)

            def keep(b):
                sp.wait_ge(dve5, now(30, b, 29))
                sp.dma_start(x_all[:, bass.ds(ST * b, ST), :], h5).then_inc(x3_out, 16)

            with sp.Fori(0, B - 1) as b:
                sp.wait_ge(dve5, now(30, b, 25))
                sp.dma_start(xr, x_mid_b[bass.ds(b + 1, 1)].rearrange("o p j n -> p (o j) n")).then_inc(x5_in, 16)
                keep(b)
            keep(B - 1)
            sp.wait_ge(x3_out, 16 * B)
            sp.wait_ge(zero_in, 16 * (E + 1))
            meet(sp, 4)

            ew = lambda w, e, k: w[bass.ds(e, 1)].rearrange("o (k p) n -> p (o k) n", p=P)

            def load_w(e, r):
                sp.dma_start(we[r], ew(t["L1_ffn_W"], e, KD)).then_inc(e_in[r], 16)
                sp.dma_start(ve[r], ew(t["L1_ffn_V"], e, KD)).then_inc(e_in[r], 16)
                sp.dma_start(woe[r], ew(t["L1_ffn_W_out"], e, 4)).then_inc(e_in[r], 16)

            def load_x(e, r):
                sp.dma_start(xe_s[r], xe[bass.ds(CAP * e, CAP)].rearrange("(j p) n -> p j n", p=P)).then_inc(e_in[r], 16)

            def store_y(e, r):
                sp.wait_ge(act6, now(6, e, 6))
                sp.dma_start(ye[bass.ds(CAP * e, CAP)].rearrange("(j p) n -> p j n", p=P), ye_s[r]).then_inc(y_out[r], 16)

            for r in range(2):
                load_w(r, r)
            sp.wait_ge(sent6, 16 * 2 * TILES)
            for r in range(2):
                load_x(r, r)
            with sp.Fori(0, E // 2 - 1) as i:
                for r in range(2):
                    sp.wait_ge(pe6, now(6, 2 * i + r, 6))
                    load_w(2 * i + (r + 2), r)
                    load_x(2 * i + (r + 2), r)
                    store_y(2 * i + r, r)
            for r in range(2):
                store_y(E - 2 + r, r)
            for c in range(TILES // TPC):
                sp.wait_ge(fin6, 6 * (c + 1))
                sp.dma_start(out_c[c], fin[c % 2]).then_inc(fin_out[c % 2], 16)
            for r in range(2):
                sp.wait_ge(fin_out[r], 16 * (TILES // TPC // 2))
            meet(sp, 5)

        @block.gpsimd
        def _(pool):
            pool.memset(ident, 0.0).then_inc(s_const, 1)
            pool.memset(wc, 0.0).then_inc(s_const, 1)
            pool.memset(half, -0.5).then_inc(s_const, 1)
            pool.wait_ge(s_const, 3)
            pool.affine_select(out=ident, in_=ident, compare_op=ALU.not_equal, fill=1.0, base=0,
                               pattern=[[-1, P]], channel_multiplier=1).then_inc(s_const, 1)
            with pool.Fori(0, 2 * B) as n:
                pool.wait_ge(s_ss, n + 1)
                pool.tensor_tensor(rn, ss, half, ALU.pow).then_inc(s_rn, 1)
            meet(pool, 1)
            meet(pool, 2)

            pool.memset(ones, 1.0).then_inc(prep_c, 1)
            pool.memset(last_row, 0.0).then_inc(prep_c, 1)
            pool.wait_ge(prep_c, 2)
            pool.memset(last_row[:, NQ:NQ + 1], 1.0).then_inc(prep_c, 1)
            pool.wait_ge(prep_pe, 5)
            pool.sem_inc(pool_pre, 8)
            pool.sem_inc(pool_ffn, 1)
            wide = lambda v: v.unsqueeze(1).to_broadcast([P, TPC, D])

            def power(done, out_, in_):
                pool.tensor_tensor(out_[:, 0:TPC], in_[:, 0:TPC], half[:, 0:TPC], ALU.pow).then_inc(done, 1)

            def pre_pool(i, r):
                n = 2 * i + r
                pool.wait_ge(c3_in[r], 32 * (i + 1))
                pool.wait_ge(dve_pre, before(21, n, 1))
                pool.tensor_tensor(xbo, xc[r], wide(bo_b), ALU.add).then_inc(pool_pre, 1)
                pool.wait_ge(dve_pre, before(21, n, 17))
                pool.tensor_tensor(xb2, xc[r], wide(be2_b), ALU.add).then_inc(pool_pre, 1)
                pool.wait_ge(dve_pre, now(21, n, 4))
                power(pool_pre, rstd, var)
                pool.wait_ge(dve_pre, now(21, n, 5))
                pool.tensor_tensor(m1, n1, wide(g1_b), ALU.mult).then_inc(pool_pre, 1)
                pool.wait_ge(pool_pre, now(8, n, 4))
                pool.wait_ge(pre_pe, before(7, n, 3))
                pool.tensor_tensor(x1, m1, wide(be1_b), ALU.add).then_inc(pool_pre, 1)
                pool.wait_ge(dve_pre, now(21, n, 15))
                power(pool_pre, rstd, var)
                pool.wait_ge(dve_pre, now(21, n, 16))
                pool.tensor_tensor(m2, n2, wide(g2_b), ALU.mult).then_inc(pool_pre, 1)
                pool.wait_ge(dve_pre, now(21, n, 20))
                power(pool_pre, rstd, var)

            def ffn_pool(i, r):
                n = 2 * i + r
                pool.wait_ge(dve_out, now(5, n, 4))
                power(pool_ffn, rstd_f, var_f)

            with pool.Fori(0, B) as i:
                for r in range(2):
                    pre_pool(i, r)
                    ffn_pool(i, r)
            meet(pool, 3)

            pool.memset(wide_x, 0.0).then_inc(const5, 1)
            pool.memset(xpad[:, :, 0:1], 0.0).then_inc(const5, 1)
            pool.memset(ones4, 1.0).then_inc(prep5, 1)
            pool.memset(xpad[:, :, S + 1:S + 2], 0.0).then_inc(prep5, 1)
            pool.sem_inc(pool5, 12)
            wide8 = lambda a: a.unsqueeze(1).to_broadcast([P, ST, D])

            def power8(in_, out_):
                pool.tensor_tensor(out_, in_, half[:, 0:ST], ALU.pow).then_inc(pool5, 1)

            pool.wait_ge(w5_in, W5_IN)
            with pool.Fori(0, B) as b:
                pool.wait_ge(x5_in, 16 * (b + 1))
                pool.wait_ge(dve5, before(30, b, 19))
                pool.tensor_tensor(xob, xr, wide8(outb_b), ALU.add).then_inc(pool5, 1)
                pool.wait_ge(dve5, now(30, b, 3))
                power8(var5, rstd5)
                pool.wait_ge(dve5, now(30, b, 4))
                pool.tensor_tensor(m5, n5, wide8(ln1g_b), ALU.mult).then_inc(pool5, 1)
                pool.wait_ge(pool5, now(12, b, 3))
                pool.wait_ge(x3_out, 16 * b)
                pool.wait_ge(pe5, before(20, b, 19))
                pool.tensor_tensor(h5, m5, wide8(ln1b_b), ALU.add).then_inc(pool5, 1)
                pool.wait_ge(act5, now(21, b, 9))
                pool.wait_ge(dve5, now(30, b, 10))
                pool.tensor_tensor(v, v, mixed, ALU.mult).then_inc(pool5, 1)
                for k in range(KD):
                    pool.wait_ge(dve5, now(30, b, 14 + k))
                    pool.wait_ge(act5, now(21, b, 10 + k))
                    pool.tensor_tensor(ct[:, k], ct[:, k], state[:, k], ALU.mult).then_inc(pool5, 1)
                pool.wait_ge(dve5, now(30, b, 19))
                pool.tensor_tensor(wide_x, x2, wide8(f2b_b), ALU.add).then_inc(pool5, 1)
                pool.wait_ge(dve5, now(30, b, 22))
                power8(var5, rstd5)
                pool.wait_ge(dve5, now(30, b, 23))
                pool.tensor_tensor(m5, n5, wide8(ln2g_b), ALU.mult).then_inc(pool5, 1)
                pool.wait_ge(pool5, now(12, b, 10))
                pool.tensor_tensor(h5, m5, wide8(ln2b_b), ALU.add).then_inc(pool5, 1)
                pool.wait_ge(dve5, now(30, b, 28))
                power8(var5, rstd5)
            meet(pool, 4)

            pool.memset(ones6, 1.0).then_inc(const6, 1)
            pool.wait_ge(const6, 1)
            pool.affine_select(out=below, in_=ones6, compare_op=ALU.is_gt, fill=0.0, base=0,
                               pattern=[[1, P]], channel_multiplier=-1).then_inc(const6, 1)
            for s in range(2):
                pool.wait_ge(idx6, s + 1)
                for c in range(TILES):
                    pool.indirect_dma_start(out=xe, out_offset=bass.IndirectOffsetOnAxis(ap=idx[s][:, c:c + 1], axis=0),
                                            in_=x_all[:, c, :], in_offset=None,
                                            bounds_check=E * CAP - 1, oob_is_err=False).then_inc(sent6, 16)
            for r in range(2):
                pool.wait_ge(y_out[r], 16 * (E // 2))

            def fetch(c):
                for s in range(2):
                    for j in range(TPC):
                        q = TPC * c + j
                        pool.indirect_dma_start(out=y_g[s][:, q, :], out_offset=None, in_=ye,
                                                in_offset=bass.IndirectOffsetOnAxis(ap=idx[s][:, q:q + 1], axis=0)).then_inc(got6[c], 16)

            fetch(0)
            for c in range(TILES // TPC):
                if c + 1 < TILES // TPC:
                    fetch(c + 1)
                pool.wait_ge(fin6, 6 * c + 5)
                pool.tensor_tensor(rstd6, var6, half[:, 0:TPC], ALU.pow).then_inc(pow6, 1)
            meet(pool, 5)

        @block.scalar
        def _(act):
            act.wait_ge(s_w, 16 * W_DMAS)
            act.wait_ge(s_fscale, 2)

            def chunk(b, r):
                n = 2 * b + r
                act.wait_ge(s_xT, n + 1)
                act.wait_ge(s_proj, 5 * n)
                act.activation(xT[:, 0, :], bank(0), ACT.Copy).then_inc(s_xTs, 1)
                act.wait_ge(s_rest, 5 * n)
                act.wait_ge(s_qq, n)
                for f in range(4):
                    act.wait_ge(s_proj, 5 * n + f + 1)
                    act.activation(feat[:, f, :], bank(2 + f), ACT.Identity, bias=bqk[:, f:f + 1]).then_inc(s_feat, 1)
                act.wait_ge(s_st[r], 96 * b)
                for f in range(4):
                    act.wait_ge(s_feat, 5 + 5 * n + f + 1)
                    act.activation(planes[r][:, f, 0, :], feat[:, f, :], ACT.Copy,
                                   scale=SCORE_SCALE if f < 2 else 1.0).then_inc(s_hi, 1)
                for f in range(4):
                    act.wait_ge(s_rest, 5 * n + f + 1)
                    act.activation(planes[r][:, f, 1, :], rest[:, f, :], ACT.Copy).then_inc(s_mid, 1)
                act.wait_ge(s_fT, n + 1)
                act.activation(feat[:, 4, :], bank(1), ACT.Copy, scale=fscale).then_inc(s_feat, 1)
                act.wait_ge(s_feat, 5 + 5 * n + 5)
                act.activation(planes[r][:, 4, 0, :], feat[:, 4, :], ACT.Copy).then_inc(s_hi, 1)
                act.wait_ge(s_rest, 5 * n + 5)
                act.activation(planes[r][:, 4, 1, :], rest[:, 4, :], ACT.Copy).then_inc(s_mid, 1)

            act.sem_inc(s_feat, 5)
            with act.Fori(0, B) as b:
                for r in range(2):
                    chunk(b, r)
            meet(act, 1)

            act.sem_inc(exp_made, UNITS)
            act.sem_inc(ev_a, 1)

            def evac(g, u):
                act.wait_ge(tr_made, 4 + 32 * g + 2 * u + 1)
                act.wait_ge(pv_made, 16 * g + u + 1)
                act.activation(pT[u % 2][:, 0:4, :], bank(4), ACT.Copy).then_inc(ev_a, 1)

            with act.Fori(0, PAIRS) as g:
                for u in range(UNITS):
                    act.wait_ge(score_made, 32 * g + u + 1)
                    if u >= 2:
                        act.wait_ge(score_used, 32 * g + u + 1)
                    act.activation(sn[u % 2], bank(2 * (u % 2), 2), ACT.Sin, scale=SIN_SCALE).then_inc(sin_made, 1)
                for u in range(UNITS):
                    act.wait_ge(score_used, 2 + 32 * g + 16 + u + 1)
                    act.wait_ge(tr_made, 32 * g + 2 * u + 2)
                    act.activation(pr[u % 2], logits[:, u, :], ACT.Exp, scale=-1.0, bias=nmax[:, u:u + 1],
                                   accum_out=rsum[:, u:u + 1]).then_inc(exp_made, 1)
                    if u >= 1:
                        evac(g, u - 1)
                evac(g, UNITS - 1)
            meet(act, 2)

            act.preload_act_table_set("silu_and_others")
            act.sem_inc(act_pre, 6)
            act.sem_inc(act_silu, 6)
            act.wait_ge(prep_pe, 1)
            act.activation(w1T.rearrange("p k n -> p (k n)"), bank(0, 4), ACT.Copy).then_inc(prep_act, 1)
            act.activation(wqoT[:, :, 0:NQ], bank(4)[:, 0:FK * NQ].rearrange("p (k q) -> p k q", q=NQ), ACT.Copy).then_inc(prep_act, 1)
            act.wait_ge(prep_pe, 2)
            act.activation(w1m.rearrange("p k n -> p (k n)"), bank(5)[:, 0:2 * NQ], ACT.Copy).then_inc(prep_act, 1)
            act.activation(qm_row[0:1], bank(5)[0:1, 2 * NQ:3 * NQ], ACT.Copy).then_inc(prep_act, 1)
            act.activation(w2q[0:NQ + 1], bank(6)[0:NQ + 1, 0:D], ACT.Copy).then_inc(prep_act, 1)
            for m, dst in enumerate((wgT, wuT, wdT)):
                act.wait_ge(prep_pe, 3 + m)
                act.activation(dst.rearrange("p k n -> p (k n)"), bank(4 * (m % 2), 3), ACT.Copy).then_inc(prep_act, 1)

            def pre_act(i, r):
                n = 2 * i + r
                act.wait_ge(pre_pe, now(7, n, 1))
                act.activation(aT.rearrange("p k n -> p (k n)"), bank(0, 2), ACT.Copy).then_inc(act_pre, 1)
                act.wait_ge(pre_pe, now(7, n, 3))
                act.activation(x1T.rearrange("p k n -> p (k n)"), bank(0, 2), ACT.Copy).then_inc(act_pre, 1)
                act.wait_ge(pre_pe, now(7, n, 4))
                act.wait_ge(dve_pre, now(21, n, 8))
                act.activation(th, bank(2)[:, 0:TPC * NQ], ACT.Tanh).then_inc(act_pre, 1)
                act.wait_ge(dve_pre, now(21, n, 10))
                act.activation(cs, turns, ACT.Sin).then_inc(act_pre, 1)
                act.wait_ge(pre_pe, now(7, n, 5))
                act.activation(qeT[0:NQ + 1], bank(3)[0:NQ + 1, :], ACT.Copy).then_inc(act_pre, 1)
                act.wait_ge(pre_pe, now(7, n, 7))
                act.activation(xpT[r].rearrange("p k n -> p (k n)"), bank(2, 2), ACT.Copy).then_inc(act_pre, 1)

            def ffn_act(i, r, a, z):
                n = 2 * i + r
                for m in range(a, z):
                    act.wait_ge(ffn_pe, now(7, n, m + 1))
                    act.wait_ge(h_made, now(6, n, m - 1))
                    act.activation(sg[m % 2], bank(4 + 2 * (m % 2)), ACT.Silu, scale=1.0 / 127.0).then_inc(act_silu, 1)

            with act.Fori(0, B) as i:
                for r in range(2):
                    pre_act(i, r)
                    ffn_act(i, r, 0, HT)
            meet(act, 3)

            act.wait_ge(w5_in, W5_IN)
            act.activation(a_neg, a_neg, ACT.Exp).then_inc(prep5_act, 1)
            act.wait_ge(prep5_act, 1)
            act.activation(a_neg, a_neg, ACT.Copy, scale=-1.0).then_inc(prep5_act, 1)
            act.wait_ge(prep5_pe, 1)
            act.activation(rt_wT, bank(0)[:, 0:KD * E].rearrange("p (k e) -> p k e", e=E), ACT.Copy).then_inc(prep5_act, 1)
            act.wait_ge(prep5_act, 3)
            act.sem_inc(act5, 21)
            seq = lambda k: slice(k * S, (k + 1) * S)

            def made(ins):
                ins.then_inc(act5, 1)

            with act.Fori(0, B) as b:
                act.wait_ge(pe5, now(20, b, 1))
                made(act.activation(T5.rearrange("p k n -> p (k n)"), bank(0, 4), ACT.Copy))
                act.wait_ge(prep5, 2)
                for k in range(KD):
                    act.wait_ge(pe5, now(20, b, 2 + k))
                    made(act.activation(xpad[:, k, 1:S + 1], bank(4 + 2 * k, 2), ACT.Identity, bias=in_b[:, k:k + 1]))
                for k in range(KD):
                    act.wait_ge(pe5, now(20, b, 4 + k))
                    made(act.activation(gate[:, k], bank(2 * k, 2), ACT.Sigmoid, bias=in_b[:, 2 + k:3 + k]))
                for k in range(KD):
                    act.wait_ge(pe5, now(20, b, 6 + k))
                    made(act.activation(z[:, k], bank(4 + 2 * k, 2), ACT.Identity, bias=dt_b[:, k:k + 1]))
                for k in range(KD):
                    act.wait_ge(pe5, now(20, b, 8 + k))
                    made(act.activation(v[:, k], bank(2 * k, 2), ACT.Tanh, bias=b_b[:, k:k + 1]))
                for k in range(KD):
                    act.wait_ge(pe5, now(20, b, 10 + k))
                    made(act.activation(ct[:, k], bank(4 + 2 * k, 2), ACT.Tanh, bias=c_b[:, k:k + 1]))
                act.preload_act_table_set("natural_log_exp_and_others")
                act.wait_ge(dve5, now(30, b, 11))
                made(act.activation(l, l, ACT.Exp))
                act.wait_ge(act5, now(21, b, 12))
                made(act.activation(l, l, ACT.Ln, bias=1.0))
                act.wait_ge(dve5, now(30, b, 12))
                for k in range(KD):
                    made(act.activation(decay[:, k], dt[:, k], ACT.Exp, scale=a_neg[:, k:k + 1]))
                act.wait_ge(pe5, now(20, b, 13))
                made(act.activation(T5.rearrange("p k n -> p (k n)"), bank(4, 4), ACT.Copy))
                for m in range(4):
                    act.wait_ge(pe5, now(20, b, 14 + m))
                    made(act.activation(gl[:, m], bank(2 * m, 2), ACT.Gelu, bias=f1_b[:, m:m + 1]))
                act.wait_ge(pe5, now(20, b, 19))
                made(act.activation(T5.rearrange("p k n -> p (k n)"), bank(4, 4), ACT.Copy))
            meet(act, 4)

            act.sem_inc(act6, 6)
            act.wait_ge(top6, TOP_STEPS_E)
            act.activation(p2, top2, ACT.Exp).then_inc(exp6, 1)
            act.preload_act_table_set("silu_and_others")
            with act.Fori(0, E // 2) as i:
                for r in range(2):
                    e = 2 * i + r
                    act.wait_ge(pe6, now(6, e, 1))
                    act.wait_ge(pe6, before(6, e, 5))
                    act.activation(XT.rearrange("p k n -> p (k n)"), bank(0, 2), ACT.Copy).then_inc(act6, 1)
                    for m in range(4):
                        act.wait_ge(pe6, now(6, e, 2 + m))
                        act.wait_ge(dve6, now(4, e, m - 1))
                        act.activation(sg6[m % 2], bank(3 + 2 * (m % 2)), ACT.Silu).then_inc(act6, 1)
                    act.wait_ge(pe6, now(6, e, 6))
                    act.wait_ge(y_out[r], 16 * i)
                    act.activation(ye_s[r].rearrange("p j n -> p (j n)"), bank(6, 2), ACT.Copy).then_inc(act6, 1)
            meet(act, 5)

        @block.vector
        def _(dve):
            dve.memset(fscale[0:64], -FID_SCALE).then_inc(s_fscale, 1)
            dve.memset(fscale[64:128], 1.0).then_inc(s_fscale, 1)
            dve.sem_inc(s_v, 1)
            dve.wait_ge(s_w, 16 * W_DMAS)

            def split(b, r, f):
                n = 2 * b + r
                dve.wait_ge(s_hi, 5 * n + f + 1)
                dve.scalar_tensor_tensor(out=rest[:, f, :], in0=feat[:, f, :], scalar=SCORE_SCALE if f < 2 else 1.0,
                                         in1=planes[r][:, f, 0, :], op0=ALU.mult, op1=ALU.subtract).then_inc(s_rest, 1)

            def low(b, r, f):
                n = 2 * b + r
                dve.wait_ge(s_mid, 5 * n + f + 1)
                dve.tensor_tensor(planes[r][:, f, 2, :], rest[:, f, :], planes[r][:, f, 1, :],
                                  ALU.subtract).then_inc(s_lo, 1)

            def chunk(b, r):
                n = 2 * b + r
                dve.wait_ge(s_xT, n + 1)
                dve.wait_ge(s_proj, 5 * n)
                dve.tensor_copy(xT[:, 1, :], bank(1)).then_inc(s_xTs, 1)
                dve.wait_ge(s_lo, 5 * n)
                dve.wait_ge(s_mid, 5 * n)
                for f in range(4):
                    split(b, r, f)
                dve.wait_ge(s_qq, n + 1)
                dve.wait_ge(s_fT, n)
                dve.tensor_tensor(qk, bank(0).rearrange("p (j n) -> p j n", j=TPC),
                                  bcb.unsqueeze(1).to_broadcast([P, TPC, P]), ALU.add).then_inc(s_qkb, 1)
                dve.wait_ge(s_qkb, n + 1)
                dve.tensor_tensor(qk2, qk, qk, ALU.mult).then_inc(s_sq, 1)
                dve.wait_ge(s_proj, 5 * n + 5)
                dve.tensor_tensor(V[:, bass.ds(4 * n, TPC), :], bank(6, 2).rearrange("p (j n) -> p j n", j=TPC),
                                  bvb.unsqueeze(1).to_broadcast([P, TPC, D]), ALU.add).then_inc(s_v, 1)
                dve.wait_ge(s_sq, 3 * n + 1)
                dve.tensor_reduce(ss, qk2.rearrange("p j (g q) -> p (j g) q", q=NQ), AX.X, ALU.add).then_inc(s_sq, 1)
                dve.wait_ge(s_sq, 3 * n + 2)
                dve.tensor_scalar(ss, ss, TINY, None, ALU.max).then_inc(s_ss, 1)
                for f in range(4):
                    low(b, r, f)
                dve.wait_ge(s_rn, n + 1)
                dve.tensor_tensor(qk.rearrange("p j (g q) -> p (j g) q", q=NQ),
                                  qk.rearrange("p j (g q) -> p (j g) q", q=NQ),
                                  rn.unsqueeze(2).to_broadcast([P, TPC * 2 * H, NQ]), ALU.mult).then_inc(s_qn, 1)
                dve.sem_inc(s_sq, 1)
                split(b, r, 4)
                low(b, r, 4)

            with dve.Fori(0, B) as b:
                for r in range(2):
                    chunk(b, r)
            meet(dve, 1)

            dve.sem_inc(score_used, 2)
            dve.sem_inc(ev_d, 1)
            dve.sem_inc(att_made, 1)

            def evac(g, u):
                dve.wait_ge(tr_made, 4 + 32 * g + 2 * u + 2)
                dve.wait_ge(pv_made, 16 * g + u + 1)
                dve.tensor_copy(pT[u % 2][:, 4:8, :], bank(5)).then_inc(ev_d, 1)

            with dve.Fori(0, B) as b:
                with dve.Fori(0, H // 2) as hp:
                    g = 4 * b + hp
                    for u in range(UNITS):
                        dve.wait_ge(sin_made, 16 * g + u + 1)
                        dve.wait_ge(exp_made, 16 * g + u + 1)
                        dve.scalar_tensor_tensor(out=logits[:, u, :], in0=sn[u % 2], scalar=10.0,
                                                 in1=bank(2 * (u % 2), 2), op0=ALU.add, op1=ALU.mult).then_inc(score_used, 1)
                    for u in range(UNITS):
                        dve.wait_ge(score_made, 32 * g + 16 + u + 1)
                        dve.wait_ge(score_used, 2 + 32 * g + u + 1)
                        dve.sem_inc(passed, 1)
                        dve.tensor_tensor_reduce(out=logits[:, u, :], in0=logits[:, u, :], in1=bank(2 * (u % 2), 2),
                                                 scale=1.0, scalar=3.0e38, op0=ALU.add, op1=ALU.min,
                                                 accum_out=nmax[:, u:u + 1]).then_inc(score_used, 1)
                        if u >= 2:
                            evac(g, u - 2)
                    evac(g, UNITS - 2)
                    evac(g, UNITS - 1)
                    dve.wait_ge(exp_made, 16 * g + 32)
                    dve.reciprocal(rinv, rsum).then_inc(rinv_made, 1)
                    dve.wait_ge(rinv_made, g + 1)
                    dve.wait_ge(pv_made, 2 + 16 * g + 16)
                    for hh in range(2):
                        dve.tensor_tensor(att[:, bass.ds(8 * b, ST), bass.ds(64 * hp + 32 * hh, HD)],
                                          bank(6)[:, hh * 256:hh * 256 + 256].rearrange("p (s d) -> p s d", d=HD),
                                          rinv[:, 8 * hh:8 * hh + 8].unsqueeze(2).to_broadcast([P, ST, HD]),
                                          ALU.mult).then_inc(att_made, 1)
            meet(dve, 2)

            dve.sem_inc(dve_pre, 21)
            dve.sem_inc(h_made, 6)
            dve.sem_inc(dve_out, 5)
            dve.memset(qe[:, :, NQ:NQ + 1], 1.0).then_inc(qe_one, 1)
            dve.wait_ge(w3_in, W3_IN)
            dve.tensor_copy(floats, ints).then_inc(prep_dve, 1)

            def step(done, v):
                def then(ins):
                    v[0] += 1
                    ins.then_inc(done, 1)
                    dve.wait_ge(done, v[0])
                then.count = v
                return then

            def normal(then, src, dst, got, v, st, mo, va, rs, tiles_, before_last=None):
                for j in range(tiles_):
                    last = dve.bn_stats(st[:, j, :], src[:, j, :])
                then(last)
                dve.sem_inc(passed, 1)
                for j in range(tiles_):
                    last = dve.bn_aggr(mo[:, j, :], st[:, j, :])
                then(last)
                then(dve.tensor_scalar(va[:, 0:tiles_], mo[:, 0:tiles_, 1], LN_EPS, None, ALU.add))
                dve.wait_ge(got, v)
                if before_last:
                    before_last()
                for j in range(tiles_):
                    last = dve.tensor_scalar(dst[:, j, :], src[:, j, :], mo[:, j, 0:1], rs[:, j:j + 1], ALU.subtract, ALU.mult)
                then(last)

            flat = lambda a: a.rearrange("p j n -> p (j n)")

            def pre_dve(i, r):
                n = 2 * i + r
                then = step(dve_pre, [now(21, n, 0)])
                dve.wait_ge(pre_pe, now(7, n, 2))
                dve.wait_ge(pool_pre, now(8, n, 1))
                then(dve.tensor_tensor(flat(r1), bank(2, 2), flat(xbo), ALU.add))
                normal(then, r1, n1, pool_pre, now(8, n, 3), stats, moments, var, rstd, TPC)
                dve.wait_ge(pre_pe, now(7, n, 4))
                qm = bank(2)[:, 0:TPC * NQ]
                then(dve.tensor_scalar(turns, qm, 0.125, ROUND, ALU.mult, ALU.add))
                then(dve.tensor_scalar(turns, turns, ROUND, -8.0, ALU.subtract, ALU.mult))
                then(dve.tensor_tensor(turns, qm, turns, ALU.add))
                then(dve.scalar_tensor_tensor(out=turns, in0=turns, scalar=-1.0, in1=turns, op0=ALU.mult, op1=ALU.max))
                then(dve.tensor_scalar(turns, turns, -PI / 4, PI / 2, ALU.mult, ALU.add))
                dve.wait_ge(act_pre, now(6, n, 4))
                then(dve.tensor_tensor(qe[:, :, 0:NQ], th.rearrange("p (j q) -> p j q", q=NQ),
                                       cs.rearrange("p (j q) -> p j q", q=NQ), ALU.mult))
                dve.wait_ge(pre_pe, now(7, n, 6))
                then(dve.tensor_tensor(flat(r2), bank(0, 2), flat(x1), ALU.add))
                normal(then, r2, n2, pool_pre, now(8, n, 6), stats, moments, var, rstd, TPC)
                dve.wait_ge(pool_pre, now(8, n, 7))
                then(dve.tensor_tensor(flat(r3), flat(m2), flat(xb2), ALU.add))
                normal(then, r3, xp[r], pool_pre, now(8, n, 8), stats, moments, var, rstd, TPC)

            def ffn_dve(i, r, a, z):
                n = 2 * i + r
                for m in range(a, z):
                    dve.wait_ge(act_silu, now(6, n, m + 1))
                    if m == 0:
                        dve.wait_ge(ffn_pe, before(7, n, 7))
                    dve.scalar_tensor_tensor(out=hT[:, m, :], in0=bank(5 + 2 * (m % 2)), scalar=1.0 / 127.0, in1=sg[m % 2],
                                             op0=ALU.mult, op1=ALU.mult).then_inc(h_made, 1)

            def out_dve(i, r):
                n = 2 * i + r
                then = step(dve_out, [now(5, n, 0)])
                dve.wait_ge(ffn_pe, now(7, n, 7))
                then(dve.scalar_tensor_tensor(out=flat(r4), in0=bank(4, 2), scalar=1.0 / 127.0, in1=flat(xp[r]),
                                              op0=ALU.mult, op1=ALU.add))
                normal(then, r4, xo[r], pool_ffn, now(1, n, 1), stats_f, moments_f, var_f, rstd_f, TPC,
                       lambda: dve.wait_ge(x_out[r], 16 * i))

            with dve.Fori(0, B) as i:
                for r in range(2):
                    pre_dve(i, r)
                    ffn_dve(i, r, 0, HT)
                    out_dve(i, r)
            meet(dve, 3)

            dve.sem_inc(dve5, 30)
            dve.wait_ge(w5_in, W5_IN)
            dve.wait_ge(zero_in, 16 * (E + 1))
            with dve.Fori(0, B) as b:
                then = step(dve5, [now(30, b, 0)])
                dve.wait_ge(x5_in, 16 * (b + 1))
                normal(then, xr, n5, pool5, now(12, b, 2), stats5, mom5, var5, rstd5, ST)
                for k in range(KD):
                    dve.wait_ge(act5, now(21, b, 2 + k))
                    then(dve.tensor_scalar(mixed[:, k], xpad[:, k, 0:S], taps[:, k, 0:1], tap_b[:, k:k + 1], ALU.mult, ALU.add))
                    for q in (1, 2):
                        then(dve.scalar_tensor_tensor(out=mixed[:, k], in0=xpad[:, k, q:S + q], scalar=taps[:, k, q:q + 1],
                                                      in1=mixed[:, k], op0=ALU.mult, op1=ALU.add))
                dve.wait_ge(act5, now(21, b, 7))
                then(dve.scalar_tensor_tensor(out=l, in0=z, scalar=-1.0, in1=z, op0=ALU.mult, op1=ALU.min))
                dve.wait_ge(act5, now(21, b, 13))
                then(dve.scalar_tensor_tensor(out=dt, in0=z, scalar=0.0, in1=l, op0=ALU.max, op1=ALU.add))
                dve.wait_ge(pool5, now(12, b, 5))
                then(dve.tensor_tensor(v, v, dt, ALU.mult))
                for k in range(KD):
                    dve.wait_ge(act5, now(21, b, 14 + k))
                    then(dve.tensor_tensor_scan(state[:, k], decay[:, k], v[:, k], 0.0, ALU.mult, ALU.add))
                for k in range(KD):
                    dve.wait_ge(pool5, now(12, b, 6 + k))
                    then(dve.scalar_tensor_tensor(out=ct[:, k], in0=mixed[:, k], scalar=skip[:, k:k + 1], in1=ct[:, k],
                                                  op0=ALU.mult, op1=ALU.add))
                then(dve.tensor_tensor(ct, ct, gate, ALU.mult))
                dve.wait_ge(pe5, now(20, b, 12))
                dve.wait_ge(pool5, now(12, b, 1))
                then(dve.tensor_tensor(flat(x2), bank(0, 4), flat(xob), ALU.add))
                normal(then, x2, n5, pool5, now(12, b, 9), stats5, mom5, var5, rstd5, ST)
                dve.wait_ge(pe5, now(20, b, 18))
                dve.wait_ge(pool5, now(12, b, 8))
                then(dve.tensor_tensor(flat(wide_x), bank(0, 4), flat(wide_x), ALU.add))
                then(dve.tensor_tensor(wide_x, wide_x, xr, ALU.add))
                normal(then, wide_x, h5, pool5, now(12, b, 12), stats5, mom5, var5, rstd5, ST)
                dve.wait_ge(pe5, now(20, b, 20))
                then(dve.tensor_copy(lg_all[:, bass.ds(ST * b, ST), :], bank(0)[:, 0:ST * E].rearrange("p (j e) -> p j e", e=E)))
            meet(dve, 4)

            top = step(top6, [0])
            over_e = lambda a: a.unsqueeze(2).to_broadcast([P, TILES, E])
            for e in range(E):
                last = dve.memset(rev[:, :, e], float(E - e))
            top(last)
            top(dve.tensor_copy(lg6, lg_all))
            for best, s, mask, src in ((top1, s1, mask1, lg6), (top2, s2, mask2, rest6)):
                top(dve.tensor_reduce(best, src, AX.X, ALU.max))
                top(dve.tensor_tensor(eq, src, over_e(best), ALU.is_equal))
                top(dve.tensor_tensor(eq, eq, rev, ALU.mult))
                top(dve.tensor_reduce(s, eq, AX.X, ALU.max))
                top(dve.tensor_tensor(mask, rev, over_e(s), ALU.is_equal))
                if src is lg6:
                    top(dve.scalar_tensor_tensor(out=rest6, in0=mask, scalar=-3.0e38, in1=src, op0=ALU.mult, op1=ALU.add))
            top(dve.tensor_tensor(both, mask1, mask2, ALU.add))
            top(dve.tensor_tensor(top2, top2, top1, ALU.subtract))
            assert top.count[0] == TOP_STEPS_E
            dve.wait_ge(count_pe, 1)
            top(dve.tensor_copy(tot, bank(1)[:, 0:TILES * E].rearrange("p (t e) -> p t e", e=E)))
            for e in range(E):
                last = dve.tensor_tensor_scan(pos[:, :, e], ones6[:, 0:TILES], tot[:, :, e], 0.0, ALU.mult, ALU.add)
            top(last)
            top(dve.tensor_tensor(pos, pos, tot, ALU.subtract))
            top(dve.tensor_tensor(pos, bank(0)[:, 0:TILES * E].rearrange("p (t e) -> p t e", e=E), pos, ALU.add))
            for k, (s, mask) in enumerate(((s1, mask1), (s2, mask2))):
                top(dve.tensor_tensor(eq, pos, mask, ALU.mult))
                top(dve.tensor_reduce(slot, eq, AX.X, ALU.add))
                top(dve.tensor_scalar(fits, slot, float(CAP), None, ALU.is_lt))
                top(dve.scalar_tensor_tensor(out=slot, in0=s, scalar=-float(CAP), in1=slot, op0=ALU.mult, op1=ALU.add))
                top(dve.tensor_tensor(slot, slot, fits, ALU.mult))
                dve.tensor_scalar(idx[k], slot, float(E * CAP), None, ALU.add).then_inc(idx6, 1)
            dve.wait_ge(exp6, 1)
            top(dve.tensor_scalar(p1, p2, 1.0, None, ALU.add))
            top(dve.reciprocal(p1, p1))
            top(dve.tensor_tensor(p2, p2, p1, ALU.mult))
            dve.sem_inc(dve6, 4)
            with dve.Fori(0, E // 2) as i:
                for r in range(2):
                    e = 2 * i + r
                    for m in range(4):
                        dve.wait_ge(act6, now(6, e, 2 + m))
                        if m == 0:
                            dve.wait_ge(pe6, before(6, e, 6))
                        dve.tensor_tensor(h6[:, m], bank(2 + 2 * (m % 2)), sg6[m % 2], ALU.mult).then_inc(dve6, 1)
            for c in range(TILES // TPC):
                r = c % 2
                then = step(fin6, [6 * c])
                dve.wait_ge(got6[c], 16 * 2 * TPC)
                for j in range(TPC):
                    q = TPC * c + j
                    last = dve.scalar_tensor_tensor(out=acc[r][:, j, :], in0=y_g[0][:, q, :], scalar=p1[:, q:q + 1],
                                                    in1=x_all[:, q, :], op0=ALU.mult, op1=ALU.add)
                then(last)
                for j in range(TPC):
                    q = TPC * c + j
                    last = dve.scalar_tensor_tensor(out=acc[r][:, j, :], in0=y_g[1][:, q, :], scalar=p2[:, q:q + 1],
                                                    in1=acc[r][:, j, :], op0=ALU.mult, op1=ALU.add)
                then(last)
                normal(then, acc[r], fin[r], pow6, c + 1, stats6, mom6, var6, rstd6, TPC,
                       (lambda: dve.wait_ge(fin_out[r], 16 * (c // 2))) if c >= 2 else None)
            meet(dve, 5)

        @block.tensor
        def _(pe):
            pe.wait_ge(s_w, 16 * W_DMAS)
            pe.wait_ge(s_const, 4)

            def chunk(b, r):
                n = 2 * b + r
                pe.wait_ge(s_x[r], 16 * (b + 1))
                pe.wait_ge(s_feat, 5 + 5 * n)
                pe.wait_ge(s_qkb, n)
                for k in range(KD):
                    for j in range(TPC):
                        last = pe.transpose(bank(k)[:, j * P:(j + 1) * P], xin[r][:, j, k * P:(k + 1) * P], ident)
                last.then_inc(s_xT, 1)
                pe.wait_ge(s_xTs, 2 * (n + 1))
                for f in range(4):
                    w = wq if f < 2 else wk
                    c = (f % 2) * P
                    for k in range(KD):
                        last = pe.matmul(bank(2 + f), w[:, k, c:c + P], xT[:, k, :], start=(k == 0), stop=(k == 1))
                    last.then_inc(s_proj, 1)
                pe.wait_ge(s_v, n + 1)
                for j in range(TPC):
                    for k in range(KD):
                        last = pe.matmul(bank(6, 2)[:, j * D:(j + 1) * D], xT[:, k, j * P:(j + 1) * P], wv[:, k, :],
                                         start=(k == 0), stop=(k == 1))
                last.then_inc(s_proj, 1)
                pe.wait_ge(s_feat, 5 + 5 * n + 4)
                for j in range(TPC):
                    for i in range(2):
                        for k in range(KD):
                            last = pe.matmul(bank(0)[:, j * P + i * 64:j * P + i * 64 + 64],
                                             feat[:, 2 * i + k, j * P:(j + 1) * P], wc[:, k, :],
                                             start=(k == 0), stop=(k == 1))
                last.then_inc(s_qq, 1)
                pe.wait_ge(s_qn, n + 1)
                for j in range(TPC):
                    last = pe.transpose(bank(1)[:, j * P:(j + 1) * P], qk[:, j, :], ident)
                last.then_inc(s_fT, 1)

            with pe.Fori(0, B) as b:
                for r in range(2):
                    chunk(b, r)
            meet(pe, 1)

            pe.sem_inc(tr_made, 4)
            pe.sem_inc(pv_made, 2)

            def turn(g, u):
                pe.wait_ge(exp_made, 16 + 16 * g + u + 1)
                for half_, ev in ((0, ev_a), (1, ev_d)):
                    pe.wait_ge(ev, 16 * g + u + 1)
                    for j in range(4):
                        c = (4 * half_ + j) * P
                        last = pe.transpose(bank(4 + half_)[:, j * P:(j + 1) * P], pr[u % 2][:, c:c + P], ident)
                    last.then_inc(tr_made, 1)

            def weigh(b, hp, g, u):
                pe.wait_ge(ev_a, 1 + 16 * g + u + 1)
                pe.wait_ge(ev_d, 1 + 16 * g + u + 1)
                if u == 0:
                    pe.wait_ge(att_made, 2 * g + 1)
                for tt in range(ST):
                    last = pe.matmul(bank(6)[:, u * HD:(u + 1) * HD], pT[u % 2][:, tt, :],
                                     V[:, bass.ds(8 * b + tt, 1), bass.ds(64 * hp + 32 * (u // ST), HD)].rearrange("p o d -> p (o d)"),
                                     start=(tt == 0), stop=(tt == ST - 1))
                last.then_inc(pv_made, 1)

            with pe.Fori(0, B) as b:
                with pe.Fori(0, H // 2) as hp:
                    g = 4 * b + hp
                    for u in range(UNITS):
                        hh, st = divmod(u, ST)
                        if st == 0:
                            pe.wait_ge(f_in[hh], F_IN * (g + 1))
                        pe.wait_ge(score_used, 32 * g + u + 1)
                        for c in range(2):
                            last = pe.matmul(bank(2 * (u % 2) + c), fq[hh][0:9 * NQ, st * P:(st + 1) * P],
                                             fk[hh][0:9 * NQ, c * 512:(c + 1) * 512], start=True, stop=True)
                        last.then_inc(score_made, 1)
                    for u in range(UNITS):
                        hh, st = divmod(u, ST)
                        if st == 0:
                            pe.wait_ge(c_in[hh], C_IN * (g + 1))
                        pe.wait_ge(score_used, 32 * g + 16 + u + 1)
                        for a in range(2):
                            for c in range(2):
                                last = pe.matmul(bank(2 * (u % 2) + c), qs[hh][:, a, st * P:(st + 1) * P],
                                                 ks[hh][:, a, c * 512:(c + 1) * 512], start=(a == 0), stop=(a == 1))
                        last.then_inc(score_made, 1)
                        if u >= 2:
                            turn(g, u - 2)
                        if u >= 3:
                            weigh(b, hp, g, u - 3)
                    turn(g, UNITS - 2)
                    weigh(b, hp, g, UNITS - 3)
                    turn(g, UNITS - 1)
                    weigh(b, hp, g, UNITS - 2)
                    weigh(b, hp, g, UNITS - 1)
            meet(pe, 2)

            pe.sem_inc(pre_pe, 7)
            pe.sem_inc(ffn_pe, 7)
            pe.wait_ge(w3_in, W3_IN)
            pe.wait_ge(prep_c, 3)
            pe.wait_ge(qe_one, 1)
            for k in range(FK):
                for m in range(KD):
                    pe.transpose(bank(k // 2)[:, (k % 2) * D + m * P:(k % 2) * D + (m + 1) * P], w1[:, m, k * P:(k + 1) * P], ident)
            for k in range(FK):
                last = pe.transpose(bank(4)[:, k * NQ:(k + 1) * NQ], wqo[0:NQ, k * P:(k + 1) * P], ident[0:NQ, 0:NQ])
            last.then_inc(prep_pe, 1)
            pe.wait_ge(prep_act, 2)
            for m in range(KD):
                for k in range(FK):
                    pe.matmul(bank(5)[:, m * NQ:(m + 1) * NQ], w1T[:, k, m * P:(m + 1) * P], wm[:, k, :], start=(k == 0), stop=(k == FK - 1))
            for k in range(FK):
                pe.matmul(bank(5)[0:1, 2 * NQ:3 * NQ], b1c[:, k:k + 1], wm[:, k, :], start=(k == 0), stop=False)
            pe.matmul(bank(5)[0:1, 2 * NQ:3 * NQ], ones[0:1, 0:1], bm[0:1], start=False, stop=True)
            for k in range(FK):
                pe.matmul(bank(6)[0:NQ + 1, 0:D], wqoT[:, k, :], w2[:, k, :], start=(k == 0), stop=False)
            pe.matmul(bank(6)[0:NQ + 1, 0:D], last_row[0:1], b2[0:1], start=False, stop=True).then_inc(prep_pe, 1)
            pe.wait_ge(prep_dve, 1)
            for w in range(3):
                f = floats[:, w * HT * D:(w + 1) * HT * D]
                pe.wait_ge(prep_act, 5 if w < 2 else 6)
                for a in range(12):
                    if w < 2:
                        k, m = divmod(a, HT)
                        src = tiles(f)[:, m, k * P:(k + 1) * P]
                    else:
                        k, m = divmod(a, KD)
                        src = f.rearrange("p (k n) -> p k n", k=KD)[:, m, k * P:(k + 1) * P]
                    last = pe.transpose(bank(4 * (w % 2), 3)[:, a * P:(a + 1) * P], src, ident)
                last.then_inc(prep_pe, 1)
            pe.wait_ge(prep_act, 8)

            def flip(dst, src, done):
                for k in range(KD):
                    for j in range(TPC):
                        last = pe.transpose(dst[:, k * CH + j * P:k * CH + (j + 1) * P], src[:, j, k * P:(k + 1) * P], ident)
                last.then_inc(done, 1)

            def pre_pe_1(i, r):
                n = 2 * i + r
                pe.wait_ge(c3_in[r], 32 * (i + 1))
                pe.wait_ge(dve_pre, before(21, n, 12))
                flip(bank(0, 2), attc[r], pre_pe)
                pe.wait_ge(act_pre, now(6, n, 1))
                for j in range(TPC):
                    for k in range(KD):
                        last = pe.matmul(bank(2, 2)[:, j * D:(j + 1) * D], aT[:, k, j * P:(j + 1) * P], wo[:, k, :],
                                         start=(k == 0), stop=(k == KD - 1))
                last.then_inc(pre_pe, 1)

            def pre_pe_2(i, r):
                n = 2 * i + r
                pe.wait_ge(pool_pre, now(8, n, 5))
                flip(bank(0, 2), x1, pre_pe)
                pe.wait_ge(act_pre, now(6, n, 2))
                for j in range(TPC):
                    q = bank(2)[:, j * NQ:(j + 1) * NQ]
                    for k in range(KD):
                        pe.matmul(q, x1T[:, k, j * P:(j + 1) * P], w1m[:, k, :], start=(k == 0), stop=False)
                    last = pe.matmul(q, ones[0:1], qm_row[0:1], start=False, stop=True)
                last.then_inc(pre_pe, 1)

            def pre_pe_3(i, r):
                n = 2 * i + r
                pe.wait_ge(dve_pre, now(21, n, 11))
                for j in range(TPC):
                    last = pe.transpose(bank(3)[0:NQ + 1, j * P:(j + 1) * P], qe[:, j, :], ident)
                last.then_inc(pre_pe, 1)
                pe.wait_ge(act_pre, now(6, n, 5))
                for j in range(TPC):
                    last = pe.matmul(bank(0, 2)[:, j * D:(j + 1) * D], qeT[0:NQ + 1, j * P:(j + 1) * P], w2q[0:NQ + 1, :],
                                     start=True, stop=True)
                last.then_inc(pre_pe, 1)

            def pre_pe_4(i, r):
                n = 2 * i + r
                pe.wait_ge(dve_pre, now(21, n, 21))
                flip(bank(2, 2), xp[r], pre_pe)

            def ffn_up(i, r, a, z):
                n = 2 * i + r
                if a == 0:
                    pe.wait_ge(act_pre, now(6, n, 6))
                    pe.wait_ge(dve_out, before(5, n, 1))
                for m in range(a, z):
                    pe.wait_ge(h_made, now(6, n, m - 1))
                    for w, at in ((wgT, 4), (wuT, 5)):
                        for k in range(KD):
                            last = pe.matmul(bank(at + 2 * (m % 2)), w[:, k, m * P:(m + 1) * P], xpT[r][:, k, :],
                                             start=(k == 0), stop=(k == KD - 1))
                    last.then_inc(ffn_pe, 1)

            def ffn_down(i, r):
                n = 2 * i + r
                pe.wait_ge(h_made, now(6, n, 6))
                for j in range(TPC):
                    for m in range(HT):
                        last = pe.matmul(bank(4, 2)[:, j * D:(j + 1) * D], hT[:, m, j * P:(j + 1) * P], wdT[:, m, :],
                                         start=(m == 0), stop=(m == HT - 1))
                last.then_inc(ffn_pe, 1)

            with pe.Fori(0, B) as i:
                for r in range(2):
                    pre_pe_1(i, r)
                    pre_pe_2(i, r)
                    pre_pe_3(i, r)
                    pre_pe_4(i, r)
                    ffn_up(i, r, 0, HT)
                    ffn_down(i, r)
            meet(pe, 3)

            pe.wait_ge(w5_in, W5_IN)
            for k in range(KD):
                last = pe.transpose(bank(0)[:, k * E:(k + 1) * E], rt_w[0:E, k * P:(k + 1) * P], ident[0:E, 0:E])
            last.then_inc(prep5_pe, 1)
            pe.wait_ge(prep5_act, 3)
            pe.wait_ge(prep5, 2)
            pe.sem_inc(pe5, 20)

            def flip8(at, src):
                for k in range(KD):
                    for j in range(ST):
                        last = pe.transpose(bank(at, 4)[:, k * S + j * P:k * S + (j + 1) * P], src[:, j, k * P:(k + 1) * P], ident)
                last.then_inc(pe5, 1)

            def project(at, w, m, src):
                for c in range(2):
                    for k in range(KD):
                        last = pe.matmul(bank(at + c), w[:, k, m * P:(m + 1) * P], src[:, k, c * CH:(c + 1) * CH],
                                         start=(k == 0), stop=(k == KD - 1))
                last.then_inc(pe5, 1)

            with pe.Fori(0, B) as b:
                pe.wait_ge(pool5, now(12, b, 4))
                pe.wait_ge(dve5, before(30, b, 30))
                flip8(0, h5)
                pe.wait_ge(act5, now(21, b, 1))
                project(4, in_w, 0, T5)
                project(6, in_w, 1, T5)
                project(0, in_w, 2, T5)
                project(2, in_w, 3, T5)
                pe.wait_ge(dve5, now(30, b, 10))
                project(4, dt_w, 0, mixed)
                project(6, dt_w, 1, mixed)
                for m in range(KD):
                    pe.wait_ge(act5, now(21, b, 4 + m))
                    project(2 * m, b_w, m, mixed)
                for m in range(KD):
                    pe.wait_ge(act5, now(21, b, 6 + m))
                    project(4 + 2 * m, c_w, m, mixed)
                pe.wait_ge(act5, now(21, b, 9))
                pe.wait_ge(dve5, now(30, b, 18))
                for j in range(ST):
                    for k in range(KD):
                        last = pe.matmul(bank(0, 4)[:, j * D:(j + 1) * D], ct[:, k, j * P:(j + 1) * P], out_w[:, k, :],
                                         start=(k == 0), stop=(k == KD - 1))
                last.then_inc(pe5, 1)
                pe.wait_ge(act5, now(21, b, 11))
                pe.wait_ge(pool5, now(12, b, 11))
                flip8(4, h5)
                pe.wait_ge(act5, now(21, b, 16))
                pe.wait_ge(dve5, now(30, b, 19))
                for m in range(4):
                    project(2 * m, f1_w, m, T5)
                pe.wait_ge(act5, now(21, b, 20))
                for j in range(ST):
                    for m in range(4):
                        last = pe.matmul(bank(0, 4)[:, j * D:(j + 1) * D], gl[:, m, j * P:(j + 1) * P], f2_w[:, m, :],
                                         start=(m == 0), stop=(m == 3))
                last.then_inc(pe5, 1)
                pe.wait_ge(dve5, now(30, b, 29))
                flip8(4, h5)
                pe.wait_ge(act5, now(21, b, 21))
                for j in range(ST):
                    q = bank(0)[:, j * E:(j + 1) * E]
                    for k in range(KD):
                        pe.matmul(q, T5[:, k, j * P:(j + 1) * P], rt_wT[:, k, :], start=(k == 0), stop=False)
                    last = pe.matmul(q, ones4[0:1], rt_b[0:1], start=False, stop=True)
                last.then_inc(pe5, 1)
            meet(pe, 4)

            pe.wait_ge(const6, 2)
            pe.wait_ge(top6, TOP_STEPS_E)
            both_f = both.rearrange("p t e -> p (t e)")
            pe.matmul(bank(0)[:, 0:TILES * E], below, both_f, start=True, stop=True)
            pe.matmul(bank(1)[:, 0:TILES * E], ones6, both_f, start=True, stop=True).then_inc(count_pe, 1)
            pe.sem_inc(pe6, 6)
            pe.wait_ge(idx6, 2)
            with pe.Fori(0, E // 2) as i:
                for r in range(2):
                    e = 2 * i + r
                    pe.wait_ge(e_in[r], 64 * (i + 1))
                    pe.wait_ge(act6, before(6, e, 1))
                    flip(bank(0, 2), xe_s[r], pe6)
                    pe.wait_ge(act6, now(6, e, 1))
                    for m in range(4):
                        pe.wait_ge(dve6, now(4, e, m - 1))
                        for w, at in ((we[r], 2), (ve[r], 3)):
                            for k in range(KD):
                                last = pe.matmul(bank(at + 2 * (m % 2)), w[:, k, m * P:(m + 1) * P], XT[:, k, :],
                                                 start=(k == 0), stop=(k == KD - 1))
                        last.then_inc(pe6, 1)
                    pe.wait_ge(dve6, now(4, e, 4))
                    pe.wait_ge(act6, before(6, e, 6))
                    for j in range(TPC):
                        for m in range(4):
                            last = pe.matmul(bank(6, 2)[:, j * D:(j + 1) * D], h6[:, m, j * P:(j + 1) * P], woe[r][:, m, :],
                                             start=(m == 0), stop=(m == 3))
                    last.then_inc(pe6, 1)
            meet(pe, 5)


_OUTS = [((B, S, D), "float32")]


def kernel(**inputs):
    import numpy as _np
    import concourse.bacc as _bacc
    from concourse import mybir as _mybir
    from concourse.bass_utils import run_bass_kernel_spmd as _run

    nc = _bacc.Bacc("TRN2", target_bir_lowering=False, num_devices=1)
    arrays, t = {}, {}
    for name in inputs:
        a = _np.ascontiguousarray(inputs[name])
        arrays["in_" + name] = a
        t[name] = nc.dram_tensor("in_" + name, a.shape, _mybir.dt.from_np(a.dtype), kind="ExternalInput").ap()
    out = nc.dram_tensor("out", (B, S, D), F32, kind="ExternalOutput").ap()
    build_program(nc, t, out)
    r = _run(nc, [arrays], core_ids=[0])
    return r.results[0]["out"]
```

```python
import concourse.bass as bass
from concourse import mybir
from concourse.alu_op_type import AluOpType as ALU
from contextlib import ExitStack

ACT = mybir.ActivationFunctionType
AX = mybir.AxisListType
F32 = mybir.dt.float32
BF16 = mybir.dt.bfloat16
I32 = mybir.dt.int32
U32 = mybir.dt.uint32

P = 128
B, S, D = 4, 1024, 256
N = B * S
TILES = N // P
H, HD, NQ = 8, 32, 8
KD = D // P
CH = 512
TPC = CH // P
ST = S // P
PAIRS = B * H // 2
UNITS = 2 * ST
FID_SCALE = 0.05
SIN_SCALE = float(-3.14159265 / FID_SCALE * (1.0 - 4e-7))
SIN_TURNS = {0: 7, 1: 8, 3: 9, 5: 10, 7: 11, 9: 12, 11: 13, 13: 14, 15: 15}
SIN_QUADS, SIN_FOLDS = {2: (1, 0), 4: (1, 1), 10: (2, 0), 12: (2, 1)}, {6: 1, 14: 2}
EXP_TURNS = {3: 0, 5: 1, 7: 2, 9: 3, 11: 4, 13: 5, 15: 6}
OLD_QUAD, OLD_FOLD, OWN_QUAD, OWN_FOLD = (1, 2), 4, (12, 14), 15
SCORE_SCALE = float(-0.5 / (HD ** 0.5))
TINY = 1e-37
RSQRT_START = 1597463007.0
FF, FK, HID, HT = 1024, 8, 768, 6
LN_EPS = 1e-5
ROUND = 12582912.0
PI = 3.141592653589793
W3_IN = 16 * (15 + 16)
E, CAP = 8, 512
TOP_STEPS_E = 15
C3_IN = 5 * 16
ZEROS = 17408
W5_IN = 16 * (15 + 8 + 2 * 7)
W_DMAS = 6 + 4 + 1 + 2 + 8


def now(per, n, k):
    return per * (n + 1) + k


def before(per, n, k):
    return per * n + k


def build_program(nc, t, out):
    ctx = ExitStack()
    with ctx:
        def sem(name):
            return ctx.enter_context(nc.semaphore(name))

        arena = ctx.enter_context(nc.sbuf_tensor("arena", [P, 51200], F32))
        banks = ctx.enter_context(nc.psum_tensor("banks", [P, 8 * 512], F32))

        def fp(at, n):
            return arena[:, at:at + n]

        def bank(i, n=1):
            return banks[:, i * 512:(i + n) * 512]

        q_planes = nc.dram_tensor("q_planes", [3, B * H, HD, S], BF16, kind="Internal").ap()
        k_planes = nc.dram_tensor("k_planes", [3, B * H, HD, S], BF16, kind="Internal").ap()
        fq_planes = nc.dram_tensor("fq_planes", [3, B * H, NQ, S], BF16, kind="Internal").ap()
        fk_planes = nc.dram_tensor("fk_planes", [3, B * H, NQ, S], BF16, kind="Internal").ap()

        ident = fp(0, 128)
        fscale = fp(128, 1)
        q_norms, k_norms = (fp(1024 + i * B * H * ST, B * H * ST).rearrange("p (h s) -> p h s", s=ST) for i in range(2))
        rsum = fp(136, UNITS)
        rinv = fp(152, UNITS)
        nmax = fp(168, UNITS)
        v_pairs = nc.dram_tensor("v_pairs", [PAIRS, S, 2 * HD], F32, kind="Internal").ap()
        att_pairs = nc.dram_tensor("att_pairs", [PAIRS, S, 2 * HD], F32, kind="Internal").ap()
        R3 = 18432

        o = R3
        def take(n):
            nonlocal o
            o += n
            return fp(o - n, n)
        wq = take(KD * D).rearrange("p (k n) -> p k n", k=KD)
        wk = take(KD * D).rearrange("p (k n) -> p k n", k=KD)
        wv = take(KD * D).rearrange("p (k n) -> p k n", k=KD)
        wc = take(KD * H * NQ).rearrange("p (k n) -> p k n", k=KD)
        bqk = take(4)
        bvb = take(D)
        bcb = take(2 * H * NQ)
        half = fp(256, 64)
        xin = [take(TPC * D).rearrange("p (j n) -> p j n", j=TPC) for _ in range(2)]
        xT = take(KD * CH).rearrange("p (k n) -> p k n", k=KD)
        feat = take(5 * CH).rearrange("p (f n) -> p f n", f=5)
        rest = take(5 * CH).rearrange("p (f n) -> p f n", f=5)
        planes = [take(5 * 3 * CH // 2).bitcast(BF16).rearrange("p (f l n) -> p f l n", f=5, l=3) for _ in range(2)]
        qk = take(TPC * P).rearrange("p (j n) -> p j n", j=TPC)
        qk2 = take(TPC * P).rearrange("p (j n) -> p j n", j=TPC)
        ss = take(TPC * 2 * H)
        rn = take(TPC * 2 * H)
        rn2 = take(TPC * 2 * H)
        assert o <= 51200

        v_out = [take(TPC * D).rearrange("p (j n) -> p j n", j=TPC) for _ in range(2)]
        assert o <= 51200

        o = 2048
        logits = take(UNITS * S).rearrange("p (u n) -> p u n", u=UNITS)
        fq = [take(S // 2).bitcast(BF16) for _ in range(2)]
        fk = [take(S // 2).bitcast(BF16) for _ in range(2)]
        qs = [take(S).bitcast(BF16).rearrange("p (a n) -> p a n", a=2) for _ in range(2)]
        ks = [take(S).bitcast(BF16).rearrange("p (a n) -> p a n", a=2) for _ in range(2)]
        sn = [take(S) for _ in range(2)]
        pT = [take(ST * 4 * P).rearrange("p (t n) -> p t n", t=ST) for _ in range(2)]
        v_pair = take(ST * 2 * HD).rearrange("p (t n) -> p t n", t=ST)
        o_sum = take(4 * P)
        att_s = take(ST * 2 * HD).rearrange("p (t n) -> p t n", t=ST)
        fold = take(HD)
        assert o <= 51200

        o = 2048
        wo = take(KD * D).rearrange("p (k n) -> p k n", k=KD)
        wgT = take(KD * HID).rearrange("p (k n) -> p k n", k=KD)
        wuT = take(KD * HID).rearrange("p (k n) -> p k n", k=KD)
        wdT = take(HT * D).rearrange("p (k n) -> p k n", k=HT)
        w1m = take(KD * NQ).rearrange("p (k n) -> p k n", k=KD)
        qm_row = take(NQ)
        w2q = take(D)
        ones = take(P)
        last_row = take(NQ + 1)
        bo_b, g1_b, be1_b, g2_b, be2_b = (take(D) for _ in range(5))
        assert o <= 10240
        o = R3
        tiles = lambda a: a.rearrange("p (j n) -> p j n", n=D)
        attc = [tiles(take(TPC * D)) for _ in range(2)]
        xc = [tiles(take(TPC * D)) for _ in range(2)]
        overlay = o
        w1 = take(KD * FF).rearrange("p (k n) -> p k n", k=KD)
        w1T = take(FK * D).rearrange("p (k n) -> p k n", k=FK)
        w2 = take(FK * D).rearrange("p (k n) -> p k n", k=FK)
        wm = take(FK * NQ).rearrange("p (k n) -> p k n", k=FK)
        b1c = take(FK)
        wqo = take(FF)
        wqoT = take(FK * (NQ + 1)).rearrange("p (k n) -> p k n", k=FK)
        bm = take(NQ)
        b2 = take(D)
        ints = take(3 * HT * D).bitcast(I32)
        floats = take(3 * HT * D)
        assert o <= 51200
        o = overlay
        xbo, xb2, r1, n1, m1, x1, r2, n2, m2, r3, r4 = (tiles(take(TPC * D)) for _ in range(11))
        xp = [tiles(take(TPC * D)) for _ in range(2)]
        xo = [tiles(take(TPC * D)) for _ in range(2)]
        aT = take(KD * CH).rearrange("p (k n) -> p k n", k=KD)
        x1T = take(KD * CH).rearrange("p (k n) -> p k n", k=KD)
        xpT = [take(KD * CH).rearrange("p (k n) -> p k n", k=KD) for _ in range(2)]
        sg = [take(CH) for _ in range(2)]
        hT = take(HT * CH).rearrange("p (k n) -> p k n", k=HT)
        turns, th, cs = (take(TPC * NQ) for _ in range(3))
        qe = take(TPC * (NQ + 1)).rearrange("p (j q) -> p j q", j=TPC)
        qeT = take(CH)
        stats = take(8 * 6).rearrange("p (j s) -> p j s", s=6)
        stats_f = take(8 * 6).rearrange("p (j s) -> p j s", s=6)
        moments = take(8 * 2).rearrange("p (j s) -> p j s", s=2)
        moments_f = take(8 * 2).rearrange("p (j s) -> p j s", s=2)
        var = take(8)
        var_f = take(8)
        rstd = take(8)
        rstd_f = take(8)
        assert o <= 51200
        x_mid = nc.dram_tensor("x_mid", [N, D], F32, kind="Internal").ap()
        x_mid_c = x_mid.rearrange("(c j p) n -> c p j n", j=TPC, p=P)
        rows = lambda w: w.rearrange("(k p) n -> p k n", p=P)

        o = 320
        ln1g_b, ln1b_b, ln2g_b, ln2b_b, outb_b, f2b_b = (take(D) for _ in range(6))
        assert o <= 2048
        x_all = tiles(fp(2048, TILES * D))
        o = 10240
        kn = lambda a, k: a.rearrange("p (k n) -> p k n", k=k)
        in_w = kn(take(KD * 2 * D), KD)
        dt_w, b_w, c_w, out_w = (kn(take(KD * D), KD) for _ in range(4))
        f1_w = kn(take(KD * 2 * D), KD)
        f2_w = kn(take(2 * KD * D), 2 * KD)
        rt_w = take(D)
        rt_wT = kn(take(KD * E), KD)
        rt_b = take(E)
        in_b = take(4)
        taps = kn(take(KD * 3), KD)
        tap_b, dt_b, b_b, c_b, a_neg, skip = (take(KD) for _ in range(6))
        f1_b = take(4)
        lg_all = take(TILES * E).rearrange("p (t e) -> p t e", e=E)
        assert o <= ZEROS
        xr = [tiles(take(ST * D)) for _ in range(2)]
        norm_a = take(ST * D)
        T_a = take(KD * S)
        gate, mixed, z, ct, dt = (kn(take(KD * S), KD) for _ in range(5))
        xpad = kn(take(KD * (S + 2)), KD)
        x2 = tiles(take(ST * D))
        l, v, state, decay = kn(norm_a, KD), kn(T_a, KD), dt, z
        norm_a, T_a = tiles(norm_a), kn(T_a, KD)
        norm_b, x3 = (tiles(take(ST * D)) for _ in range(2))
        T_b = kn(take(KD * S), KD)
        gl = kn(take(2 * KD * S), 2 * KD)
        stats5 = take(ST * 6).rearrange("p (j s) -> p j s", s=6)
        mom5 = take(ST * 2).rearrange("p (j s) -> p j s", s=2)
        var5, rstd5 = take(ST), take(ST)
        stats_b = take(ST * 6).rearrange("p (j s) -> p j s", s=6)
        mom_b = take(ST * 2).rearrange("p (j s) -> p j s", s=2)
        var_b, rstd_b = take(ST), take(ST)
        zeros = fp(ZEROS, TPC * D)
        ones4 = take(P)
        assert o <= 51200, o
        x_mid_b = x_mid.rearrange("(b j p) n -> b p j n", j=ST, p=P)
        xe = nc.dram_tensor("x_by_expert", [E * CAP, D], F32, kind="Internal").ap()
        ye = nc.dram_tensor("y_by_expert", [E * CAP + 1, D], F32, kind="Internal").ap()

        o = 26624
        lg6 = take(TILES * E).rearrange("p (t e) -> p t e", e=E)
        rev, eq, mask1, mask2, both, rest6, tot, pos = (take(TILES * E).rearrange("p (t e) -> p t e", e=E) for _ in range(8))
        top1, top2, s1, s2, p1, p2, slot, fits = (take(TILES) for _ in range(8))
        idx = [take(TILES).bitcast(U32) for _ in range(2)]
        below, ones6 = take(P), take(P)
        xe_s = [tiles(take(TPC * D)) for _ in range(2)]
        we = [kn(take(KD * CAP), KD) for _ in range(2)]
        ve = [kn(take(KD * CAP), KD) for _ in range(2)]
        woe = [kn(take(4 * D), 4) for _ in range(2)]
        XT = kn(take(KD * CAP), KD)
        sg6 = [take(CAP) for _ in range(2)]
        h6 = kn(take(4 * CAP), 4)
        ye_s = [tiles(take(TPC * D)) for _ in range(2)]
        y_g = [tiles(fp(10240 + s * TILES * D, TILES * D)) for s in range(2)]
        acc = [tiles(take(TPC * D)) for _ in range(2)]
        fin = [tiles(take(TPC * D)) for _ in range(2)]
        stats6 = take(TPC * 6).rearrange("p (j s) -> p j s", s=6)
        mom6 = take(TPC * 2).rearrange("p (j s) -> p j s", s=2)
        var6, rstd6 = take(TPC), take(TPC)
        assert o <= 51200, o
        got6 = [sem(f"got6_{c}") for c in range(TILES // TPC)]
        out_c = out.rearrange("b (c j p) n -> (b c) p j n", j=TPC, p=P)

        qe_one = sem("qe_one")
        c3_in = [sem("c3_in0"), sem("c3_in1")]
        x_out = [sem("x_out0"), sem("x_out1")]
        w3_in = sem("w3_in")
        prep_pe = sem("prep_pe")
        prep_act = sem("prep_act")
        prep_dve = sem("prep_dve")
        prep_c = sem("prep_c")
        pre_pe = sem("pre_pe")
        ffn_pe = sem("ffn_pe")
        act_pre = sem("act_pre")
        act_silu = sem("act_silu")
        dve_pre = sem("dve_pre")
        h_made = sem("h_made")
        dve_out = sem("dve_out")
        pool_pre = sem("pool_pre")
        pool_ffn = sem("pool_ffn")
        x5_in = [sem("x5_in0"), sem("x5_in1")]
        w5_in = sem("w5_in")
        zero_in = sem("zero_in")
        x3_out = sem("x3_out")
        pe_a = sem("pe_a")
        pe_b = sem("pe_b")
        act_a = sem("act_a")
        act_b = sem("act_b")
        dve_a = sem("dve_a")
        dve_f = sem("dve_f")
        dve_b = sem("dve_b")
        pool_a = sem("pool_a")
        pool_f = sem("pool_f")
        pool_b = sem("pool_b")
        prep5_pe = sem("prep5_pe")
        prep5_act = sem("prep5_act")
        prep5 = sem("prep5")
        const5 = sem("const5")
        e_in = [sem("e_in0"), sem("e_in1")]
        y_out = [sem("y_out0"), sem("y_out1")]
        const6 = sem("const6")
        rank_made = sem("rank_made")
        count_pe = sem("count_pe")
        top6 = sem("top6")
        exp6 = sem("exp6")
        idx6 = sem("idx6")
        sent6 = sem("sent6")
        pe6 = sem("pe6")
        act6 = sem("act6")
        dve6 = sem("dve6")
        lg_in = sem("lg_in")
        fin6 = sem("fin6")
        pow6 = sem("pow6")
        fin_out = [sem("fin_out0"), sem("fin_out1")]
        s_const = sem("s_const")
        s_w = sem("s_w")
        s_fscale = sem("s_fscale")
        passed = sem("passed")
        s_x = [sem("s_x0"), sem("s_x1")]
        s_xT = sem("s_xT")
        s_xTs = sem("s_xTs")
        s_proj = sem("s_proj")
        s_feat = sem("s_feat")
        s_feat_f = sem("s_feat_f")
        s_v = sem("s_v")
        s_qq = sem("s_qq")
        s_qkb = sem("s_qkb")
        s_sq = sem("s_sq")
        s_ss = sem("s_ss")
        s_rn = sem("s_rn")
        s_qn = sem("s_qn")
        s_fT = sem("s_fT")
        s_hi = sem("s_hi")
        s_hi_f = sem("s_hi_f")
        s_rest = sem("s_rest")
        s_rest_f = sem("s_rest_f")
        s_mid = sem("s_mid")
        s_mid_f = sem("s_mid_f")
        s_lo = sem("s_lo")
        s_lo_f = sem("s_lo_f")
        s_st = [sem("s_st0"), sem("s_st1")]
        stage = sem("stage")

        rows_cleared = sem("rows_cleared")
        score_made = sem("score_made")
        score_used = sem("score_used")
        sin_made = sem("sin_made")
        exp_made = sem("exp_made")
        tr_made = sem("tr_made")
        ev_a = sem("ev_a")
        ev_d = sem("ev_d")
        pv_made = sem("pv_made")
        att_made = sem("att_made")
        fold_made = sem("fold_made")
        o_kept = sem("o_kept")
        folded = sem("folded")
        v_in = sem("v_in")
        att_out = sem("att_out")
        vs_out = [sem("vs_out0"), sem("vs_out1")]
        rinv_made = sem("rinv_made")
        f_in = [sem("f_in0"), sem("f_in1")]
        c_in = [sem("c_in0"), sem("c_in1")]

        block = ctx.enter_context(nc.Block())

        def meet(eng, k):
            eng.drain().then_inc(stage, 1)
            eng.wait_ge(stage, 5 * k)

        x_tok = t["L0_attn_x"].rearrange("b (c j p) n -> (b c) p j n", j=TPC, p=P)
        wview = lambda w: w.rearrange("h (k p) d -> p k h d", p=P)
        FQR = 9 * NQ


        def load_f(sp, g, hh):
            gh = 2 * g + hh
            for rep in range(3):
                sp.dma_start(fq[hh][rep * 24:rep * 24 + 24, :],
                             fq_planes[:, bass.ds(gh, 1), :, :].rearrange("l o d n -> l (o d) n")).then_inc(f_in[hh], 16)
                sp.dma_start(fk[hh][rep * 24:rep * 24 + 24, :],
                             fk_planes[rep, bass.ds(gh, 1), :, :].rearrange("o d n -> (o d) n").partition_broadcast(3)).then_inc(f_in[hh], 16)

        def load_c(sp, g, hh):
            gh = 2 * g + hh
            q = lambda a, z: q_planes[a:z, bass.ds(gh, 1), :, :].rearrange("l o d n -> l (o d) n")
            k = lambda l, n: k_planes[l, bass.ds(gh, 1), :, :].rearrange("o d n -> (o d) n").partition_broadcast(n)
            for dst, src in ((qs[hh][0:96, 0, :], q(0, 3)), (qs[hh][96:128, 0, :], q(0, 1)),
                             (qs[hh][0:64, 1, :], q(1, 3)), (qs[hh][64:128, 1, :], q(0, 2)),
                             (ks[hh][0:96, 0, :], k(0, 3)), (ks[hh][96:128, 0, :], k(1, 1)),
                             (ks[hh][0:64, 1, :], k(1, 2)), (ks[hh][64:128, 1, :], k(2, 2))):
                sp.dma_start(dst, src).then_inc(c_in[hh], 16)

        F_IN, C_IN = 6 * 16, 8 * 16

        @block.sync
        def _(sp):
            for k in range(KD):
                for dst, src in ((wq, "L0_attn_Wq"), (wk, "L0_attn_Wk"), (wv, "L0_attn_Wv")):
                    sp.dma_start(dst[:, k, :].rearrange("p (h d) -> p h d", h=H),
                                 t[src][:, k * P:(k + 1) * P, :].rearrange("h p d -> p h d")).then_inc(s_w, 16)
            for i, n in enumerate(("L0_attn_bq", "L0_attn_bk")):
                for k in range(KD):
                    sp.dma_start(bqk[:, 2 * i + k:2 * i + k + 1],
                                 t[n].rearrange("(k h) d -> k (h d)", k=KD)[k].rearrange("(p o) -> p o", o=1)).then_inc(s_w, 16)
            sp.dma_start(bvb, t["L0_attn_bv"].rearrange("h d -> (h d)").partition_broadcast(P)).then_inc(s_w, 16)
            for i in range(2):
                sp.dma_start(bcb[:, i * 64:(i + 1) * 64], t["L0_attn_bc2q"].rearrange("h d -> (h d)").partition_broadcast(P)).then_inc(s_w, 16)
            sp.wait_ge(s_const, 4)
            for h in range(H):
                sp.dma_start(wc[(h % 4) * 32:(h % 4 + 1) * 32, h // 4, h * NQ:(h + 1) * NQ], t["L0_attn_Wc2q"][h]).then_inc(s_w, 16)
            for r in range(2):
                sp.dma_start(xin[r], x_tok[r]).then_inc(s_x[r], 16)

            def store_v(i, r):
                sp.wait_ge(s_v, now(1, 2 * i + r, 1))
                for hp in range(H // 2):
                    sp.dma_start(v_pairs[bass.ds(4 * i + hp, 1), r * CH:(r + 1) * CH, :].rearrange("o (j p) d -> p (o j) d", p=P),
                                 v_out[r][:, :, hp * 64:(hp + 1) * 64]).then_inc(vs_out[r], 16)

            def store_qk(i, r):
                sp.wait_ge(s_lo, now(4, 2 * i + r, 4))
                for f, dst in enumerate((q_planes, q_planes, k_planes, k_planes)):
                    d = dst[:, bass.ds(i * H + 4 * (f % 2), 4), :, r * CH:(r + 1) * CH].rearrange("l h d n -> (h d) l n")
                    sp.dma_start(d, planes[r][:, f]).then_inc(s_st[r], 16)

            def store_features(i, r):
                sp.wait_ge(s_lo_f, now(1, 2 * i + r, 1))
                for f, dst in enumerate((fq_planes, fk_planes)):
                    d = dst[:, bass.ds(i * H, H), :, r * CH:(r + 1) * CH].rearrange("l h d n -> (h d) l n")
                    sp.dma_start(d, planes[r][64 * f:64 * f + 64, 4]).then_inc(s_st[r], 16)

            def step1_sp(i, r, ahead=True):
                if ahead:
                    store_v(i + r, 1 - r)
                store_features(i, r)
                if ahead:
                    store_qk(i + r, 1 - r)

            store_v(0, 0)
            store_qk(0, 0)
            with sp.Fori(0, B - 1) as b:
                for r in range(2):
                    sp.wait_ge(s_xT, now(1, 2 * b + r, 1))
                    sp.dma_start(xin[r], x_tok[bass.ds(2 * b + (2 + r), 1)].rearrange("o p j n -> p (o j) n")).then_inc(s_x[r], 16)
                    step1_sp(b, r)
            step1_sp(B - 1, 0)
            step1_sp(B - 1, 1, ahead=False)
            for r in range(2):
                sp.wait_ge(s_st[r], 96 * (B + 1))
                sp.wait_ge(vs_out[r], 64 * (B + 1))
            meet(sp, 1)

            def load_v(g):
                sp.dma_start(v_pair, v_pairs[bass.ds(g, 1)].rearrange("o (t p) d -> p (o t) d", p=P)).then_inc(v_in, 16)

            def store_att(g):
                sp.wait_ge(att_made, 2 * g + 2)
                sp.dma_start(att_pairs[bass.ds(g, 1)].rearrange("o (t p) d -> p (o t) d", p=P), att_s).then_inc(att_out, 16)

            def pair_sp(g, first=False, last=False):
                for hh in range(2):
                    if not last:
                        sp.wait_ge(score_made, 32 * g + 8 * (hh + 1))
                        load_f(sp, g + 1, hh)
                if not first:
                    sp.wait_ge(pv_made, 4 * g)
                    load_v(g)
                    store_att(g - 1)
                for hh in range(2):
                    if not last:
                        sp.wait_ge(score_made, 32 * g + 16 + 8 * (hh + 1))
                        load_c(sp, g + 1, hh)

            sp.wait_ge(rows_cleared, 4)
            for hh in range(2):
                load_f(sp, 0, hh)
            for hh in range(2):
                load_c(sp, 0, hh)
            load_v(0)
            pair_sp(0, first=True)
            with sp.Fori(1, PAIRS - 1) as g:
                pair_sp(g)
            pair_sp(PAIRS - 1, last=True)
            store_att(PAIRS - 1)
            sp.wait_ge(att_out, 16 * PAIRS)
            meet(sp, 2)

            for dst, src in ((wo, rows(t["L0_attn_Wo"])), (w1, rows(t["L0_attn_W1"])), (w2, rows(t["L0_attn_W2"])),
                             (wm, rows(t["L0_attn_Wm"])), (wqo[0:NQ], t["L0_attn_Wqo"]),
                             (bm[0:1], t["L0_attn_bm"].unsqueeze(0)), (b2[0:1], t["L0_attn_b2"].unsqueeze(0)),
                             (bo_b, t["L0_attn_bo"].partition_broadcast(P)),
                             (g1_b, t["L0_attn_g1"].partition_broadcast(P)), (be1_b, t["L0_attn_beta1"].partition_broadcast(P)),
                             (g2_b, t["L0_attn_g2"].partition_broadcast(P)), (be2_b, t["L0_attn_beta2"].partition_broadcast(P)),
                             (tiles(ints[:, 0:HT * D]), rows(t["L0_ffn_w_gate"])), (tiles(ints[:, HT * D:2 * HT * D]), rows(t["L0_ffn_w_up"])),
                             (ints[:, 2 * HT * D:].rearrange("p (k n) -> p k n", k=KD), rows(t["L0_ffn_w_down"]))):
                sp.dma_start(dst, src).then_inc(w3_in, 16)
            for k in range(FK):
                sp.dma_start(b1c[:, k:k + 1], t["L0_attn_b1"][k * P:(k + 1) * P].unsqueeze(1)).then_inc(w3_in, 16)
                sp.dma_start(wqoT[:, k, NQ:NQ + 1], t["L0_attn_bqo"][k * P:(k + 1) * P].unsqueeze(1)).then_inc(w3_in, 16)

            def load3(i, r):
                for hp in range(H // 2):
                    sp.dma_start(attc[r][:, :, hp * 64:(hp + 1) * 64],
                                 att_pairs[bass.ds(4 * i + hp, 1), r * CH:(r + 1) * CH, :].rearrange("o (j p) d -> p (o j) d", p=P)).then_inc(c3_in[r], 16)
                sp.dma_start(xc[r], x_tok[bass.ds(2 * i + r, 1)].rearrange("o p j n -> p (o j) n")).then_inc(c3_in[r], 16)

            def store3(n, r):
                sp.wait_ge(dve_out, now(5, n, 5))
                sp.dma_start(x_mid_c[bass.ds(n, 1)].rearrange("o p j n -> p (o j) n"), xo[r]).then_inc(x_out[r], 16)

            for r in range(2):
                load3(0, r)
            col = lambda w, k: w.rearrange("(k p) -> k p", p=P)[k].unsqueeze(1)
            for dst, src in ((in_w, rows(t["L1_attn_in_W"])), (dt_w, rows(t["L1_attn_dt_W"])), (b_w, rows(t["L1_attn_b_W"])),
                             (c_w, rows(t["L1_attn_c_W"])), (out_w, rows(t["L1_attn_out_W"])), (f1_w, rows(t["L1_attn_f1_W"])),
                             (f2_w, rows(t["L1_attn_f2_W"])), (rt_w[0:E], t["L1_ffn_router_w"]),
                             (rt_b[0:1], t["L1_ffn_router_b"].unsqueeze(0)),
                             (ln1g_b, t["L1_attn_ln1_g"].partition_broadcast(P)), (ln1b_b, t["L1_attn_ln1_b"].partition_broadcast(P)),
                             (ln2g_b, t["L1_attn_ln2_g"].partition_broadcast(P)), (ln2b_b, t["L1_attn_ln2_b"].partition_broadcast(P)),
                             (outb_b, t["L1_attn_out_b"].partition_broadcast(P)), (f2b_b, t["L1_attn_f2_b"].partition_broadcast(P))):
                sp.dma_start(dst, src).then_inc(w5_in, 16)
            for k in range(4):
                sp.dma_start(in_b[:, k:k + 1], col(t["L1_attn_in_b"], k)).then_inc(w5_in, 16)
                sp.dma_start(f1_b[:, k:k + 1], col(t["L1_attn_f1_b"], k)).then_inc(w5_in, 16)
            for k in range(KD):
                sp.dma_start(taps[:, k, :], t["L1_attn_dw_W"][k * P:(k + 1) * P].rearrange("p o q -> p (o q)")).then_inc(w5_in, 16)
                for dst, src in ((tap_b, "dw_b"), (dt_b, "dt_b"), (b_b, "b_b"), (c_b, "c_b"), (a_neg, "a_log"), (skip, "d_skip")):
                    sp.dma_start(dst[:, k:k + 1], col(t["L1_attn_" + src], k)).then_inc(w5_in, 16)
            sp.wait_ge(const5, 1)
            for q in range(E):
                sp.dma_start(xe[q * CAP:(q + 1) * CAP].rearrange("(p r) n -> p (r n)", p=P), zeros).then_inc(zero_in, 16)
            sp.dma_start(ye[E * CAP:E * CAP + 1], zeros[0:1, 0:D]).then_inc(zero_in, 16)

            with sp.Fori(0, B - 1) as i:
                for r in range(2):
                    sp.wait_ge(pre_pe, now(7, 2 * i + r, 1))
                    sp.wait_ge(pool_pre, now(8, 2 * i + r, 2))
                    load3(i + 1, r)
                for r in range(2):
                    store3(2 * i + r, r)
            for r in range(2):
                store3(2 * (B - 1) + r, r)
            for r in range(2):
                sp.wait_ge(x_out[r], 16 * (B + 1))
            sp.wait_ge(zero_in, 16 * (E + 1))
            meet(sp, 3)

            def load4(i, r):
                sp.dma_start(xr[r], x_mid_b[bass.ds(2 * i + r, 1)].rearrange("o p j n -> p (o j) n")).then_inc(x5_in[r], 16)

            def keep(i, r):
                sp.wait_ge(dve_b, now(10, 2 * i + r, 9))
                sp.dma_start(x_all[:, bass.ds(ST * (2 * i + r), ST), :], norm_b).then_inc(x3_out, 16)

            for r in range(2):
                load4(0, r)
            with sp.Fori(0, B // 2 - 1) as i:
                for r in range(2):
                    sp.wait_ge(pool_b, now(6, 2 * i + r, 5))
                    load4(i + 1, r)
                    keep(i, r)
            for r in range(2):
                keep(B // 2 - 1, r)
            sp.wait_ge(x3_out, 16 * (B + 1))
            meet(sp, 4)

            ew = lambda w, e, k: w[bass.ds(e, 1)].rearrange("o (k p) n -> p (o k) n", p=P)

            def load_w(e, r):
                sp.dma_start(we[r], ew(t["L1_ffn_W"], e, KD)).then_inc(e_in[r], 16)
                sp.dma_start(ve[r], ew(t["L1_ffn_V"], e, KD)).then_inc(e_in[r], 16)
                sp.dma_start(woe[r], ew(t["L1_ffn_W_out"], e, 4)).then_inc(e_in[r], 16)

            def load_x(e, r):
                sp.dma_start(xe_s[r], xe[bass.ds(CAP * e, CAP)].rearrange("(j p) n -> p j n", p=P)).then_inc(e_in[r], 16)

            def store_y(e, r):
                sp.wait_ge(act6, now(6, e, 6))
                sp.dma_start(ye[bass.ds(CAP * e, CAP)].rearrange("(j p) n -> p j n", p=P), ye_s[r]).then_inc(y_out[r], 16)

            for r in range(2):
                load_w(r, r)
            sp.wait_ge(sent6, 16 * 2 * TILES)
            for r in range(2):
                load_x(r, r)
            with sp.Fori(0, E // 2 - 1) as i:
                for r in range(2):
                    sp.wait_ge(pe6, now(6, 2 * i + r, 6))
                    load_w(2 * i + (r + 2), r)
                    load_x(2 * i + (r + 2), r)
                    store_y(2 * i + r, r)
            for r in range(2):
                store_y(E - 2 + r, r)
            for c in range(TILES // TPC):
                sp.wait_ge(fin6, 6 * (c + 1))
                sp.dma_start(out_c[c], fin[c % 2]).then_inc(fin_out[c % 2], 16)
            for r in range(2):
                sp.wait_ge(fin_out[r], 16 * (TILES // TPC // 2))
            meet(sp, 5)

        @block.gpsimd
        def _(pool):
            pool.memset(ident, 0.0).then_inc(s_const, 1)
            pool.memset(wc, 0.0).then_inc(s_const, 1)
            pool.memset(half, -0.5).then_inc(s_const, 1)
            pool.wait_ge(s_const, 3)
            pool.affine_select(out=ident, in_=ident, compare_op=ALU.not_equal, fill=1.0, base=0,
                               pattern=[[-1, P]], channel_multiplier=1).then_inc(s_const, 1)
            meet(pool, 1)
            for a in fq + fk:
                pool.memset(a, 0.0).then_inc(rows_cleared, 1)
            pool.memset(fold, 0.0).then_inc(fold_made, 1)
            for q in range(4):
                pool.wait_ge(fold_made, q + 1)
                pool.affine_select(out=fold, in_=fold, compare_op=ALU.not_equal, fill=1.0, base=-HD * q,
                                   pattern=[[-1, HD]], channel_multiplier=1).then_inc(fold_made, 1)
            meet(pool, 2)

            pool.memset(ones, 1.0).then_inc(prep_c, 1)
            pool.memset(last_row, 0.0).then_inc(prep_c, 1)
            pool.memset(zeros, 0.0).then_inc(const5, 1)
            pool.wait_ge(prep_c, 2)
            pool.memset(last_row[:, NQ:NQ + 1], 1.0).then_inc(prep_c, 1)
            pool.wait_ge(prep_pe, 5)
            pool.sem_inc(pool_pre, 8)
            pool.sem_inc(pool_ffn, 1)
            wide = lambda v: v.unsqueeze(1).to_broadcast([P, TPC, D])

            def power(done, out_, in_):
                pool.tensor_tensor(out_[:, 0:TPC], in_[:, 0:TPC], half[:, 0:TPC], ALU.pow).then_inc(done, 1)

            def pre_pool(i, r):
                n = 2 * i + r
                pool.wait_ge(c3_in[r], C3_IN * (i + 1))
                pool.wait_ge(dve_pre, before(21, n, 1))
                pool.tensor_tensor(xbo, xc[r], wide(bo_b), ALU.add).then_inc(pool_pre, 1)
                pool.wait_ge(dve_pre, before(21, n, 17))
                pool.tensor_tensor(xb2, xc[r], wide(be2_b), ALU.add).then_inc(pool_pre, 1)
                pool.wait_ge(dve_pre, now(21, n, 4))
                power(pool_pre, rstd, var)
                pool.wait_ge(dve_pre, now(21, n, 5))
                pool.tensor_tensor(m1, n1, wide(g1_b), ALU.mult).then_inc(pool_pre, 1)
                pool.wait_ge(pool_pre, now(8, n, 4))
                pool.wait_ge(pre_pe, before(7, n, 3))
                pool.tensor_tensor(x1, m1, wide(be1_b), ALU.add).then_inc(pool_pre, 1)
                pool.wait_ge(dve_pre, now(21, n, 15))
                power(pool_pre, rstd, var)
                pool.wait_ge(dve_pre, now(21, n, 16))
                pool.tensor_tensor(m2, n2, wide(g2_b), ALU.mult).then_inc(pool_pre, 1)
                pool.wait_ge(dve_pre, now(21, n, 20))
                power(pool_pre, rstd, var)

            def ffn_pool(i, r):
                n = 2 * i + r
                pool.wait_ge(dve_out, now(5, n, 4))
                power(pool_ffn, rstd_f, var_f)

            pre_pool(0, 0)
            with pool.Fori(0, B - 1) as i:
                for r in range(2):
                    pre_pool(i + r, 1 - r)
                    ffn_pool(i, r)
            pre_pool(B - 1, 1)
            for r in range(2):
                ffn_pool(B - 1, r)
            meet(pool, 3)

            pool.memset(xpad[:, :, 0:1], 0.0).then_inc(prep5, 1)
            pool.memset(ones4, 1.0).then_inc(prep5, 1)
            pool.memset(xpad[:, :, S + 1:S + 2], 0.0).then_inc(prep5, 1)
            pool.sem_inc(pool_a, 4)
            pool.sem_inc(pool_f, 3)
            pool.sem_inc(pool_b, 6)
            pool.sem_inc(x3_out, 16)
            wide8 = lambda a: a.unsqueeze(1).to_broadcast([P, ST, D])

            def power8(done, in_, out_):
                pool.tensor_tensor(out_, in_, half[:, 0:ST], ALU.pow).then_inc(done, 1)

            def first_pool(i, r):
                n = 2 * i + r
                pool.wait_ge(dve_f, now(4, n, 3))
                power8(pool_f, var5, rstd5)
                pool.wait_ge(dve_f, now(4, n, 4))
                pool.tensor_tensor(norm_a, norm_a, wide8(ln1g_b), ALU.mult).then_inc(pool_f, 1)
                pool.wait_ge(pool_f, now(3, n, 2))
                pool.tensor_tensor(norm_a, norm_a, wide8(ln1b_b), ALU.add).then_inc(pool_f, 1)

            def scan_pool_1(i, r):
                n = 2 * i + r
                pool.wait_ge(act_a, now(15, n, 9))
                pool.wait_ge(dve_a, now(15, n, 6))
                pool.tensor_tensor(v, v, mixed, ALU.mult).then_inc(pool_a, 1)
                pool.wait_ge(x5_in[r], 16 * (i + 1))
                pool.wait_ge(dve_b, before(10, n, 4))
                pool.wait_ge(pool_b, before(6, n, 4))
                pool.tensor_tensor(x2, xr[r], wide8(outb_b), ALU.add).then_inc(pool_a, 1)

            def scan_pool_2(i, r):
                n = 2 * i + r
                for k in range(KD):
                    pool.wait_ge(dve_a, now(15, n, 10 + k))
                    pool.wait_ge(act_a, now(15, n, 14 + k))
                    pool.tensor_tensor(ct[:, k], ct[:, k], state[:, k], ALU.mult).then_inc(pool_a, 1)

            def second_pool_1(i, r):
                n = 2 * i + r
                pool.wait_ge(dve_b, now(10, n, 3))
                power8(pool_b, var_b, rstd_b)
                pool.wait_ge(dve_b, now(10, n, 4))
                pool.tensor_tensor(norm_b, norm_b, wide8(ln2g_b), ALU.mult).then_inc(pool_b, 1)
                pool.wait_ge(pool_b, now(6, n, 2))
                pool.tensor_tensor(norm_b, norm_b, wide8(ln2b_b), ALU.add).then_inc(pool_b, 1)
                pool.wait_ge(dve_b, before(10, n, 9))
                pool.tensor_tensor(x3, x2, wide8(f2b_b), ALU.add).then_inc(pool_b, 1)
                pool.wait_ge(pool_b, now(6, n, 4))
                pool.tensor_tensor(x3, x3, xr[r], ALU.add).then_inc(pool_b, 1)

            def second_pool_2(i, r):
                pool.wait_ge(dve_b, now(10, 2 * i + r, 8))
                power8(pool_b, var_b, rstd_b)

            def step4_pool(i, r, scan=True, first=True):
                second_pool_1(i, r)
                if scan:
                    scan_pool_1(i + r, 1 - r)
                if first:
                    first_pool(i + 1, r)
                if scan:
                    scan_pool_2(i + r, 1 - r)
                second_pool_2(i, r)

            pool.wait_ge(w5_in, W5_IN)
            first_pool(0, 0)
            scan_pool_1(0, 0)
            first_pool(0, 1)
            scan_pool_2(0, 0)
            with pool.Fori(0, B // 2 - 1) as i:
                for r in range(2):
                    step4_pool(i, r)
            step4_pool(B // 2 - 1, 0, first=False)
            step4_pool(B // 2 - 1, 1, scan=False, first=False)
            meet(pool, 4)

            pool.memset(ones6, 1.0).then_inc(const6, 1)
            pool.wait_ge(const6, 1)
            pool.affine_select(out=below, in_=ones6, compare_op=ALU.is_gt, fill=0.0, base=0,
                               pattern=[[1, P]], channel_multiplier=-1).then_inc(const6, 1)
            for s in range(2):
                pool.wait_ge(idx6, s + 1)
                for c in range(TILES):
                    pool.indirect_dma_start(out=xe, out_offset=bass.IndirectOffsetOnAxis(ap=idx[s][:, c:c + 1], axis=0),
                                            in_=x_all[:, c, :], in_offset=None,
                                            bounds_check=E * CAP - 1, oob_is_err=False).then_inc(sent6, 16)
            for r in range(2):
                pool.wait_ge(y_out[r], 16 * (E // 2))

            def fetch(c):
                for s in range(2):
                    for j in range(TPC):
                        q = TPC * c + j
                        pool.indirect_dma_start(out=y_g[s][:, q, :], out_offset=None, in_=ye,
                                                in_offset=bass.IndirectOffsetOnAxis(ap=idx[s][:, q:q + 1], axis=0)).then_inc(got6[c], 16)

            fetch(0)
            for c in range(TILES // TPC):
                if c + 1 < TILES // TPC:
                    fetch(c + 1)
                pool.wait_ge(fin6, 6 * c + 5)
                pool.tensor_tensor(rstd6, var6, half[:, 0:TPC], ALU.pow).then_inc(pow6, 1)
            meet(pool, 5)

        @block.scalar
        def _(act):
            act.wait_ge(s_w, 16 * W_DMAS)
            act.wait_ge(s_fscale, 2)

            for sems, per in (((s_feat, s_hi, s_mid), 4), ((s_feat_f, s_hi_f, s_mid_f), 1)):
                for one in sems:
                    act.sem_inc(one, per)
            act.sem_inc(s_xTs, 2)

            def xT_act(i, r):
                n = 2 * i + r
                act.wait_ge(s_xT, now(1, n, 1))
                act.wait_ge(s_proj, before(5, n, 5))
                act.activation(xT[:, 0, :], bank(6), ACT.Copy).then_inc(s_xTs, 1)

            def feat_act(i, r, f):
                n = 2 * i + r
                act.wait_ge(s_proj, now(5, n, 1 + f + 1))
                act.wait_ge(s_rest, before(4, n, f + 1))
                act.activation(feat[:, f, :], bank(2 + f), ACT.Identity, bias=bqk[:, f:f + 1]).then_inc(s_feat, 1)
                if f == 0:
                    act.wait_ge(s_st[r], 96 * (i + 1))
                act.wait_ge(s_feat, now(4, n, f + 1))
                act.activation(planes[r][:, f, 0, :], feat[:, f, :], ACT.Copy,
                               scale=SCORE_SCALE if f < 2 else 1.0).then_inc(s_hi, 1)

            def mid_act(i, r, f):
                n = 2 * i + r
                act.wait_ge(s_rest, now(4, n, f + 1))
                act.activation(planes[r][:, f, 1, :], rest[:, f, :], ACT.Copy).then_inc(s_mid, 1)

            def features_act(i, r):
                n = 2 * i + r
                act.wait_ge(s_fT, now(1, n, 1))
                act.wait_ge(s_rest_f, before(1, n, 1))
                act.activation(feat[:, 4, :], bank(1), ACT.Copy, scale=fscale).then_inc(s_feat_f, 1)
                act.wait_ge(s_feat_f, now(1, n, 1))
                act.activation(planes[r][:, 4, 0, :], feat[:, 4, :], ACT.Copy).then_inc(s_hi_f, 1)

            def mid_features_act(i, r):
                act.wait_ge(s_rest_f, now(1, 2 * i + r, 1))
                act.activation(planes[r][:, 4, 1, :], rest[:, 4, :], ACT.Copy).then_inc(s_mid_f, 1)

            def step1_act(i, r, ahead=True):
                nxt = (i + r, 1 - r)
                if ahead:
                    xT_act(*nxt)
                    for f in range(2):
                        feat_act(*nxt, f)
                features_act(i, r)
                if ahead:
                    feat_act(*nxt, 2)
                mid_features_act(i, r)
                if ahead:
                    feat_act(*nxt, 3)
                    for f in range(4):
                        mid_act(*nxt, f)

            xT_act(0, 0)
            for f in range(4):
                feat_act(0, 0, f)
            for f in range(4):
                mid_act(0, 0, f)
            with act.Fori(0, B - 1) as b:
                for r in range(2):
                    step1_act(b, r)
            step1_act(B - 1, 0)
            step1_act(B - 1, 1, ahead=False)
            meet(act, 1)

            def evac_act(g, k, first):
                act.wait_ge(tr_made, 32 * g + 2 * k + 1)
                if not (first and k < 8):
                    act.wait_ge(pv_made, 4 * g + k // 4 - 1)
                act.activation(pT[k // 4 % 2][:, 0:4, (k % 4) * P:(k % 4 + 1) * P],
                               bank(4).rearrange("p (t n) -> p t n", t=4), ACT.Copy).then_inc(ev_a, 1)

            def keep_sum(g, q, first):
                act.wait_ge(pv_made, 4 * g + q + 1)
                if not (first and q == 0):
                    act.wait_ge(folded, 4 * g + q)
                act.activation(o_sum, bank(6), ACT.Copy).then_inc(o_kept, 1)

            def sin_act(g, prev=True, scores=True):
                for u in range(UNITS + 1):
                    if scores and u < UNITS:
                        act.wait_ge(score_made, 32 * g + u + 1)
                        if u >= 2:
                            act.wait_ge(score_used, 32 * g + u + 1)
                        act.activation(sn[u % 2], bank(2 * (u % 2), 2), ACT.Sin, scale=SIN_SCALE).then_inc(sin_made, 1)
                    if prev and u - 1 in SIN_TURNS:
                        evac_act(g - 1, SIN_TURNS[u - 1], False)
                    if prev and u - 1 in SIN_QUADS and SIN_QUADS[u - 1][1] == 1:
                        keep_sum(g - 1, SIN_QUADS[u - 1][0], False)

            def exp_act(g, first=False):
                for u in range(UNITS):
                    act.wait_ge(score_used, 2 + 32 * g + 16 + u + 1)
                    act.activation(logits[:, u, :], logits[:, u, :], ACT.Exp, scale=-1.0, bias=nmax[:, u:u + 1],
                                   accum_out=rsum[:, u:u + 1]).then_inc(exp_made, 1)
                    if not first and u == OLD_QUAD[1]:
                        keep_sum(g - 1, 3, False)
                    if u + 1 in EXP_TURNS:
                        evac_act(g, EXP_TURNS[u + 1], first)
                    if u == OWN_QUAD[1]:
                        keep_sum(g, 0, first)

            sin_act(0, prev=False)
            exp_act(0, first=True)
            with act.Fori(1, PAIRS) as g:
                sin_act(g)
                exp_act(g)
            sin_act(PAIRS, scores=False)
            keep_sum(PAIRS - 1, 3, False)
            meet(act, 2)

            act.preload_act_table_set("silu_and_others")
            act.sem_inc(act_pre, 6)
            act.sem_inc(act_silu, 6)
            act.wait_ge(prep_pe, 1)
            act.activation(w1T.rearrange("p k n -> p (k n)"), bank(0, 4), ACT.Copy).then_inc(prep_act, 1)
            act.activation(wqoT[:, :, 0:NQ], bank(4)[:, 0:FK * NQ].rearrange("p (k q) -> p k q", q=NQ), ACT.Copy).then_inc(prep_act, 1)
            act.wait_ge(prep_pe, 2)
            act.activation(w1m.rearrange("p k n -> p (k n)"), bank(5)[:, 0:2 * NQ], ACT.Copy).then_inc(prep_act, 1)
            act.activation(qm_row[0:1], bank(5)[0:1, 2 * NQ:3 * NQ], ACT.Copy).then_inc(prep_act, 1)
            act.activation(w2q[0:NQ + 1], bank(6)[0:NQ + 1, 0:D], ACT.Copy).then_inc(prep_act, 1)
            for m, dst in enumerate((wgT, wuT, wdT)):
                act.wait_ge(prep_pe, 3 + m)
                act.activation(dst.rearrange("p k n -> p (k n)"), bank(4 * (m % 2), 3), ACT.Copy).then_inc(prep_act, 1)

            def pre_act_1(i, r):
                n = 2 * i + r
                act.wait_ge(pre_pe, now(7, n, 1))
                act.activation(aT.rearrange("p k n -> p (k n)"), bank(0, 2), ACT.Copy).then_inc(act_pre, 1)

            def pre_act_2(i, r):
                n = 2 * i + r
                act.wait_ge(pre_pe, now(7, n, 3))
                act.activation(x1T.rearrange("p k n -> p (k n)"), bank(0, 2), ACT.Copy).then_inc(act_pre, 1)

            def pre_act_3(i, r):
                n = 2 * i + r
                act.wait_ge(pre_pe, now(7, n, 4))
                act.wait_ge(dve_pre, now(21, n, 8))
                act.activation(th, bank(2)[:, 0:TPC * NQ], ACT.Tanh).then_inc(act_pre, 1)
                act.wait_ge(dve_pre, now(21, n, 10))
                act.activation(cs, turns, ACT.Sin).then_inc(act_pre, 1)

            def pre_act_4(i, r):
                n = 2 * i + r
                act.wait_ge(pre_pe, now(7, n, 5))
                act.activation(qeT[0:NQ + 1], bank(3)[0:NQ + 1, :], ACT.Copy).then_inc(act_pre, 1)
                act.wait_ge(pre_pe, now(7, n, 7))
                act.activation(xpT[r].rearrange("p k n -> p (k n)"), bank(2, 2), ACT.Copy).then_inc(act_pre, 1)

            def ffn_act(i, r, a, z):
                n = 2 * i + r
                for m in range(a, z):
                    act.wait_ge(ffn_pe, now(7, n, m + 1))
                    act.wait_ge(h_made, now(6, n, m - 1))
                    act.activation(sg[m % 2], bank(4 + 2 * (m % 2)), ACT.Silu, scale=1.0 / 127.0).then_inc(act_silu, 1)

            def step_act(i, r, ahead=True):
                nxt = (i + r, 1 - r)
                if ahead:
                    pre_act_1(*nxt)
                ffn_act(i, r, 0, 4)
                if ahead:
                    pre_act_2(*nxt)
                ffn_act(i, r, 4, 5)
                if ahead:
                    pre_act_3(*nxt)
                ffn_act(i, r, 5, HT)
                if ahead:
                    pre_act_4(*nxt)

            for part in (pre_act_1, pre_act_2, pre_act_3, pre_act_4):
                part(0, 0)
            with act.Fori(0, B - 1) as i:
                for r in range(2):
                    step_act(i, r)
            step_act(B - 1, 0)
            step_act(B - 1, 1, ahead=False)
            meet(act, 3)

            act.wait_ge(w5_in, W5_IN)
            act.activation(a_neg, a_neg, ACT.Exp).then_inc(prep5_act, 1)
            act.wait_ge(prep5_act, 1)
            act.activation(a_neg, a_neg, ACT.Copy, scale=-1.0).then_inc(prep5_act, 1)
            act.wait_ge(prep5_pe, 1)
            act.activation(rt_wT, bank(0)[:, 0:KD * E].rearrange("p (k e) -> p k e", e=E), ACT.Copy).then_inc(prep5_act, 1)
            act.wait_ge(prep5_act, 3)
            act.sem_inc(act_a, 15)
            act.sem_inc(act_b, 6)
            flat2 = lambda a: a.rearrange("p k n -> p (k n)")

            def first_act(i, r):
                n = 2 * i + r
                act.wait_ge(pe_a, now(12, n, 1))
                act.activation(flat2(T_a), bank(0, 4), ACT.Copy).then_inc(act_a, 1)
                act.wait_ge(prep5, 3)
                for k in range(KD):
                    act.wait_ge(pe_a, now(12, n, 2 + k))
                    act.activation(xpad[:, k, 1:S + 1], bank(2 * k, 2), ACT.Identity, bias=in_b[:, k:k + 1]).then_inc(act_a, 1)
                for k in range(KD):
                    act.wait_ge(pe_a, now(12, n, 4 + k))
                    act.activation(gate[:, k], bank(2 * k, 2), ACT.Sigmoid, bias=in_b[:, 2 + k:3 + k]).then_inc(act_a, 1)

            def scan_act_1(i, r):
                n = 2 * i + r
                for k in range(KD):
                    act.wait_ge(pe_a, now(12, n, 6 + k))
                    act.activation(z[:, k], bank(2 * k, 2), ACT.Identity, bias=dt_b[:, k:k + 1]).then_inc(act_a, 1)
                for k in range(KD):
                    act.wait_ge(pe_a, now(12, n, 8 + k))
                    act.activation(v[:, k], bank(2 * k, 2), ACT.Tanh, bias=b_b[:, k:k + 1]).then_inc(act_a, 1)

            def decay_act(i, r):
                n = 2 * i + r
                act.preload_act_table_set("natural_log_exp_and_others")
                act.wait_ge(dve_a, now(15, n, 7))
                act.activation(l, l, ACT.Exp).then_inc(act_a, 1)
                act.wait_ge(act_a, now(15, n, 12))
                act.activation(l, l, ACT.Ln, bias=1.0).then_inc(act_a, 1)
                act.wait_ge(dve_a, now(15, n, 8))
                for k in range(KD):
                    act.activation(decay[:, k], dt[:, k], ACT.Exp, scale=a_neg[:, k:k + 1]).then_inc(act_a, 1)

            def scan_act_2(i, r):
                n = 2 * i + r
                for k in range(KD):
                    act.wait_ge(pe_a, now(12, n, 10 + k))
                    act.activation(ct[:, k], bank(2 * k, 2), ACT.Tanh, bias=c_b[:, k:k + 1]).then_inc(act_a, 1)

            def turned_act(i, r, k, m):
                act.wait_ge(pe_b, now(8, 2 * i + r, k))
                act.activation(flat2(T_b), bank(4, 4), ACT.Copy).then_inc(act_b, 1)

            def gelu_act(i, r):
                n = 2 * i + r
                for m in range(4):
                    act.wait_ge(pe_b, now(8, n, 2 + m))
                    act.activation(gl[:, m], bank(4 + 2 * (m % 2), 2), ACT.Gelu, bias=f1_b[:, m:m + 1]).then_inc(act_b, 1)

            def step4_act(i, r, scan=True):
                nxt = (i + r, 1 - r)
                if scan:
                    first_act(*nxt)
                turned_act(i, r, 1, 1)
                if scan:
                    scan_act_1(*nxt)
                    scan_act_2(*nxt)
                    decay_act(*nxt)
                gelu_act(i, r)
                turned_act(i, r, 7, 6)

            first_act(0, 0)
            scan_act_1(0, 0)
            scan_act_2(0, 0)
            decay_act(0, 0)
            with act.Fori(0, B // 2 - 1) as i:
                for r in range(2):
                    step4_act(i, r)
            step4_act(B // 2 - 1, 0)
            step4_act(B // 2 - 1, 1, scan=False)
            meet(act, 4)

            act.sem_inc(act6, 6)
            act.wait_ge(top6, TOP_STEPS_E)
            act.activation(p2, top2, ACT.Exp).then_inc(exp6, 1)
            act.preload_act_table_set("silu_and_others")
            with act.Fori(0, E // 2) as i:
                for r in range(2):
                    e = 2 * i + r
                    act.wait_ge(pe6, now(6, e, 1))
                    act.wait_ge(pe6, before(6, e, 5))
                    act.activation(XT.rearrange("p k n -> p (k n)"), bank(0, 2), ACT.Copy).then_inc(act6, 1)
                    for m in range(4):
                        act.wait_ge(pe6, now(6, e, 2 + m))
                        act.wait_ge(dve6, now(4, e, m - 1))
                        act.activation(sg6[m % 2], bank(3 + 2 * (m % 2)), ACT.Silu).then_inc(act6, 1)
                    act.wait_ge(pe6, now(6, e, 6))
                    act.wait_ge(y_out[r], 16 * i)
                    act.activation(ye_s[r].rearrange("p j n -> p (j n)"), bank(6, 2), ACT.Copy).then_inc(act6, 1)
            meet(act, 5)

        @block.vector
        def _(dve):
            dve.memset(fscale[0:64], -FID_SCALE).then_inc(s_fscale, 1)
            dve.memset(fscale[64:128], 1.0).then_inc(s_fscale, 1)
            for one, per in ((s_v, 1), (s_rest, 4), (s_rest_f, 1), (s_lo, 4), (s_lo_f, 1), (s_qkb, 1), (s_sq, 4), (s_qn, 1),
                             (s_ss, 1), (s_rn, 13), (vs_out[0], 64), (vs_out[1], 64), (s_st[0], 96), (s_st[1], 96)):
                dve.sem_inc(one, per)
            dve.wait_ge(s_w, 16 * W_DMAS)

            def step(done, v):
                def then(ins):
                    v[0] += 1
                    ins.then_inc(done, 1)
                    dve.wait_ge(done, v[0])
                then.count = v
                return then

            def split(n, r, f, hi, mid, done, per, k):
                dve.wait_ge(hi, now(per, n, k))
                dve.wait_ge(mid, before(per, n, k))
                dve.scalar_tensor_tensor(out=rest[:, f, :], in0=feat[:, f, :], scalar=SCORE_SCALE if f < 2 else 1.0,
                                         in1=planes[r][:, f, 0, :], op0=ALU.mult, op1=ALU.subtract).then_inc(done, 1)

            def low(n, r, f, mid, done, per, k):
                dve.wait_ge(mid, now(per, n, k))
                dve.tensor_tensor(planes[r][:, f, 2, :], rest[:, f, :], planes[r][:, f, 1, :],
                                  ALU.subtract).then_inc(done, 1)

            def xT_dve(i, r):
                n = 2 * i + r
                dve.wait_ge(s_xT, now(1, n, 1))
                dve.wait_ge(s_proj, before(5, n, 5))
                dve.tensor_copy(xT[:, 1, :], bank(7)).then_inc(s_xTs, 1)

            def v_dve(i, r):
                dve.wait_ge(s_proj, now(5, 2 * i + r, 1))
                dve.wait_ge(vs_out[r], 64 * (i + 1))
                dve.tensor_tensor(v_out[r], bank(6, 2).rearrange("p (j n) -> p j n", j=TPC),
                                  bvb.unsqueeze(1).to_broadcast([P, TPC, D]), ALU.add).then_inc(s_v, 1)

            def norms_dve(i, r):
                n = 2 * i + r
                dve.wait_ge(s_qq, now(1, n, 1))
                dve.wait_ge(s_fT, before(1, n, 1))
                dve.tensor_tensor(qk, bank(0).rearrange("p (j n) -> p j n", j=TPC),
                                  bcb.unsqueeze(1).to_broadcast([P, TPC, P]), ALU.add).then_inc(s_qkb, 1)
                dve.wait_ge(s_qkb, now(1, n, 1))
                dve.tensor_tensor(qk2, qk, qk, ALU.mult).then_inc(s_sq, 1)
                dve.wait_ge(s_sq, now(4, n, 1))
                dve.tensor_reduce(ss, qk2.rearrange("p j (g q) -> p (j g) q", q=NQ), AX.X, ALU.add).then_inc(s_sq, 1)
                dve.wait_ge(s_sq, now(4, n, 2))
                dve.tensor_scalar(ss, ss, TINY, None, ALU.max).then_inc(s_sq, 1)
                dve.wait_ge(s_sq, now(4, n, 3))
                for at, dst in enumerate((q_norms, k_norms)):
                    last = dve.tensor_copy(dst[:, bass.ds(H * i, H), r * TPC:(r + 1) * TPC].rearrange("p h j -> p j h"),
                                           ss.rearrange("p (j g) -> p j g", j=TPC)[:, :, at * H:(at + 1) * H])
                last.then_inc(s_ss, 1)
                then = step(s_rn, [now(13, n, 0)])
                then(dve.tensor_scalar(rn.bitcast(I32), ss.bitcast(I32), -0.5, RSQRT_START, ALU.mult, ALU.add))
                for _ in range(4):
                    then(dve.tensor_tensor(rn2, rn, rn, ALU.mult))
                    then(dve.scalar_tensor_tensor(out=rn2, in0=rn2, scalar=-0.5, in1=ss, op0=ALU.mult, op1=ALU.mult))
                    then(dve.scalar_tensor_tensor(out=rn, in0=rn2, scalar=1.5, in1=rn, op0=ALU.add, op1=ALU.mult))

            def unit_dve(i, r):
                n = 2 * i + r
                dve.tensor_tensor(qk.rearrange("p j (g q) -> p (j g) q", q=NQ),
                                  qk.rearrange("p j (g q) -> p (j g) q", q=NQ),
                                  rn.unsqueeze(2).to_broadcast([P, TPC * 2 * H, NQ]), ALU.mult).then_inc(s_qn, 1)
                dve.sem_inc(s_sq, 1)

            def step1_dve(i, r, ahead=True):
                nxt = (i + r, 1 - r)
                m = 2 * nxt[0] + nxt[1]
                n = 2 * i + r
                if ahead:
                    xT_dve(*nxt)
                norms_dve(i, r)
                if ahead:
                    v_dve(*nxt)
                unit_dve(i, r)
                if ahead:
                    for f in range(2):
                        split(m, 1 - r, f, s_hi, s_mid, s_rest, 4, f + 1)
                split(n, r, 4, s_hi_f, s_mid_f, s_rest_f, 1, 1)
                if ahead:
                    split(m, 1 - r, 2, s_hi, s_mid, s_rest, 4, 3)
                low(n, r, 4, s_mid_f, s_lo_f, 1, 1)
                if ahead:
                    split(m, 1 - r, 3, s_hi, s_mid, s_rest, 4, 4)
                    for f in range(4):
                        low(m, 1 - r, f, s_mid, s_lo, 4, f + 1)

            xT_dve(0, 0)
            v_dve(0, 0)
            for f in range(4):
                split(0, 0, f, s_hi, s_mid, s_rest, 4, f + 1)
            for f in range(4):
                low(0, 0, f, s_mid, s_lo, 4, f + 1)
            with dve.Fori(0, B - 1) as b:
                for r in range(2):
                    step1_dve(b, r)
            step1_dve(B - 1, 0)
            step1_dve(B - 1, 1, ahead=False)
            meet(dve, 1)

            dve.sem_inc(score_used, 2)

            def evac_dve(g, k, first):
                dve.wait_ge(tr_made, 32 * g + 2 * k + 2)
                if not (first and k < 8):
                    dve.wait_ge(pv_made, 4 * g + k // 4 - 1)
                dve.tensor_copy(pT[k // 4 % 2][:, 4:8, (k % 4) * P:(k % 4 + 1) * P],
                                bank(5).rearrange("p (t n) -> p t n", t=4)).then_inc(ev_d, 1)

            def normalize(g, hh, first):
                dve.wait_ge(folded, 4 * g + 2 * hh + 2)
                dve.wait_ge(rinv_made, g + 1)
                if not first:
                    dve.wait_ge(att_out, 16 * g)
                dve.tensor_tensor(att_s[:, :, hh * HD:(hh + 1) * HD],
                                  bank(7)[:, hh * 256:hh * 256 + 256].rearrange("p (s d) -> p s d", d=HD),
                                  rinv[:, 8 * hh:8 * hh + 8].unsqueeze(2).to_broadcast([P, ST, HD]),
                                  ALU.mult).then_inc(att_made, 1)

            def sin_dve(g, prev=True, scores=True):
                for u in range(UNITS):
                    if scores:
                        dve.wait_ge(sin_made, 16 * g + u + 1)
                        if prev:
                            dve.wait_ge(tr_made, 32 * g - 32 + 2 * u + 2)
                        dve.scalar_tensor_tensor(out=logits[:, u, :], in0=sn[u % 2], scalar=10.0,
                                                 in1=bank(2 * (u % 2), 2), op0=ALU.add, op1=ALU.mult).then_inc(score_used, 1)
                    if prev and u == 1:
                        dve.wait_ge(exp_made, 16 * g)
                        dve.reciprocal(rinv, rsum).then_inc(rinv_made, 1)
                    if prev and u in SIN_TURNS:
                        evac_dve(g - 1, SIN_TURNS[u], False)
                    if prev and u == 8:
                        normalize(g - 1, 0, False)

            def exp_dve(g, first=False):
                for u in range(UNITS):
                    dve.wait_ge(score_made, 32 * g + 16 + u + 1)
                    dve.wait_ge(score_used, 2 + 32 * g + u + 1)
                    dve.sem_inc(passed, 1)
                    dve.tensor_tensor_reduce(out=logits[:, u, :], in0=logits[:, u, :], in1=bank(2 * (u % 2), 2),
                                             scale=1.0, scalar=3.0e38, op0=ALU.add, op1=ALU.min,
                                             accum_out=nmax[:, u:u + 1]).then_inc(score_used, 1)
                    if u in EXP_TURNS:
                        evac_dve(g, EXP_TURNS[u], first)
                    if not first and u == OLD_FOLD + 2:
                        normalize(g - 1, 1, False)

            sin_dve(0, prev=False)
            exp_dve(0, first=True)
            with dve.Fori(1, PAIRS) as g:
                sin_dve(g)
                exp_dve(g)
            sin_dve(PAIRS, scores=False)
            normalize(PAIRS - 1, 1, False)
            meet(dve, 2)

            dve.sem_inc(dve_pre, 21)
            dve.sem_inc(h_made, 6)
            dve.sem_inc(dve_out, 5)
            for r in range(2):
                dve.sem_inc(x_out[r], 16)
            dve.memset(qe[:, :, NQ:NQ + 1], 1.0).then_inc(qe_one, 1)
            dve.wait_ge(w3_in, W3_IN)
            dve.tensor_copy(floats, ints).then_inc(prep_dve, 1)

            def normal(then, src, dst, got, v, st, mo, va, rs, tiles_, before_last=None):
                for j in range(tiles_):
                    last = dve.bn_stats(st[:, j, :], src[:, j, :])
                then(last)
                dve.sem_inc(passed, 1)
                for j in range(tiles_):
                    last = dve.bn_aggr(mo[:, j, :], st[:, j, :])
                then(last)
                then(dve.tensor_scalar(va[:, 0:tiles_], mo[:, 0:tiles_, 1], LN_EPS, None, ALU.add))
                dve.wait_ge(got, v)
                if before_last:
                    before_last()
                for j in range(tiles_):
                    last = dve.tensor_scalar(dst[:, j, :], src[:, j, :], mo[:, j, 0:1], rs[:, j:j + 1], ALU.subtract, ALU.mult)
                then(last)

            flat = lambda a: a.rearrange("p j n -> p (j n)")

            def pre_dve_1(i, r):
                n = 2 * i + r
                then = step(dve_pre, [now(21, n, 0)])
                dve.wait_ge(pre_pe, now(7, n, 2))
                dve.wait_ge(pool_pre, now(8, n, 1))
                then(dve.tensor_tensor(flat(r1), bank(2, 2), flat(xbo), ALU.add))
                normal(then, r1, n1, pool_pre, now(8, n, 3), stats, moments, var, rstd, TPC)

            def pre_dve_2(i, r):
                n = 2 * i + r
                then = step(dve_pre, [now(21, n, 5)])
                dve.wait_ge(pre_pe, now(7, n, 4))
                qm = bank(2)[:, 0:TPC * NQ]
                then(dve.tensor_scalar(turns, qm, 0.125, ROUND, ALU.mult, ALU.add))
                then(dve.tensor_scalar(turns, turns, ROUND, -8.0, ALU.subtract, ALU.mult))
                then(dve.tensor_tensor(turns, qm, turns, ALU.add))
                then(dve.scalar_tensor_tensor(out=turns, in0=turns, scalar=-1.0, in1=turns, op0=ALU.mult, op1=ALU.max))
                then(dve.tensor_scalar(turns, turns, -PI / 4, PI / 2, ALU.mult, ALU.add))
                dve.wait_ge(act_pre, now(6, n, 4))
                then(dve.tensor_tensor(qe[:, :, 0:NQ], th.rearrange("p (j q) -> p j q", q=NQ),
                                       cs.rearrange("p (j q) -> p j q", q=NQ), ALU.mult))

            def pre_dve_3(i, r):
                n = 2 * i + r
                then = step(dve_pre, [now(21, n, 11)])
                dve.wait_ge(pre_pe, now(7, n, 6))
                then(dve.tensor_tensor(flat(r2), bank(0, 2), flat(x1), ALU.add))
                normal(then, r2, n2, pool_pre, now(8, n, 6), stats, moments, var, rstd, TPC)
                dve.wait_ge(pool_pre, now(8, n, 7))
                then(dve.tensor_tensor(flat(r3), flat(m2), flat(xb2), ALU.add))
                normal(then, r3, xp[r], pool_pre, now(8, n, 8), stats, moments, var, rstd, TPC)

            def ffn_dve(i, r, a, z):
                n = 2 * i + r
                for m in range(a, z):
                    dve.wait_ge(act_silu, now(6, n, m + 1))
                    if m == 0:
                        dve.wait_ge(ffn_pe, before(7, n, 7))
                    dve.scalar_tensor_tensor(out=hT[:, m, :], in0=bank(5 + 2 * (m % 2)), scalar=1.0 / 127.0, in1=sg[m % 2],
                                             op0=ALU.mult, op1=ALU.mult).then_inc(h_made, 1)

            def out_dve(i, r):
                n = 2 * i + r
                then = step(dve_out, [now(5, n, 0)])
                dve.wait_ge(ffn_pe, now(7, n, 7))
                then(dve.scalar_tensor_tensor(out=flat(r4), in0=bank(4, 2), scalar=1.0 / 127.0, in1=flat(xp[r]),
                                              op0=ALU.mult, op1=ALU.add))
                normal(then, r4, xo[r], pool_ffn, now(1, n, 1), stats_f, moments_f, var_f, rstd_f, TPC,
                       lambda: dve.wait_ge(x_out[r], 16 * (i + 1)))

            def step_dve(i, r, ahead=True):
                nxt = (i + r, 1 - r)
                ffn_dve(i, r, 0, 1)
                if ahead:
                    pre_dve_1(*nxt)
                ffn_dve(i, r, 1, 5)
                if ahead:
                    pre_dve_2(*nxt)
                ffn_dve(i, r, 5, HT)
                if ahead:
                    pre_dve_3(*nxt)
                out_dve(i, r)

            for part in (pre_dve_1, pre_dve_2, pre_dve_3):
                part(0, 0)
            with dve.Fori(0, B - 1) as i:
                for r in range(2):
                    step_dve(i, r)
            step_dve(B - 1, 0)
            step_dve(B - 1, 1, ahead=False)
            meet(dve, 3)

            dve.sem_inc(dve_a, 15)
            dve.sem_inc(dve_f, 4)
            dve.sem_inc(dve_b, 10)
            dve.wait_ge(w5_in, W5_IN)

            def first_dve(i, r):
                n = 2 * i + r
                then = step(dve_f, [now(4, n, 0)])
                dve.wait_ge(x5_in[r], 16 * (i + 1))
                normal(then, xr[r], norm_a, pool_f, now(3, n, 1), stats5, mom5, var5, rstd5, ST)

            def conv_dve(i, r):
                n = 2 * i + r
                then = step(dve_a, [now(15, n, 0)])
                for k in range(KD):
                    dve.wait_ge(act_a, now(15, n, 2 + k))
                    then(dve.tensor_scalar(mixed[:, k], xpad[:, k, 0:S], taps[:, k, 0:1], tap_b[:, k:k + 1], ALU.mult, ALU.add))
                    for q in (1, 2):
                        then(dve.scalar_tensor_tensor(out=mixed[:, k], in0=xpad[:, k, q:S + q], scalar=taps[:, k, q:q + 1],
                                                      in1=mixed[:, k], op0=ALU.mult, op1=ALU.add))

            def scan_dve(i, r):
                n = 2 * i + r
                then = step(dve_a, [now(15, n, 6)])
                dve.wait_ge(act_a, now(15, n, 7))
                then(dve.scalar_tensor_tensor(out=l, in0=z, scalar=-1.0, in1=z, op0=ALU.mult, op1=ALU.min))
                dve.wait_ge(act_a, now(15, n, 13))
                then(dve.scalar_tensor_tensor(out=dt, in0=z, scalar=0.0, in1=l, op0=ALU.max, op1=ALU.add))
                dve.wait_ge(pool_a, now(4, n, 1))
                then(dve.tensor_tensor(v, v, dt, ALU.mult))
                for k in range(KD):
                    dve.wait_ge(act_a, now(15, n, 15))
                    then(dve.tensor_tensor_scan(state[:, k], decay[:, k], v[:, k], 0.0, ALU.mult, ALU.add))

            def gate_dve(i, r):
                n = 2 * i + r
                then = step(dve_a, [now(15, n, 11)])
                for k in range(KD):
                    dve.wait_ge(pool_a, now(4, n, 3 + k))
                    then(dve.scalar_tensor_tensor(out=ct[:, k], in0=mixed[:, k], scalar=skip[:, k:k + 1], in1=ct[:, k],
                                                  op0=ALU.mult, op1=ALU.add))
                then(dve.tensor_tensor(ct, ct, gate, ALU.mult))

            def mix_dve(i, r):
                n = 2 * i + r
                then = step(dve_a, [now(15, n, 14)])
                dve.wait_ge(pe_a, now(12, n, 12))
                dve.wait_ge(pool_a, now(4, n, 2))
                then(dve.tensor_tensor(flat(x2), bank(0, 4), flat(x2), ALU.add))

            def second_dve_1(i, r):
                n = 2 * i + r
                then = step(dve_b, [now(10, n, 0)])
                normal(then, x2, norm_b, pool_b, now(6, n, 1), stats_b, mom_b, var_b, rstd_b, ST,
                       lambda: (dve.wait_ge(pe_b, before(8, n, 7)), dve.wait_ge(x3_out, 16 * (n + 1))))

            def second_dve_2(i, r):
                n = 2 * i + r
                then = step(dve_b, [now(10, n, 4)])
                dve.wait_ge(pe_b, now(8, n, 6))
                dve.wait_ge(pool_b, now(6, n, 5))
                then(dve.tensor_tensor(flat(x3), bank(4, 4), flat(x3), ALU.add))
                normal(then, x3, norm_b, pool_b, now(6, n, 6), stats_b, mom_b, var_b, rstd_b, ST)

            def logits_dve(i, r):
                n = 2 * i + r
                dve.wait_ge(pe_b, now(8, n, 8))
                dve.tensor_copy(lg_all[:, bass.ds(ST * n, ST), :],
                                bank(4)[:, 0:ST * E].rearrange("p (j e) -> p j e", e=E)).then_inc(dve_b, 1)

            def step4_dve(i, r, scan=True, first=True):
                nxt = (i + r, 1 - r)
                second_dve_1(i, r)
                if scan:
                    conv_dve(*nxt)
                    scan_dve(*nxt)
                if first:
                    first_dve(i + 1, r)
                if scan:
                    gate_dve(*nxt)
                second_dve_2(i, r)
                if scan:
                    mix_dve(*nxt)
                logits_dve(i, r)

            first_dve(0, 0)
            conv_dve(0, 0)
            scan_dve(0, 0)
            first_dve(0, 1)
            gate_dve(0, 0)
            mix_dve(0, 0)
            with dve.Fori(0, B // 2 - 1) as i:
                for r in range(2):
                    step4_dve(i, r)
            step4_dve(B // 2 - 1, 0, first=False)
            step4_dve(B // 2 - 1, 1, scan=False, first=False)
            meet(dve, 4)

            top = step(top6, [0])
            over_e = lambda a: a.unsqueeze(2).to_broadcast([P, TILES, E])
            for e in range(E):
                last = dve.memset(rev[:, :, e], float(E - e))
            top(last)
            top(dve.tensor_copy(lg6, lg_all))
            for best, s, mask, src in ((top1, s1, mask1, lg6), (top2, s2, mask2, rest6)):
                top(dve.tensor_reduce(best, src, AX.X, ALU.max))
                top(dve.tensor_tensor(eq, src, over_e(best), ALU.is_equal))
                top(dve.tensor_tensor(eq, eq, rev, ALU.mult))
                top(dve.tensor_reduce(s, eq, AX.X, ALU.max))
                top(dve.tensor_tensor(mask, rev, over_e(s), ALU.is_equal))
                if src is lg6:
                    top(dve.scalar_tensor_tensor(out=rest6, in0=mask, scalar=-3.0e38, in1=src, op0=ALU.mult, op1=ALU.add))
            top(dve.tensor_tensor(both, mask1, mask2, ALU.add))
            top(dve.tensor_tensor(top2, top2, top1, ALU.subtract))
            assert top.count[0] == TOP_STEPS_E
            dve.wait_ge(count_pe, 1)
            top(dve.tensor_copy(tot, bank(1)[:, 0:TILES * E].rearrange("p (t e) -> p t e", e=E)))
            for e in range(E):
                last = dve.tensor_tensor_scan(pos[:, :, e], ones6[:, 0:TILES], tot[:, :, e], 0.0, ALU.mult, ALU.add)
            top(last)
            top(dve.tensor_tensor(pos, pos, tot, ALU.subtract))
            top(dve.tensor_tensor(pos, bank(0)[:, 0:TILES * E].rearrange("p (t e) -> p t e", e=E), pos, ALU.add))
            for k, (s, mask) in enumerate(((s1, mask1), (s2, mask2))):
                top(dve.tensor_tensor(eq, pos, mask, ALU.mult))
                top(dve.tensor_reduce(slot, eq, AX.X, ALU.add))
                top(dve.tensor_scalar(fits, slot, float(CAP), None, ALU.is_lt))
                top(dve.scalar_tensor_tensor(out=slot, in0=s, scalar=-float(CAP), in1=slot, op0=ALU.mult, op1=ALU.add))
                top(dve.tensor_tensor(slot, slot, fits, ALU.mult))
                dve.tensor_scalar(idx[k], slot, float(E * CAP), None, ALU.add).then_inc(idx6, 1)
            dve.wait_ge(exp6, 1)
            top(dve.tensor_scalar(p1, p2, 1.0, None, ALU.add))
            top(dve.reciprocal(p1, p1))
            top(dve.tensor_tensor(p2, p2, p1, ALU.mult))
            dve.sem_inc(dve6, 4)
            with dve.Fori(0, E // 2) as i:
                for r in range(2):
                    e = 2 * i + r
                    for m in range(4):
                        dve.wait_ge(act6, now(6, e, 2 + m))
                        if m == 0:
                            dve.wait_ge(pe6, before(6, e, 6))
                        dve.tensor_tensor(h6[:, m], bank(2 + 2 * (m % 2)), sg6[m % 2], ALU.mult).then_inc(dve6, 1)
            for c in range(TILES // TPC):
                r = c % 2
                then = step(fin6, [6 * c])
                dve.wait_ge(got6[c], 16 * 2 * TPC)
                for j in range(TPC):
                    q = TPC * c + j
                    last = dve.scalar_tensor_tensor(out=acc[r][:, j, :], in0=y_g[0][:, q, :], scalar=p1[:, q:q + 1],
                                                    in1=x_all[:, q, :], op0=ALU.mult, op1=ALU.add)
                then(last)
                for j in range(TPC):
                    q = TPC * c + j
                    last = dve.scalar_tensor_tensor(out=acc[r][:, j, :], in0=y_g[1][:, q, :], scalar=p2[:, q:q + 1],
                                                    in1=acc[r][:, j, :], op0=ALU.mult, op1=ALU.add)
                then(last)
                normal(then, acc[r], fin[r], pow6, c + 1, stats6, mom6, var6, rstd6, TPC,
                       (lambda: dve.wait_ge(fin_out[r], 16 * (c // 2))) if c >= 2 else None)
            meet(dve, 5)

        @block.tensor
        def _(pe):
            pe.wait_ge(s_w, 16 * W_DMAS)
            pe.wait_ge(s_const, 4)

            for one, per in ((s_xT, 1), (s_proj, 5), (s_qq, 1), (s_fT, 1)):
                pe.sem_inc(one, per)

            def xT_pe(i, r):
                n = 2 * i + r
                pe.wait_ge(s_x[r], 16 * (i + 1))
                pe.wait_ge(s_v, before(1, n, 1))
                for k in range(KD):
                    for j in range(TPC):
                        last = pe.transpose(bank(6 + k)[:, j * P:(j + 1) * P], xin[r][:, j, k * P:(k + 1) * P], ident)
                last.then_inc(s_xT, 1)

            def values_pe(i, r):
                n = 2 * i + r
                pe.wait_ge(s_xTs, now(2, n, 2))
                for j in range(TPC):
                    for k in range(KD):
                        last = pe.matmul(bank(6, 2)[:, j * D:(j + 1) * D], xT[:, k, j * P:(j + 1) * P], wv[:, k, :],
                                         start=(k == 0), stop=(k == 1))
                last.then_inc(s_proj, 1)

            def project_pe(i, r, f):
                n = 2 * i + r
                pe.wait_ge(s_feat, before(4, n, f + 1))
                c = (f % 2) * P
                for k in range(KD):
                    last = pe.matmul(bank(2 + f), (wq if f < 2 else wk)[:, k, c:c + P], xT[:, k, :], start=(k == 0), stop=(k == 1))
                last.then_inc(s_proj, 1)

            def features_pe(i, r):
                n = 2 * i + r
                pe.wait_ge(s_feat, now(4, n, 4))
                pe.wait_ge(s_qkb, before(1, n, 1))
                for j in range(TPC):
                    for w in range(2):
                        for k in range(KD):
                            last = pe.matmul(bank(0)[:, j * P + w * 64:j * P + w * 64 + 64],
                                             feat[:, 2 * w + k, j * P:(j + 1) * P], wc[:, k, :],
                                             start=(k == 0), stop=(k == 1))
                last.then_inc(s_qq, 1)

            def turn_features_pe(i, r):
                n = 2 * i + r
                pe.wait_ge(s_qn, now(1, n, 1))
                pe.wait_ge(s_feat_f, before(1, n, 1))
                for j in range(TPC):
                    last = pe.transpose(bank(1)[:, j * P:(j + 1) * P], qk[:, j, :], ident)
                last.then_inc(s_fT, 1)

            def step1_pe(i, r, ahead=True):
                nxt = (i + r, 1 - r)
                if ahead:
                    xT_pe(*nxt)
                features_pe(i, r)
                if ahead:
                    values_pe(*nxt)
                    for f in range(2):
                        project_pe(*nxt, f)
                turn_features_pe(i, r)
                if ahead:
                    for f in range(2, 4):
                        project_pe(*nxt, f)

            xT_pe(0, 0)
            values_pe(0, 0)
            for f in range(4):
                project_pe(0, 0, f)
            with pe.Fori(0, B - 1) as b:
                for r in range(2):
                    step1_pe(b, r)
            step1_pe(B - 1, 0)
            step1_pe(B - 1, 1, ahead=False)
            meet(pe, 1)

            pe.wait_ge(fold_made, 5)

            def turn(g, k):
                pe.wait_ge(exp_made, 16 * g + k + 1)
                for part, ev in ((0, ev_a), (1, ev_d)):
                    pe.wait_ge(ev, 16 * g + k)
                    for j in range(4):
                        c = (4 * part + j) * P
                        last = pe.transpose(bank(4 + part)[:, j * P:(j + 1) * P], logits[:, k, c:c + P], ident)
                    last.then_inc(tr_made, 1)

            def quad(g, q, part, first=False):
                if part == 0:
                    pe.wait_ge(ev_a, 16 * g + 4 * q + 4)
                    pe.wait_ge(ev_d, 16 * g + 4 * q + 4)
                    if q == 0:
                        pe.wait_ge(v_in, 16 * g + 16)
                    if not (first and q == 0):
                        pe.wait_ge(o_kept, 4 * g + q)
                for tt in range(4 * part, 4 * part + 4):
                    j = tt % 4
                    last = pe.matmul(bank(6)[HD * j:HD * (j + 1), :], v_pair[:, tt, HD * (q // 2):HD * (q // 2 + 1)],
                                     pT[q % 2][:, tt, :], start=(tt < 4), stop=(tt >= 4))
                if part == 1:
                    last.then_inc(pv_made, 1)

            def combine(g, q, first=False):
                pe.wait_ge(o_kept, 4 * g + q + 1)
                if not first:
                    pe.wait_ge(att_made, 2 * g - 1 + q // 2)
                for j in range(4):
                    u = 4 * q + j
                    last = pe.matmul(bank(7)[:, u * HD:(u + 1) * HD], o_sum[:, j * P:(j + 1) * P], fold, start=True, stop=True)
                last.then_inc(folded, 1)

            def sin_pe(g, prev=True, scores=True, second=False):
                for u in range(UNITS):
                    hh, st = divmod(u, ST)
                    if scores:
                        if st == 0:
                            pe.wait_ge(f_in[hh], F_IN * (g + 1))
                        pe.wait_ge(score_used, 32 * g + u + 1)
                        for c in range(2):
                            last = pe.matmul(bank(2 * (u % 2) + c), fq[hh][:, st * P:(st + 1) * P],
                                             fk[hh][:, c * 512:(c + 1) * 512], start=True, stop=True)
                        last.then_inc(score_made, 1)
                    if prev:
                        if u in SIN_TURNS:
                            turn(g - 1, SIN_TURNS[u])
                        if u in SIN_QUADS:
                            quad(g - 1, *SIN_QUADS[u])
                        if u in SIN_FOLDS:
                            combine(g - 1, SIN_FOLDS[u], second)

            def exp_pe(g, first=False, second=False):
                for u in range(UNITS):
                    hh, st = divmod(u, ST)
                    if st == 0:
                        pe.wait_ge(c_in[hh], C_IN * (g + 1))
                    pe.wait_ge(score_used, 32 * g + 16 + u + 1)
                    for a in range(2):
                        for c in range(2):
                            last = pe.matmul(bank(2 * (u % 2) + c), qs[hh][:, a, st * P:(st + 1) * P],
                                             ks[hh][:, a, c * 512:(c + 1) * 512], start=(a == 0), stop=(a == 1))
                    last.then_inc(score_made, 1)
                    if not first and u in OLD_QUAD:
                        quad(g - 1, 3, OLD_QUAD.index(u))
                    if not first and u == OLD_FOLD:
                        combine(g - 1, 3, second)
                    if u in EXP_TURNS:
                        turn(g, EXP_TURNS[u])
                    if u in OWN_QUAD:
                        quad(g, 0, OWN_QUAD.index(u), first)
                    if u == OWN_FOLD:
                        combine(g, 0, first)

            sin_pe(0, prev=False)
            exp_pe(0, first=True)
            sin_pe(1, second=True)
            exp_pe(1, second=True)
            with pe.Fori(2, PAIRS) as g:
                sin_pe(g)
                exp_pe(g)
            sin_pe(PAIRS, scores=False)
            for part in range(2):
                quad(PAIRS - 1, 3, part)
            combine(PAIRS - 1, 3)
            meet(pe, 2)

            pe.sem_inc(pre_pe, 7)
            pe.sem_inc(ffn_pe, 7)
            pe.wait_ge(w3_in, W3_IN)
            pe.wait_ge(prep_c, 3)
            pe.wait_ge(qe_one, 1)
            for k in range(FK):
                for m in range(KD):
                    pe.transpose(bank(k // 2)[:, (k % 2) * D + m * P:(k % 2) * D + (m + 1) * P], w1[:, m, k * P:(k + 1) * P], ident)
            for k in range(FK):
                last = pe.transpose(bank(4)[:, k * NQ:(k + 1) * NQ], wqo[0:NQ, k * P:(k + 1) * P], ident[0:NQ, 0:NQ])
            last.then_inc(prep_pe, 1)
            pe.wait_ge(prep_act, 2)
            for m in range(KD):
                for k in range(FK):
                    pe.matmul(bank(5)[:, m * NQ:(m + 1) * NQ], w1T[:, k, m * P:(m + 1) * P], wm[:, k, :], start=(k == 0), stop=(k == FK - 1))
            for k in range(FK):
                pe.matmul(bank(5)[0:1, 2 * NQ:3 * NQ], b1c[:, k:k + 1], wm[:, k, :], start=(k == 0), stop=False)
            pe.matmul(bank(5)[0:1, 2 * NQ:3 * NQ], ones[0:1, 0:1], bm[0:1], start=False, stop=True)
            for k in range(FK):
                pe.matmul(bank(6)[0:NQ + 1, 0:D], wqoT[:, k, :], w2[:, k, :], start=(k == 0), stop=False)
            pe.matmul(bank(6)[0:NQ + 1, 0:D], last_row[0:1], b2[0:1], start=False, stop=True).then_inc(prep_pe, 1)
            pe.wait_ge(prep_dve, 1)
            for w in range(3):
                f = floats[:, w * HT * D:(w + 1) * HT * D]
                pe.wait_ge(prep_act, 5 if w < 2 else 6)
                for a in range(12):
                    if w < 2:
                        k, m = divmod(a, HT)
                        src = tiles(f)[:, m, k * P:(k + 1) * P]
                    else:
                        k, m = divmod(a, KD)
                        src = f.rearrange("p (k n) -> p k n", k=KD)[:, m, k * P:(k + 1) * P]
                    last = pe.transpose(bank(4 * (w % 2), 3)[:, a * P:(a + 1) * P], src, ident)
                last.then_inc(prep_pe, 1)
            pe.wait_ge(prep_act, 8)

            def flip(dst, src, done):
                for k in range(KD):
                    for j in range(TPC):
                        last = pe.transpose(dst[:, k * CH + j * P:k * CH + (j + 1) * P], src[:, j, k * P:(k + 1) * P], ident)
                last.then_inc(done, 1)

            def pre_pe_1(i, r):
                n = 2 * i + r
                pe.wait_ge(c3_in[r], C3_IN * (i + 1))
                pe.wait_ge(dve_pre, before(21, n, 12))
                flip(bank(0, 2), attc[r], pre_pe)

            def pre_pe_1b(i, r):
                n = 2 * i + r
                pe.wait_ge(act_pre, now(6, n, 1))
                for j in range(TPC):
                    for k in range(KD):
                        last = pe.matmul(bank(2, 2)[:, j * D:(j + 1) * D], aT[:, k, j * P:(j + 1) * P], wo[:, k, :],
                                         start=(k == 0), stop=(k == KD - 1))
                last.then_inc(pre_pe, 1)

            def pre_pe_2(i, r):
                n = 2 * i + r
                pe.wait_ge(pool_pre, now(8, n, 5))
                flip(bank(0, 2), x1, pre_pe)

            def pre_pe_2b(i, r):
                n = 2 * i + r
                pe.wait_ge(act_pre, now(6, n, 2))
                for j in range(TPC):
                    q = bank(2)[:, j * NQ:(j + 1) * NQ]
                    for k in range(KD):
                        pe.matmul(q, x1T[:, k, j * P:(j + 1) * P], w1m[:, k, :], start=(k == 0), stop=False)
                    last = pe.matmul(q, ones[0:1], qm_row[0:1], start=False, stop=True)
                last.then_inc(pre_pe, 1)

            def pre_pe_3(i, r):
                n = 2 * i + r
                pe.wait_ge(dve_pre, now(21, n, 11))
                for j in range(TPC):
                    last = pe.transpose(bank(3)[0:NQ + 1, j * P:(j + 1) * P], qe[:, j, :], ident)
                last.then_inc(pre_pe, 1)

            def pre_pe_3b(i, r):
                n = 2 * i + r
                pe.wait_ge(act_pre, now(6, n, 5))
                for j in range(TPC):
                    last = pe.matmul(bank(0, 2)[:, j * D:(j + 1) * D], qeT[0:NQ + 1, j * P:(j + 1) * P], w2q[0:NQ + 1, :],
                                     start=True, stop=True)
                last.then_inc(pre_pe, 1)

            def pre_pe_4(i, r):
                n = 2 * i + r
                pe.wait_ge(dve_pre, now(21, n, 21))
                flip(bank(2, 2), xp[r], pre_pe)

            def ffn_up(i, r, a, z):
                n = 2 * i + r
                if a == 0:
                    pe.wait_ge(act_pre, now(6, n, 6))
                    pe.wait_ge(dve_out, before(5, n, 1))
                for m in range(a, z):
                    pe.wait_ge(h_made, now(6, n, m - 1))
                    for w, at in ((wgT, 4), (wuT, 5)):
                        for k in range(KD):
                            last = pe.matmul(bank(at + 2 * (m % 2)), w[:, k, m * P:(m + 1) * P], xpT[r][:, k, :],
                                             start=(k == 0), stop=(k == KD - 1))
                    last.then_inc(ffn_pe, 1)

            def ffn_down(i, r, a, z):
                n = 2 * i + r
                if a == 0:
                    pe.wait_ge(h_made, now(6, n, 6))
                for j in range(a, z):
                    for m in range(HT):
                        last = pe.matmul(bank(4, 2)[:, j * D:(j + 1) * D], hT[:, m, j * P:(j + 1) * P], wdT[:, m, :],
                                         start=(m == 0), stop=(m == HT - 1))
                if z == TPC:
                    last.then_inc(ffn_pe, 1)

            def step_pe(i, r, ahead=True):
                nxt = (i + r, 1 - r)
                if ahead:
                    pre_pe_1(*nxt)
                ffn_up(i, r, 0, 1)
                if ahead:
                    pre_pe_1b(*nxt)
                ffn_up(i, r, 1, 4)
                if ahead:
                    pre_pe_2(*nxt)
                ffn_up(i, r, 4, 5)
                if ahead:
                    pre_pe_2b(*nxt)
                ffn_up(i, r, 5, HT)
                if ahead:
                    pre_pe_3(*nxt)
                ffn_down(i, r, 0, 1)
                if ahead:
                    pre_pe_3b(*nxt)
                ffn_down(i, r, 1, TPC)
                if ahead:
                    pre_pe_4(*nxt)

            for part in (pre_pe_1, pre_pe_1b, pre_pe_2, pre_pe_2b, pre_pe_3, pre_pe_3b, pre_pe_4):
                part(0, 0)
            with pe.Fori(0, B - 1) as i:
                for r in range(2):
                    step_pe(i, r)
            step_pe(B - 1, 0)
            step_pe(B - 1, 1, ahead=False)
            meet(pe, 3)

            pe.wait_ge(w5_in, W5_IN)
            for k in range(KD):
                last = pe.transpose(bank(0)[:, k * E:(k + 1) * E], rt_w[0:E, k * P:(k + 1) * P], ident[0:E, 0:E])
            last.then_inc(prep5_pe, 1)
            pe.wait_ge(prep5_act, 3)
            pe.wait_ge(prep5, 3)
            pe.sem_inc(pe_a, 12)
            pe.sem_inc(pe_b, 8)

            def flip8(at, src, done):
                for k in range(KD):
                    for j in range(ST):
                        last = pe.transpose(bank(at, 4)[:, k * S + j * P:k * S + (j + 1) * P], src[:, j, k * P:(k + 1) * P], ident)
                last.then_inc(done, 1)

            def project(at, w, m, src, done):
                for c in range(2):
                    for k in range(KD):
                        last = pe.matmul(bank(at + c), w[:, k, m * P:(m + 1) * P], src[:, k, c * CH:(c + 1) * CH],
                                         start=(k == 0), stop=(k == KD - 1))
                last.then_inc(done, 1)

            def first_pe(i, r):
                n = 2 * i + r
                pe.wait_ge(pool_f, now(3, n, 3))
                pe.wait_ge(dve_a, before(15, n, 15))
                flip8(0, norm_a, pe_a)
                pe.wait_ge(act_a, now(15, n, 1))
                project(0, in_w, 0, T_a, pe_a)
                project(2, in_w, 1, T_a, pe_a)
                for m in range(KD):
                    pe.wait_ge(act_a, now(15, n, 2 + m))
                    project(2 * m, in_w, 2 + m, T_a, pe_a)

            def scan_pe_1(i, r):
                n = 2 * i + r
                pe.wait_ge(dve_a, now(15, n, 6))
                for m in range(KD):
                    pe.wait_ge(act_a, now(15, n, 4 + m))
                    project(2 * m, dt_w, m, mixed, pe_a)
                for m in range(KD):
                    pe.wait_ge(act_a, now(15, n, 6 + m))
                    project(2 * m, b_w, m, mixed, pe_a)

            def scan_pe_2(i, r):
                n = 2 * i + r
                for m in range(KD):
                    pe.wait_ge(act_a, now(15, n, 8 + m))
                    project(2 * m, c_w, m, mixed, pe_a)

            def mix_pe(i, r):
                n = 2 * i + r
                pe.wait_ge(act_a, now(15, n, 15))
                pe.wait_ge(dve_a, now(15, n, 14))
                for j in range(ST):
                    for k in range(KD):
                        last = pe.matmul(bank(0, 4)[:, j * D:(j + 1) * D], ct[:, k, j * P:(j + 1) * P], out_w[:, k, :],
                                         start=(k == 0), stop=(k == KD - 1))
                last.then_inc(pe_a, 1)

            def second_pe(i, r):
                n = 2 * i + r
                pe.wait_ge(pool_b, now(6, n, 3))
                pe.wait_ge(dve_b, before(10, n, 10))
                flip8(4, norm_b, pe_b)

            def up_pe(i, r):
                n = 2 * i + r
                pe.wait_ge(act_b, now(6, n, 1))
                for m in range(4):
                    if m >= 2:
                        pe.wait_ge(act_b, now(6, n, m))
                    project(4 + 2 * (m % 2), f1_w, m, T_b, pe_b)

            def down_pe(i, r):
                n = 2 * i + r
                pe.wait_ge(act_b, now(6, n, 5))
                for j in range(ST):
                    for m in range(4):
                        last = pe.matmul(bank(4, 4)[:, j * D:(j + 1) * D], gl[:, m, j * P:(j + 1) * P], f2_w[:, m, :],
                                         start=(m == 0), stop=(m == 3))
                last.then_inc(pe_b, 1)

            def turn_pe(i, r):
                n = 2 * i + r
                pe.wait_ge(dve_b, now(10, n, 9))
                flip8(4, norm_b, pe_b)

            def logits_pe(i, r):
                n = 2 * i + r
                pe.wait_ge(act_b, now(6, n, 6))
                for j in range(ST):
                    q = bank(4)[:, j * E:(j + 1) * E]
                    for k in range(KD):
                        pe.matmul(q, T_b[:, k, j * P:(j + 1) * P], rt_wT[:, k, :], start=(k == 0), stop=False)
                    last = pe.matmul(q, ones4[0:1], rt_b[0:1], start=False, stop=True)
                last.then_inc(pe_b, 1)

            def step4_pe(i, r, scan=True):
                nxt = (i + r, 1 - r)
                if scan:
                    first_pe(*nxt)
                second_pe(i, r)
                if scan:
                    scan_pe_1(*nxt)
                    scan_pe_2(*nxt)
                up_pe(i, r)
                down_pe(i, r)
                if scan:
                    mix_pe(*nxt)
                turn_pe(i, r)
                logits_pe(i, r)

            first_pe(0, 0)
            scan_pe_1(0, 0)
            scan_pe_2(0, 0)
            mix_pe(0, 0)
            with pe.Fori(0, B // 2 - 1) as i:
                for r in range(2):
                    step4_pe(i, r)
            step4_pe(B // 2 - 1, 0)
            step4_pe(B // 2 - 1, 1, scan=False)
            meet(pe, 4)

            pe.wait_ge(const6, 2)
            pe.wait_ge(top6, TOP_STEPS_E)
            both_f = both.rearrange("p t e -> p (t e)")
            pe.matmul(bank(0)[:, 0:TILES * E], below, both_f, start=True, stop=True)
            pe.matmul(bank(1)[:, 0:TILES * E], ones6, both_f, start=True, stop=True).then_inc(count_pe, 1)
            pe.sem_inc(pe6, 6)
            pe.wait_ge(idx6, 2)
            with pe.Fori(0, E // 2) as i:
                for r in range(2):
                    e = 2 * i + r
                    pe.wait_ge(e_in[r], 64 * (i + 1))
                    pe.wait_ge(act6, before(6, e, 1))
                    flip(bank(0, 2), xe_s[r], pe6)
                    pe.wait_ge(act6, now(6, e, 1))
                    for m in range(4):
                        pe.wait_ge(dve6, now(4, e, m - 1))
                        for w, at in ((we[r], 2), (ve[r], 3)):
                            for k in range(KD):
                                last = pe.matmul(bank(at + 2 * (m % 2)), w[:, k, m * P:(m + 1) * P], XT[:, k, :],
                                                 start=(k == 0), stop=(k == KD - 1))
                        last.then_inc(pe6, 1)
                    pe.wait_ge(dve6, now(4, e, 4))
                    pe.wait_ge(act6, before(6, e, 6))
                    for j in range(TPC):
                        for m in range(4):
                            last = pe.matmul(bank(6, 2)[:, j * D:(j + 1) * D], h6[:, m, j * P:(j + 1) * P], woe[r][:, m, :],
                                             start=(m == 0), stop=(m == 3))
                    last.then_inc(pe6, 1)
            meet(pe, 5)


_OUTS = [((B, S, D), "float32")]


def kernel(**inputs):
    import numpy as _np
    import concourse.bacc as _bacc
    from concourse import mybir as _mybir
    from concourse.bass_utils import run_bass_kernel_spmd as _run

    nc = _bacc.Bacc("TRN2", target_bir_lowering=False, num_devices=1)
    arrays, t = {}, {}
    for name in inputs:
        a = _np.ascontiguousarray(inputs[name])
        arrays["in_" + name] = a
        t[name] = nc.dram_tensor("in_" + name, a.shape, _mybir.dt.from_np(a.dtype), kind="ExternalInput").ap()
    out = nc.dram_tensor("out", (B, S, D), F32, kind="ExternalOutput").ap()
    build_program(nc, t, out)
    r = _run(nc, [arrays], core_ids=[0])
    return r.results[0]["out"]
```

```python
import concourse.bass as bass
from concourse import mybir
from concourse.alu_op_type import AluOpType as ALU
from contextlib import ExitStack

ACT = mybir.ActivationFunctionType
AX = mybir.AxisListType
F32 = mybir.dt.float32
BF16 = mybir.dt.bfloat16
I32 = mybir.dt.int32
U32 = mybir.dt.uint32

P = 128
B, S, D = 4, 1024, 256
N = B * S
TILES = N // P
H, HD, NQ = 8, 32, 8
KD = D // P
CH = 512
TPC = CH // P
ST = S // P
PAIRS = B * H // 2
UNITS = 2 * ST
FID_SCALE = 0.05
SIN_SCALE = float(-3.14159265 / FID_SCALE * (1.0 - 4e-7))
SIN_TURNS = {1: 8, 3: 9, 5: 10, 7: 11, 9: 12, 11: 13, 13: 14, 15: 15}
SIN_QUADS, SIN_FOLDS = {2: (1, 0), 4: (1, 1), 10: (2, 0), 12: (2, 1)}, {6: 1, 14: 2}
EXP_TURNS = {3: 0, 5: 1, 7: 2, 9: 3, 11: 4, 13: 5, 14: 6, 15: 7}
OLD_QUAD, OLD_FOLD, OWN_QUAD, OWN_FOLD = (1, 2), 4, (12, 14), 15
SCORE_SCALE = float(-0.5 / (HD ** 0.5))
TINY = 1e-37
EPS_COS = 1e-8
SMALL_NORM = 1.1e-4
RSQRT_START = 1597463007.0
FF, FK, HID, HT = 1024, 8, 768, 6
LN_EPS = 1e-5
ROUND = 12582912.0
PI = 3.141592653589793
W3_IN = 16 * (15 + 2 * FK)
E, CAP = 8, 512
TOP_A, TOP_B = 13, 16
C3_IN = 16 * (H // 2 + 1)
ZEROS = 9216
W5_IN = 16 * (15 + 8 + 2 * 7)
W_DMAS = 6 + 4 + 1 + 2 + 8


def now(per, n, k):
    return per * (n + 1) + k


def before(per, n, k):
    return per * n + k


def build_program(nc, t, out):
    ctx = ExitStack()
    with ctx:
        def sem(name):
            return ctx.enter_context(nc.semaphore(name))

        arena = ctx.enter_context(nc.sbuf_tensor("arena", [P, 51200], F32))
        banks = ctx.enter_context(nc.psum_tensor("banks", [P, 8 * 512], F32))

        def fp(at, n):
            return arena[:, at:at + n]

        def bank(i, n=1):
            return banks[:, i * 512:(i + n) * 512]

        q_planes = nc.dram_tensor("q_planes", [3, B * H, HD, S], BF16, kind="Internal").ap()
        k_planes = nc.dram_tensor("k_planes", [3, B * H, HD, S], BF16, kind="Internal").ap()
        fq_planes = nc.dram_tensor("fq_planes", [3, B * H, NQ, S], BF16, kind="Internal").ap()
        fk_planes = nc.dram_tensor("fk_planes", [3, B * H, NQ, S], BF16, kind="Internal").ap()

        ident = fp(0, 128)
        fscale = fp(128, 1)
        q_norms, k_norms = (fp(1024 + i * B * H * ST, B * H * ST).rearrange("p (h s) -> p h s", s=ST) for i in range(2))
        rsum = fp(136, UNITS)
        rinv = fp(152, UNITS)
        nmax = fp(168, UNITS)
        v_pairs = nc.dram_tensor("v_pairs", [PAIRS, S, 2 * HD], F32, kind="Internal").ap()
        att_pairs = nc.dram_tensor("att_pairs", [PAIRS, S, 2 * HD], F32, kind="Internal").ap()
        key_norms = nc.dram_tensor("key_norms", [B * H, S], F32, kind="Internal").ap()
        flag = fp(200, 1)[0:1].bitcast(I32)
        low_norm = fp(208, 1)
        R3 = 18432

        o = R3
        def take(n):
            nonlocal o
            o += n
            return fp(o - n, n)
        wq = take(KD * D).rearrange("p (k n) -> p k n", k=KD)
        wk = take(KD * D).rearrange("p (k n) -> p k n", k=KD)
        wv = take(KD * D).rearrange("p (k n) -> p k n", k=KD)
        wc = take(KD * H * NQ).rearrange("p (k n) -> p k n", k=KD)
        bqk = take(4)
        bvb = take(D)
        bcb = take(2 * H * NQ)
        half = fp(256, 64)
        xin = [take(TPC * D).rearrange("p (j n) -> p j n", j=TPC) for _ in range(2)]
        xT = take(KD * CH).rearrange("p (k n) -> p k n", k=KD)
        feat = take(5 * CH).rearrange("p (f n) -> p f n", f=5)
        rest = take(5 * CH).rearrange("p (f n) -> p f n", f=5)
        planes = [take(5 * 3 * CH // 2).bitcast(BF16).rearrange("p (f l n) -> p f l n", f=5, l=3) for _ in range(2)]
        qk = take(TPC * P).rearrange("p (j n) -> p j n", j=TPC)
        qk2 = take(TPC * P).rearrange("p (j n) -> p j n", j=TPC)
        ss = take(TPC * 2 * H)
        rn = take(TPC * 2 * H)
        rn2 = take(TPC * 2 * H)
        assert o <= 51200

        v_out = [take(TPC * D).rearrange("p (j n) -> p j n", j=TPC) for _ in range(2)]
        assert o <= 51200

        o = 2048
        logits = take(UNITS * S).rearrange("p (u n) -> p u n", u=UNITS)
        fq = [take(S // 2).bitcast(BF16) for _ in range(2)]
        fk = [take(S // 2).bitcast(BF16) for _ in range(2)]
        qs = [take(S).bitcast(BF16).rearrange("p (a n) -> p a n", a=2) for _ in range(2)]
        ks = [take(S).bitcast(BF16).rearrange("p (a n) -> p a n", a=2) for _ in range(2)]
        sn = [take(S) for _ in range(2)]
        pT = [take(ST * 4 * P).rearrange("p (t n) -> p t n", t=ST) for _ in range(2)]
        v_pair = take(ST * 2 * HD).rearrange("p (t n) -> p t n", t=ST)
        o_sum = take(4 * P)
        att_s = take(ST * 2 * HD).rearrange("p (t n) -> p t n", t=ST)
        fold = take(HD)
        key_norm = [take(S) for _ in range(2)]
        query_norm = [take(ST) for _ in range(2)]
        share = take(S)
        prefetched = o
        w1 = take(KD * FF).rearrange("p (k n) -> p k n", k=KD)
        w2 = take(FK * D).rearrange("p (k n) -> p k n", k=FK)
        wm = take(FK * NQ).rearrange("p (k n) -> p k n", k=FK)
        ints = take(3 * HT * D).bitcast(I32)
        b1c = take(FK)
        wqo = take(FF)
        wqoT = take(FK * (NQ + 1)).rearrange("p (k n) -> p k n", k=FK)
        bm = take(NQ)
        b2 = take(D)
        prefetched_end = o
        assert o <= 51200

        o = 2048
        wo = take(KD * D).rearrange("p (k n) -> p k n", k=KD)
        wgT = take(KD * HID).rearrange("p (k n) -> p k n", k=KD)
        wuT = take(KD * HID).rearrange("p (k n) -> p k n", k=KD)
        wdT = take(HT * D).rearrange("p (k n) -> p k n", k=HT)
        w1m = take(KD * NQ).rearrange("p (k n) -> p k n", k=KD)
        qm_col = take(NQ)[:, 0:1]
        w2q = take(D)
        ones = take(P)
        last_row = take(NQ + 1)
        bo_b, g1_b, be1_b, g2_b, be2_b = (take(D) for _ in range(5))
        assert o <= ZEROS
        o = R3
        tiles = lambda a: a.rearrange("p (j n) -> p j n", n=D)
        attc = [tiles(take(TPC * D)) for _ in range(2)]
        xc = [tiles(take(TPC * D)) for _ in range(2)]
        xbo, xb2, r1, x1, r2, r3 = (tiles(take(TPC * D)) for _ in range(6))
        aT = take(KD * CH).rearrange("p (k n) -> p k n", k=KD)
        x1T = take(KD * CH).rearrange("p (k n) -> p k n", k=KD)
        xp, xpT, whole = [], [], []
        for _ in range(2):
            whole.append(o)
            xp.append(tiles(take(TPC * D)))
            xpT.append(take(KD * CH).rearrange("p (k n) -> p k n", k=KD))
        mid_q, turns, th, cs = (take(CH)[0:NQ] for _ in range(4))
        qeT = take(CH)
        stats = take(8 * 6).rearrange("p (j s) -> p j s", s=6)
        stats_f = take(8 * 6).rearrange("p (j s) -> p j s", s=6)
        moments = take(8 * 2).rearrange("p (j s) -> p j s", s=2)
        moments_f = take(8 * 2).rearrange("p (j s) -> p j s", s=2)
        var = take(8)
        var_f = take(8)
        rstd = take(8)
        rstd_f = take(8)
        w1T = fp(16384, FK * D).rearrange("p (k n) -> p k n", k=FK)
        floats = [fp(at, HT * D) for at in (o, 51200 - HT * D, whole[1])]
        assert o + HT * D <= prefetched and prefetched_end <= 51200 - HT * D and HT * D <= TPC * D + KD * CH
        r4 = tiles(take(TPC * D))
        xo = [tiles(take(TPC * D)) for _ in range(2)]
        sg = [take(CH) for _ in range(2)]
        hT = take(HT * CH).rearrange("p (k n) -> p k n", k=HT)
        assert o <= 51200
        x_mid = nc.dram_tensor("x_mid", [N, D], F32, kind="Internal").ap()
        x_mid_c = x_mid.rearrange("(c j p) n -> c p j n", j=TPC, p=P)
        rows = lambda w: w.rearrange("(k p) n -> p k n", p=P)

        o = 320
        ln1g_b, ln1b_b, ln2g_b, ln2b_b, outb_b, f2b_b = (take(D) for _ in range(6))
        assert o <= 2048
        x_all = tiles(fp(2048, TILES * D))
        o = 10240
        kn = lambda a, k: a.rearrange("p (k n) -> p k n", k=k)
        in_w = kn(take(KD * 2 * D), KD)
        dt_w, b_w, c_w, out_w = (kn(take(KD * D), KD) for _ in range(4))
        f1_w = kn(take(KD * 2 * D), KD)
        f2_w = kn(take(2 * KD * D), 2 * KD)
        rt_w = take(D)
        rt_wT = kn(take(KD * E), KD)
        rt_b = take(E)
        in_b = take(4)
        taps = kn(take(KD * 3), KD)
        tap_b, dt_b, b_b, c_b, a_neg, skip = (take(KD) for _ in range(6))
        f1_b = take(4)
        lg_all = take(TILES * E).rearrange("p (t e) -> p t e", e=E)
        xr = [tiles(take(ST * D)) for _ in range(2)]
        assert o - ST * D <= R3
        norm_a = take(ST * D)
        T_a = take(KD * S)
        gate, mixed, z, ct, dt = (kn(take(KD * S), KD) for _ in range(5))
        xpad = kn(take(KD * (S + 2)), KD)
        x2 = tiles(take(ST * D))
        l, v, state, decay = kn(norm_a, KD), kn(T_a, KD), dt, z
        norm_a, T_a = tiles(norm_a), kn(T_a, KD)
        norm_b, x3 = (tiles(take(ST * D)) for _ in range(2))
        T_b = kn(take(KD * S), KD)
        gl = kn(take(2 * KD * S), 2 * KD)
        stats5 = take(ST * 6).rearrange("p (j s) -> p j s", s=6)
        mom5 = take(ST * 2).rearrange("p (j s) -> p j s", s=2)
        var5, rstd5 = take(ST), take(ST)
        stats_b = take(ST * 6).rearrange("p (j s) -> p j s", s=6)
        mom_b = take(ST * 2).rearrange("p (j s) -> p j s", s=2)
        var_b, rstd_b = take(ST), take(ST)
        zeros = fp(ZEROS, TPC * D)
        ones4 = take(P)

        TOP_AT = o
        by_expert = lambda: take(TILES * E).rearrange("p (t e) -> p t e", e=E)
        rev, mask1, mask2, both = (by_expert() for _ in range(4))
        eq, rest6, tot, pos = (take(ST * E).rearrange("p (t e) -> p t e", e=E) for _ in range(4))
        top1, top2, s1, s2, p1, p2, slot, fits = (take(TILES) for _ in range(8))
        idx = [take(TILES).bitcast(U32) for _ in range(2)]
        below, ones6 = take(P), take(P)
        carry = take((B + 1) * E).rearrange("p (b e) -> p b e", e=E)
        assert o <= 51200, o
        x_mid_b = x_mid.rearrange("(b j p) n -> b p j n", j=ST, p=P)
        xe = nc.dram_tensor("x_by_expert", [E * CAP, D], F32, kind="Internal").ap()
        ye = nc.dram_tensor("y_by_expert", [E * CAP + 1, D], F32, kind="Internal").ap()

        o = 26624
        xe_s = [tiles(take(TPC * D)) for _ in range(2)]
        we = [kn(take(KD * CAP), KD) for _ in range(2)]
        ve = [kn(take(KD * CAP), KD) for _ in range(2)]
        woe = [kn(take(4 * D), 4) for _ in range(2)]
        XT = kn(take(KD * CAP), KD)
        sg6 = [take(CAP) for _ in range(2)]
        h6 = kn(take(4 * CAP), 4)
        ye_s = [tiles(take(TPC * D)) for _ in range(2)]
        y_g = [tiles(fp(10240 + s * TILES * D, TILES * D)) for s in range(2)]
        acc = [tiles(take(TPC * D)) for _ in range(2)]
        fin = [tiles(take(TPC * D)) for _ in range(2)]
        stats6 = take(TPC * 6).rearrange("p (j s) -> p j s", s=6)
        mom6 = take(TPC * 2).rearrange("p (j s) -> p j s", s=2)
        var6, rstd6 = take(TPC), take(TPC)
        assert o <= TOP_AT, o
        got6 = [sem(f"got6_{c}") for c in range(TILES // TPC)]
        out_c = out.rearrange("b (c j p) n -> (b c) p j n", j=TPC, p=P)

        qe_one = sem("qe_one")
        c3_in = [sem("c3_in0"), sem("c3_in1")]
        x_out = [sem("x_out0"), sem("x_out1")]
        w3_in = sem("w3_in")
        prep_pe = sem("prep_pe")
        prep_act = sem("prep_act")
        prep_dve = sem("prep_dve")
        prep_c = sem("prep_c")
        pre_pe = sem("pre_pe")
        ffn_pe = sem("ffn_pe")
        act_pre = sem("act_pre")
        act_silu = sem("act_silu")
        dve_pre = sem("dve_pre")
        h_made = sem("h_made")
        dve_out = sem("dve_out")
        pool_pre = sem("pool_pre")
        pool_ffn = sem("pool_ffn")
        x5_in = [sem("x5_in0"), sem("x5_in1")]
        w5_in = sem("w5_in")
        zero_in = sem("zero_in")
        x3_out = sem("x3_out")
        pe_a = sem("pe_a")
        pe_b = sem("pe_b")
        act_a = sem("act_a")
        act_b = sem("act_b")
        dve_a = sem("dve_a")
        dve_f = sem("dve_f")
        dve_b = sem("dve_b")
        pool_a = sem("pool_a")
        pool_f = sem("pool_f")
        pool_b = sem("pool_b")
        prep5_pe = sem("prep5_pe")
        prep5_act = sem("prep5_act")
        prep5 = sem("prep5")
        const5 = sem("const5")
        e_in = [sem("e_in0"), sem("e_in1")]
        y_out = [sem("y_out0"), sem("y_out1")]
        const6 = sem("const6")
        count_pe = sem("count_pe")
        top6 = sem("top6")
        exp6 = sem("exp6")
        idx6 = sem("idx6")
        sent6 = sem("sent6")
        pe6 = sem("pe6")
        act6 = sem("act6")
        dve6 = sem("dve6")
        fin6 = sem("fin6")
        pow6 = sem("pow6")
        fin_out = [sem("fin_out0"), sem("fin_out1")]
        s_const = sem("s_const")
        s_w = sem("s_w")
        s_fscale = sem("s_fscale")
        passed = sem("passed")
        s_x = [sem("s_x0"), sem("s_x1")]
        s_xT = sem("s_xT")
        s_xTs = sem("s_xTs")
        s_proj = sem("s_proj")
        s_feat = sem("s_feat")
        s_feat_f = sem("s_feat_f")
        s_v = sem("s_v")
        s_qq = sem("s_qq")
        s_qkb = sem("s_qkb")
        s_sq = sem("s_sq")
        norms_made = sem("norms_made")
        s_rn = sem("s_rn")
        s_qn = sem("s_qn")
        s_fT = sem("s_fT")
        s_hi = sem("s_hi")
        s_hi_f = sem("s_hi_f")
        s_rest = sem("s_rest")
        s_rest_f = sem("s_rest_f")
        s_mid = sem("s_mid")
        s_mid_f = sem("s_mid_f")
        s_lo = sem("s_lo")
        s_lo_f = sem("s_lo_f")
        s_st = [sem("s_st0"), sem("s_st1")]
        stage = sem("stage")

        rows_cleared = sem("rows_cleared")
        score_made = sem("score_made")
        score_used = sem("score_used")
        sin_made = sem("sin_made")
        exp_made = sem("exp_made")
        tr_made = sem("tr_made")
        ev_a = sem("ev_a")
        ev_d = sem("ev_d")
        pv_made = sem("pv_made")
        att_made = sem("att_made")
        fold_made = sem("fold_made")
        o_kept = sem("o_kept")
        folded = sem("folded")
        v_in = sem("v_in")
        att_out = sem("att_out")
        vs_out = [sem("vs_out0"), sem("vs_out1")]
        flag_pe = sem("flag_pe")
        flag_made = sem("flag_made")
        norms_out = sem("norms_out")
        norms_in = [sem("norms_in0"), sem("norms_in1")]
        guarded = sem("guarded")
        share_made = sem("share_made")
        rinv_made = sem("rinv_made")
        f_in = [sem("f_in0"), sem("f_in1")]
        c_in = [sem("c_in0"), sem("c_in1")]

        block = ctx.enter_context(nc.Block())

        def meet(eng, k):
            eng.drain().then_inc(stage, 1)
            eng.wait_ge(stage, 5 * k)

        x_tok = t["L0_attn_x"].rearrange("b (c j p) n -> (b c) p j n", j=TPC, p=P)


        def load_f(sp, g, hh):
            gh = 2 * g + hh
            for rep in range(3):
                sp.dma_start(fq[hh][rep * 24:rep * 24 + 24, :],
                             fq_planes[:, bass.ds(gh, 1), :, :].rearrange("l o d n -> l (o d) n")).then_inc(f_in[hh], 16)
                sp.dma_start(fk[hh][rep * 24:rep * 24 + 24, :],
                             fk_planes[rep, bass.ds(gh, 1), :, :].rearrange("o d n -> (o d) n").partition_broadcast(3)).then_inc(f_in[hh], 16)

        def load_c(sp, g, hh):
            gh = 2 * g + hh
            q = lambda a, z: q_planes[a:z, bass.ds(gh, 1), :, :].rearrange("l o d n -> l (o d) n")
            k = lambda l, n: k_planes[l, bass.ds(gh, 1), :, :].rearrange("o d n -> (o d) n").partition_broadcast(n)
            for dst, src in ((qs[hh][0:96, 0, :], q(0, 3)), (qs[hh][96:128, 0, :], q(0, 1)),
                             (qs[hh][0:64, 1, :], q(1, 3)), (qs[hh][64:128, 1, :], q(0, 2)),
                             (ks[hh][0:96, 0, :], k(0, 3)), (ks[hh][96:128, 0, :], k(1, 1)),
                             (ks[hh][0:64, 1, :], k(1, 2)), (ks[hh][64:128, 1, :], k(2, 2))):
                sp.dma_start(dst, src).then_inc(c_in[hh], 16)

        F_IN, C_IN = 6 * 16, 8 * 16

        @block.sync
        def _(sp):
            for r in range(2):
                sp.dma_start(xin[r], x_tok[r]).then_inc(s_x[r], 16)
            for k in range(KD):
                for dst, src in ((wq, "L0_attn_Wq"), (wk, "L0_attn_Wk"), (wv, "L0_attn_Wv")):
                    sp.dma_start(dst[:, k, :].rearrange("p (h d) -> p h d", h=H),
                                 t[src][:, k * P:(k + 1) * P, :].rearrange("h p d -> p h d")).then_inc(s_w, 16)
            for i, n in enumerate(("L0_attn_bq", "L0_attn_bk")):
                for k in range(KD):
                    sp.dma_start(bqk[:, 2 * i + k:2 * i + k + 1],
                                 t[n].rearrange("(k h) d -> k (h d)", k=KD)[k].rearrange("(p o) -> p o", o=1)).then_inc(s_w, 16)
            sp.dma_start(bvb, t["L0_attn_bv"].rearrange("h d -> (h d)").partition_broadcast(P)).then_inc(s_w, 16)

            def store_v(i, r):
                sp.wait_ge(s_v, now(1, 2 * i + r, 1))
                for hp in range(H // 2):
                    sp.dma_start(v_pairs[bass.ds(4 * i + hp, 1), r * CH:(r + 1) * CH, :].rearrange("o (j p) d -> p (o j) d", p=P),
                                 v_out[r][:, :, hp * 64:(hp + 1) * 64]).then_inc(vs_out[r], 16)

            def store_qk(i, r):
                sp.wait_ge(s_lo, now(4, 2 * i + r, 4))
                for f, dst in enumerate((q_planes, q_planes, k_planes, k_planes)):
                    d = dst[:, bass.ds(i * H + 4 * (f % 2), 4), :, r * CH:(r + 1) * CH].rearrange("l h d n -> (h d) l n")
                    sp.dma_start(d, planes[r][:, f]).then_inc(s_st[r], 16)

            def store_features(i, r):
                sp.wait_ge(s_lo_f, now(1, 2 * i + r, 1))
                for f, dst in enumerate((fq_planes, fk_planes)):
                    d = dst[:, bass.ds(i * H, H), :, r * CH:(r + 1) * CH].rearrange("l h d n -> (h d) l n")
                    sp.dma_start(d, planes[r][64 * f:64 * f + 64, 4]).then_inc(s_st[r], 16)

            def step1_sp(i, r, ahead=True):
                if ahead:
                    store_v(i + r, 1 - r)
                store_features(i, r)
                if ahead:
                    store_qk(i + r, 1 - r)

            store_v(0, 0)
            store_qk(0, 0)
            with sp.Fori(0, B - 1) as b:
                for r in range(2):
                    sp.wait_ge(s_xT, now(1, 2 * b + r, 1))
                    sp.dma_start(xin[r], x_tok[bass.ds(2 * b + (2 + r), 1)].rearrange("o p j n -> p (o j) n")).then_inc(s_x[r], 16)
                    step1_sp(b, r)
            step1_sp(B - 1, 0)
            step1_sp(B - 1, 1, ahead=False)
            for r in range(2):
                sp.wait_ge(s_st[r], 96 * (B + 1))
                sp.wait_ge(vs_out[r], 64 * (B + 1))
            meet(sp, 1)

            def load_norms(g, hh):
                gh = 2 * g + hh
                sp.dma_start(key_norm[hh], key_norms[bass.ds(gh, 1)].rearrange("o s -> (o s)").partition_broadcast(P)).then_inc(norms_in[hh], 16)
                sp.dma_start(query_norm[hh], q_norms[:, bass.ds(gh, 1), :].rearrange("p o s -> p (o s)")).then_inc(norms_in[hh], 16)

            sp.wait_ge(flag_made, 3)
            small = sp.value_load(flag)
            with sp.If(small > 0):
                with sp.Fori(0, B * H) as gh:
                    sp.dma_start(key_norms[bass.ds(gh, 1)].rearrange("o (s p) -> p (o s)", p=P),
                                 k_norms[:, bass.ds(gh, 1), :].rearrange("p o s -> p (o s)"),
                                 allow_slow_non_contiguous=True).then_inc(norms_out, 16)
                sp.wait_ge(norms_out, B * H * 16)
                for hh in range(2):
                    load_norms(0, hh)

            def load_v(g):
                sp.dma_start(v_pair, v_pairs[bass.ds(g, 1)].rearrange("o (t p) d -> p (o t) d", p=P)).then_inc(v_in, 16)

            def store_att(g):
                sp.wait_ge(att_made, 2 * g + 2)
                sp.dma_start(att_pairs[bass.ds(g, 1)].rearrange("o (t p) d -> p (o t) d", p=P), att_s).then_inc(att_out, 16)

            def pair_sp(g, first=False, last=False):
                for hh in range(2):
                    if not last:
                        sp.wait_ge(score_made, 32 * g + 8 * (hh + 1))
                        load_f(sp, g + 1, hh)
                        with sp.If(small > 0):
                            sp.wait_ge(share_made, 16 * g + 8 * (hh + 1))
                            load_norms(g + 1, hh)
                if not first:
                    sp.wait_ge(pv_made, 4 * g)
                    load_v(g)
                    store_att(g - 1)
                for hh in range(2):
                    if not last:
                        sp.wait_ge(score_made, 32 * g + 16 + 8 * (hh + 1))
                        load_c(sp, g + 1, hh)

            sp.wait_ge(rows_cleared, 4)
            for hh in range(2):
                load_f(sp, 0, hh)
            for hh in range(2):
                load_c(sp, 0, hh)
            load_v(0)
            for dst, src in ((w1, rows(t["L0_attn_W1"])), (w2, rows(t["L0_attn_W2"])), (wm, rows(t["L0_attn_Wm"])),
                             (wqo[0:NQ], t["L0_attn_Wqo"]), (bm[0:1], t["L0_attn_bm"].unsqueeze(0)), (b2[0:1], t["L0_attn_b2"].unsqueeze(0)),
                             (tiles(ints[:, 0:HT * D]), rows(t["L0_ffn_w_gate"])), (tiles(ints[:, HT * D:2 * HT * D]), rows(t["L0_ffn_w_up"])),
                             (ints[:, 2 * HT * D:].rearrange("p (k n) -> p k n", k=KD), rows(t["L0_ffn_w_down"]))):
                sp.dma_start(dst, src).then_inc(w3_in, 16)
            for k in range(FK):
                sp.dma_start(b1c[:, k:k + 1], t["L0_attn_b1"][k * P:(k + 1) * P].unsqueeze(1)).then_inc(w3_in, 16)
                sp.dma_start(wqoT[:, k, NQ:NQ + 1], t["L0_attn_bqo"][k * P:(k + 1) * P].unsqueeze(1)).then_inc(w3_in, 16)
            pair_sp(0, first=True)
            with sp.Fori(1, PAIRS - 1) as g:
                pair_sp(g)
            pair_sp(PAIRS - 1, last=True)
            store_att(PAIRS - 1)
            sp.wait_ge(att_out, 16 * PAIRS)
            meet(sp, 2)

            for dst, src in ((wo, rows(t["L0_attn_Wo"])), (bo_b, t["L0_attn_bo"].partition_broadcast(P)),
                             (g1_b, t["L0_attn_g1"].partition_broadcast(P)), (be1_b, t["L0_attn_beta1"].partition_broadcast(P)),
                             (g2_b, t["L0_attn_g2"].partition_broadcast(P)), (be2_b, t["L0_attn_beta2"].partition_broadcast(P))):
                sp.dma_start(dst, src).then_inc(w3_in, 16)

            def load3(i, r):
                for hp in range(H // 2):
                    sp.dma_start(attc[r][:, :, hp * 64:(hp + 1) * 64],
                                 att_pairs[bass.ds(4 * i + hp, 1), r * CH:(r + 1) * CH, :].rearrange("o (j p) d -> p (o j) d", p=P)).then_inc(c3_in[r], 16)
                sp.dma_start(xc[r], x_tok[bass.ds(2 * i + r, 1)].rearrange("o p j n -> p (o j) n")).then_inc(c3_in[r], 16)

            def store3(n, r):
                sp.wait_ge(dve_out, now(5, n, 5))
                sp.dma_start(x_mid_c[bass.ds(n, 1)].rearrange("o p j n -> p (o j) n"), xo[r]).then_inc(x_out[r], 16)

            for r in range(2):
                load3(0, r)
            col = lambda w, k: w.rearrange("(k p) -> k p", p=P)[k].unsqueeze(1)
            for dst, src in ((in_w, rows(t["L1_attn_in_W"])), (dt_w, rows(t["L1_attn_dt_W"])), (b_w, rows(t["L1_attn_b_W"])),
                             (c_w, rows(t["L1_attn_c_W"])), (out_w, rows(t["L1_attn_out_W"])), (f1_w, rows(t["L1_attn_f1_W"])),
                             (f2_w, rows(t["L1_attn_f2_W"])), (rt_w[0:E], t["L1_ffn_router_w"]),
                             (rt_b[0:1], t["L1_ffn_router_b"].unsqueeze(0)),
                             (ln1g_b, t["L1_attn_ln1_g"].partition_broadcast(P)), (ln1b_b, t["L1_attn_ln1_b"].partition_broadcast(P)),
                             (ln2g_b, t["L1_attn_ln2_g"].partition_broadcast(P)), (ln2b_b, t["L1_attn_ln2_b"].partition_broadcast(P)),
                             (outb_b, t["L1_attn_out_b"].partition_broadcast(P)), (f2b_b, t["L1_attn_f2_b"].partition_broadcast(P))):
                sp.dma_start(dst, src).then_inc(w5_in, 16)
            for k in range(4):
                sp.dma_start(in_b[:, k:k + 1], col(t["L1_attn_in_b"], k)).then_inc(w5_in, 16)
                sp.dma_start(f1_b[:, k:k + 1], col(t["L1_attn_f1_b"], k)).then_inc(w5_in, 16)
            for k in range(KD):
                sp.dma_start(taps[:, k, :], t["L1_attn_dw_W"][k * P:(k + 1) * P].rearrange("p o q -> p (o q)")).then_inc(w5_in, 16)
                for dst, src in ((tap_b, "dw_b"), (dt_b, "dt_b"), (b_b, "b_b"), (c_b, "c_b"), (a_neg, "a_log"), (skip, "d_skip")):
                    sp.dma_start(dst[:, k:k + 1], col(t["L1_attn_" + src], k)).then_inc(w5_in, 16)
            sp.wait_ge(const5, 1)
            for q in range(E):
                sp.dma_start(xe[q * CAP:(q + 1) * CAP].rearrange("(p r) n -> p (r n)", p=P), zeros).then_inc(zero_in, 16)
            sp.dma_start(ye[E * CAP:E * CAP + 1], zeros[0:1, 0:D]).then_inc(zero_in, 16)

            with sp.Fori(0, B - 1) as i:
                for r in range(2):
                    sp.wait_ge(pre_pe, now(6, 2 * i + r, 1))
                    sp.wait_ge(pool_pre, now(5, 2 * i + r, 2))
                    load3(i + 1, r)
                for r in range(2):
                    store3(2 * i + r, r)
            def load4(i, r):
                sp.dma_start(xr[r], x_mid_b[bass.ds(2 * i + r, 1)].rearrange("o p j n -> p (o j) n")).then_inc(x5_in[r], 16)

            for r in range(2):
                sp.wait_ge(x_out[r], 16 * 2)
            load4(0, 0)
            for r in range(2):
                store3(2 * (B - 1) + r, r)
            for r in range(2):
                sp.wait_ge(x_out[r], 16 * (B + 1))
            sp.wait_ge(zero_in, 16 * (E + 1))
            meet(sp, 3)

            def keep(i, r):
                sp.wait_ge(dve_b, now(11, 2 * i + r, 10))
                sp.dma_start(x_all[:, bass.ds(ST * (2 * i + r), ST), :], norm_b).then_inc(x3_out, 16)

            load4(0, 1)
            for i in range(B // 2 - 1):
                for r in range(2):
                    sp.wait_ge(pool_b, now(4, 2 * i + r, 3))
                    load4(i + 1, r)
                    keep(i, r)
            for r in range(2):
                keep(B // 2 - 1, r)
            sp.wait_ge(x3_out, 16 * (B + 1))
            meet(sp, 4)

            ew = lambda w, e, k: w[bass.ds(e, 1)].rearrange("o (k p) n -> p (o k) n", p=P)

            def load_w(e, r):
                sp.dma_start(we[r], ew(t["L1_ffn_W"], e, KD)).then_inc(e_in[r], 16)
                sp.dma_start(ve[r], ew(t["L1_ffn_V"], e, KD)).then_inc(e_in[r], 16)
                sp.dma_start(woe[r], ew(t["L1_ffn_W_out"], e, 4)).then_inc(e_in[r], 16)

            def load_x(e, r):
                sp.dma_start(xe_s[r], xe[bass.ds(CAP * e, CAP)].rearrange("(j p) n -> p j n", p=P)).then_inc(e_in[r], 16)

            def store_y(e, r):
                sp.wait_ge(act6, now(6, e, 6))
                sp.dma_start(ye[bass.ds(CAP * e, CAP)].rearrange("(j p) n -> p j n", p=P), ye_s[r]).then_inc(y_out[r], 16)

            for r in range(2):
                load_w(r, r)
            sp.wait_ge(sent6, 16 * 2 * TILES)
            for r in range(2):
                load_x(r, r)
            with sp.Fori(0, E // 2 - 1) as i:
                for r in range(2):
                    sp.wait_ge(pe6, now(6, 2 * i + r, 6))
                    load_w(2 * i + (r + 2), r)
                    load_x(2 * i + (r + 2), r)
                    store_y(2 * i + r, r)
            for r in range(2):
                store_y(E - 2 + r, r)
            for c in range(TILES // TPC):
                sp.wait_ge(fin6, 6 * (c + 1))
                sp.dma_start(out_c[c], fin[c % 2]).then_inc(fin_out[c % 2], 16)
            for r in range(2):
                sp.wait_ge(fin_out[r], 16 * (TILES // TPC // 2))
            meet(sp, 5)

        @block.gpsimd
        def _(pool):
            pool.memset(ident, 0.0).then_inc(s_const, 1)
            pool.memset(wc, 0.0).then_inc(s_const, 1)
            pool.memset(half, -0.5).then_inc(s_const, 1)
            pool.wait_ge(s_const, 3)
            pool.affine_select(out=ident, in_=ident, compare_op=ALU.not_equal, fill=1.0, base=0,
                               pattern=[[-1, P]], channel_multiplier=1).then_inc(s_const, 1)
            meet(pool, 1)
            for a in fq + fk:
                pool.memset(a, 0.0).then_inc(rows_cleared, 1)
            pool.memset(fold, 0.0).then_inc(fold_made, 1)
            for q in range(4):
                pool.wait_ge(fold_made, q + 1)
                pool.affine_select(out=fold, in_=fold, compare_op=ALU.not_equal, fill=1.0, base=-HD * q,
                                   pattern=[[-1, HD]], channel_multiplier=1).then_inc(fold_made, 1)
            meet(pool, 2)

            pool.memset(ones, 1.0).then_inc(prep_c, 1)
            pool.memset(last_row, 0.0).then_inc(prep_c, 1)
            pool.memset(zeros, 0.0).then_inc(const5, 1)
            pool.wait_ge(prep_c, 2)
            pool.memset(last_row[:, NQ:NQ + 1], 1.0).then_inc(prep_c, 1)
            pool.sem_inc(pool_pre, 5)
            pool.sem_inc(pool_ffn, 1)
            wide = lambda v: v.unsqueeze(1).to_broadcast([P, TPC, D])

            def power(done, out_, in_):
                pool.tensor_tensor(out_[:, 0:TPC], in_[:, 0:TPC], half[:, 0:TPC], ALU.pow).then_inc(done, 1)

            def pre_pool(i, r):
                n = 2 * i + r
                pool.wait_ge(c3_in[r], C3_IN * (i + 1))
                pool.wait_ge(dve_pre, before(23, n, 1))
                pool.tensor_tensor(xbo, xc[r], wide(bo_b), ALU.add).then_inc(pool_pre, 1)
                pool.wait_ge(dve_pre, before(23, n, 19))
                pool.tensor_tensor(xb2, xc[r], wide(be2_b), ALU.add).then_inc(pool_pre, 1)
                for k in (4, 17, 22):
                    pool.wait_ge(dve_pre, now(23, n, k))
                    power(pool_pre, rstd, var)

            def ffn_pool(i, r):
                n = 2 * i + r
                pool.wait_ge(dve_out, now(5, n, 4))
                power(pool_ffn, rstd_f, var_f)

            pre_pool(0, 0)
            with pool.Fori(0, B - 1) as i:
                for r in range(2):
                    pre_pool(i + r, 1 - r)
                    ffn_pool(i, r)
            pre_pool(B - 1, 1)
            for r in range(2):
                ffn_pool(B - 1, r)
            meet(pool, 3)

            pool.memset(xpad[:, :, 0:1], 0.0).then_inc(prep5, 1)
            pool.memset(ones4, 1.0).then_inc(prep5, 1)
            pool.memset(xpad[:, :, S + 1:S + 2], 0.0).then_inc(prep5, 1)
            pool.sem_inc(pool_a, 4)
            pool.sem_inc(pool_f, 1)
            pool.sem_inc(pool_b, 4)
            pool.sem_inc(x3_out, 16)
            pool.memset(ones6, 1.0).then_inc(const6, 1)
            pool.memset(carry, 0.0).then_inc(const6, 1)
            for e in range(E):
                pool.memset(rev[:, :, e], float(E - e)).then_inc(const6, 1)
            pool.wait_ge(const6, E + 2)
            pool.affine_select(out=below, in_=ones6, compare_op=ALU.is_gt, fill=0.0, base=0,
                               pattern=[[1, P]], channel_multiplier=-1).then_inc(const6, 1)
            wide8 = lambda a: a.unsqueeze(1).to_broadcast([P, ST, D])

            def send(b, k):
                pool.wait_ge(idx6, 2 * b + k + 1)
                pool.wait_ge(x3_out, 16 * (b + 2))
                for c in range(ST * b, ST * (b + 1)):
                    pool.indirect_dma_start(out=xe, out_offset=bass.IndirectOffsetOnAxis(ap=idx[k][:, c:c + 1], axis=0),
                                            in_=x_all[:, c, :], in_offset=None,
                                            bounds_check=E * CAP - 1, oob_is_err=False).then_inc(sent6, 16)

            def power8(done, in_, out_):
                pool.tensor_tensor(out_, in_, half[:, 0:ST], ALU.pow).then_inc(done, 1)

            def first_pool(i, r):
                n = 2 * i + r
                pool.wait_ge(dve_f, now(5, n, 3))
                power8(pool_f, var5, rstd5)

            def scan_pool_1(i, r):
                n = 2 * i + r
                pool.wait_ge(act_a, now(15, n, 9))
                pool.wait_ge(dve_a, now(15, n, 6))
                pool.tensor_tensor(v, v, mixed, ALU.mult).then_inc(pool_a, 1)
                pool.wait_ge(x5_in[r], 16 * (i + 1))
                pool.wait_ge(dve_b, before(11, n, 4))
                pool.wait_ge(pool_b, before(4, n, 2))
                pool.tensor_tensor(x2, xr[r], wide8(outb_b), ALU.add).then_inc(pool_a, 1)

            def scan_pool_2(i, r):
                n = 2 * i + r
                for k in range(KD):
                    pool.wait_ge(dve_a, now(15, n, 10 + k))
                    pool.wait_ge(act_a, now(15, n, 14 + k))
                    pool.tensor_tensor(ct[:, k], ct[:, k], state[:, k], ALU.mult).then_inc(pool_a, 1)

            def second_pool_1(i, r):
                n = 2 * i + r
                pool.wait_ge(dve_b, now(11, n, 3))
                power8(pool_b, var_b, rstd_b)
                pool.wait_ge(dve_b, before(11, n, 10))
                pool.tensor_tensor(x3, x2, wide8(f2b_b), ALU.add).then_inc(pool_b, 1)
                pool.wait_ge(pool_b, now(4, n, 2))
                pool.tensor_tensor(x3, x3, xr[r], ALU.add).then_inc(pool_b, 1)

            def second_pool_2(i, r):
                pool.wait_ge(dve_b, now(11, 2 * i + r, 9))
                power8(pool_b, var_b, rstd_b)

            def step4_pool(i, r, scan=True, first=True):
                b = 2 * i + r
                second_pool_1(i, r)
                if b >= 1:
                    send(b - 1, 0)
                if scan:
                    scan_pool_1(i + r, 1 - r)
                if first:
                    first_pool(i + 1, r)
                if scan:
                    scan_pool_2(i + r, 1 - r)
                if b >= 1:
                    send(b - 1, 1)
                second_pool_2(i, r)

            pool.wait_ge(w5_in, W5_IN)
            first_pool(0, 0)
            scan_pool_1(0, 0)
            first_pool(0, 1)
            scan_pool_2(0, 0)
            for i in range(B // 2 - 1):
                for r in range(2):
                    step4_pool(i, r)
            step4_pool(B // 2 - 1, 0, first=False)
            step4_pool(B // 2 - 1, 1, scan=False, first=False)
            meet(pool, 4)

            for k in range(2):
                send(B - 1, k)
            for r in range(2):
                pool.wait_ge(y_out[r], 16 * (E // 2 + 1))

            def fetch(c):
                for s in range(2):
                    for j in range(TPC):
                        q = TPC * c + j
                        pool.indirect_dma_start(out=y_g[s][:, q, :], out_offset=None, in_=ye,
                                                in_offset=bass.IndirectOffsetOnAxis(ap=idx[s][:, q:q + 1], axis=0)).then_inc(got6[c], 16)

            fetch(0)
            for c in range(TILES // TPC):
                if c + 1 < TILES // TPC:
                    fetch(c + 1)
                pool.wait_ge(fin6, 6 * c + 5)
                pool.tensor_tensor(rstd6, var6, half[:, 0:TPC], ALU.pow).then_inc(pow6, 1)
            meet(pool, 5)

        @block.scalar
        def _(act):
            for i in range(2):
                act.dma_start(bcb[:, i * 64:(i + 1) * 64], t["L0_attn_bc2q"].rearrange("h d -> (h d)").partition_broadcast(P)).then_inc(s_w, 16)
            act.wait_ge(s_const, 4)
            for h in range(H):
                act.dma_start(wc[(h % 4) * 32:(h % 4 + 1) * 32, h // 4, h * NQ:(h + 1) * NQ], t["L0_attn_Wc2q"][h]).then_inc(s_w, 16)
            act.wait_ge(s_fscale, 2)

            for sems, per in (((s_feat, s_hi, s_mid), 4), ((s_feat_f, s_hi_f, s_mid_f), 1)):
                for one in sems:
                    act.sem_inc(one, per)
            act.sem_inc(s_xTs, 2)

            def xT_act(i, r):
                n = 2 * i + r
                act.wait_ge(s_xT, now(1, n, 1))
                act.wait_ge(s_proj, before(5, n, 5))
                act.activation(xT[:, 0, :], bank(6), ACT.Copy).then_inc(s_xTs, 1)

            def feat_act(i, r, f):
                n = 2 * i + r
                act.wait_ge(s_proj, now(5, n, 1 + f + 1))
                act.wait_ge(s_rest, before(4, n, f + 1))
                act.activation(feat[:, f, :], bank(2 + f), ACT.Identity, bias=bqk[:, f:f + 1]).then_inc(s_feat, 1)
                if f == 0:
                    act.wait_ge(s_st[r], 96 * (i + 1))
                act.wait_ge(s_feat, now(4, n, f + 1))
                act.activation(planes[r][:, f, 0, :], feat[:, f, :], ACT.Copy,
                               scale=SCORE_SCALE if f < 2 else 1.0).then_inc(s_hi, 1)

            def mid_act(i, r, f):
                n = 2 * i + r
                act.wait_ge(s_rest, now(4, n, f + 1))
                act.activation(planes[r][:, f, 1, :], rest[:, f, :], ACT.Copy).then_inc(s_mid, 1)

            def features_act(i, r):
                n = 2 * i + r
                act.wait_ge(s_fT, now(1, n, 1))
                act.wait_ge(s_rest_f, before(1, n, 1))
                act.activation(feat[:, 4, :], bank(1), ACT.Copy, scale=fscale).then_inc(s_feat_f, 1)
                act.wait_ge(s_feat_f, now(1, n, 1))
                act.activation(planes[r][:, 4, 0, :], feat[:, 4, :], ACT.Copy).then_inc(s_hi_f, 1)

            def mid_features_act(i, r):
                act.wait_ge(s_rest_f, now(1, 2 * i + r, 1))
                act.activation(planes[r][:, 4, 1, :], rest[:, 4, :], ACT.Copy).then_inc(s_mid_f, 1)

            def step1_act(i, r, ahead=True):
                nxt = (i + r, 1 - r)
                if ahead:
                    xT_act(*nxt)
                    for f in range(2):
                        feat_act(*nxt, f)
                features_act(i, r)
                if ahead:
                    feat_act(*nxt, 2)
                mid_features_act(i, r)
                if ahead:
                    feat_act(*nxt, 3)
                    for f in range(4):
                        mid_act(*nxt, f)

            xT_act(0, 0)
            act.wait_ge(s_w, 16 * W_DMAS)
            for f in range(4):
                feat_act(0, 0, f)
            for f in range(4):
                mid_act(0, 0, f)
            with act.Fori(0, B - 1) as b:
                for r in range(2):
                    step1_act(b, r)
            step1_act(B - 1, 0)
            step1_act(B - 1, 1, ahead=False)
            meet(act, 1)

            def evac_act(g, k, first):
                act.wait_ge(tr_made, 32 * g + 2 * k + 1)
                if not (first and k < 8):
                    act.wait_ge(pv_made, 4 * g + k // 4 - 1)
                act.activation(pT[k // 4 % 2][:, 0:4, (k % 4) * P:(k % 4 + 1) * P],
                               bank(4).rearrange("p (t n) -> p t n", t=4), ACT.Copy).then_inc(ev_a, 1)

            def keep_sum(g, q, first):
                act.wait_ge(pv_made, 4 * g + q + 1)
                if not (first and q == 0):
                    act.wait_ge(folded, 4 * g + q)
                act.activation(o_sum, bank(6), ACT.Copy).then_inc(o_kept, 1)

            act.wait_ge(flag_made, 3)
            small = act.value_load(flag)

            def sin_act(g, prev=True, scores=True, guard=False):
                for u in range(UNITS + 1):
                    if scores and u < UNITS:
                        act.wait_ge(score_made, 32 * g + u + 1)
                        if guard:
                            act.wait_ge(guarded, 16 * g + u + 1)
                        if u >= 2:
                            act.wait_ge(score_used, 32 * g + u + 1)
                        act.activation(sn[u % 2], bank(2 * (u % 2), 2), ACT.Sin, scale=SIN_SCALE).then_inc(sin_made, 1)
                    if prev and u - 1 in SIN_TURNS:
                        evac_act(g - 1, SIN_TURNS[u - 1], False)
                    if prev and u - 1 in SIN_QUADS and SIN_QUADS[u - 1][1] == 1:
                        keep_sum(g - 1, SIN_QUADS[u - 1][0], False)

            def exp_act(g, first=False):
                for u in range(UNITS):
                    act.wait_ge(score_used, 2 + 32 * g + 16 + u + 1)
                    act.activation(logits[:, u, :], logits[:, u, :], ACT.Exp, scale=-1.0, bias=nmax[:, u:u + 1],
                                   accum_out=rsum[:, u:u + 1]).then_inc(exp_made, 1)
                    if not first and u == OLD_QUAD[1]:
                        keep_sum(g - 1, 3, False)
                    if u + 1 in EXP_TURNS:
                        evac_act(g, EXP_TURNS[u + 1], first)
                    if u == OWN_QUAD[1]:
                        keep_sum(g, 0, first)

            def sines_act(g, prev=True):
                with act.If(small > 0):
                    sin_act(g, prev, guard=True)
                with act.If(small < 1):
                    sin_act(g, prev)

            sines_act(0, prev=False)
            exp_act(0, first=True)
            with act.Fori(1, PAIRS) as g:
                sines_act(g)
                exp_act(g)
            sin_act(PAIRS, scores=False)
            keep_sum(PAIRS - 1, 3, False)
            meet(act, 2)

            act.preload_act_table_set("silu_and_others")
            act.sem_inc(act_pre, 5)
            act.sem_inc(act_silu, 6)
            act.wait_ge(prep_pe, 1)
            act.activation(w1T.rearrange("p k n -> p (k n)"), bank(0, 4), ACT.Copy).then_inc(prep_act, 1)
            act.activation(wqoT[:, :, 0:NQ], bank(4)[:, 0:FK * NQ].rearrange("p (k q) -> p k q", q=NQ), ACT.Copy).then_inc(prep_act, 1)

            def made_act():
                act.wait_ge(prep_pe, 2)
                act.activation(w1m.rearrange("p k n -> p (k n)"), bank(5)[:, 0:2 * NQ], ACT.Copy).then_inc(prep_act, 1)
                act.activation(qm_col[0:NQ], bank(5)[0:NQ, 2 * NQ:2 * NQ + 1], ACT.Copy).then_inc(prep_act, 1)
                act.activation(w2q[0:NQ + 1], bank(6)[0:NQ + 1, 0:D], ACT.Copy).then_inc(prep_act, 1)

            def weight_act(w):
                act.wait_ge(prep_pe, 3 + w)
                act.activation((wgT, wuT, wdT)[w].rearrange("p k n -> p (k n)"), bank(4, 3), ACT.Copy).then_inc(prep_act, 1)

            def pre_act_1(i, r):
                act.wait_ge(pre_pe, now(6, 2 * i + r, 1))
                act.activation(aT.rearrange("p k n -> p (k n)"), bank(0, 2), ACT.Copy).then_inc(act_pre, 1)

            def pre_act_2(i, r):
                act.wait_ge(pre_pe, now(6, 2 * i + r, 3))
                act.activation(x1T.rearrange("p k n -> p (k n)"), bank(0, 2), ACT.Copy).then_inc(act_pre, 1)

            def pre_act_3(i, r):
                act.wait_ge(dve_pre, now(23, 2 * i + r, 7))
                act.activation(th, mid_q, ACT.Tanh).then_inc(act_pre, 1)

            def pre_act_4(i, r):
                act.wait_ge(dve_pre, now(23, 2 * i + r, 12))
                act.activation(cs, turns, ACT.Sin).then_inc(act_pre, 1)

            def pre_act_5(i, r):
                act.wait_ge(pre_pe, now(6, 2 * i + r, 6))
                act.activation(xpT[r].rearrange("p k n -> p (k n)"), bank(2, 2), ACT.Copy).then_inc(act_pre, 1)

            def ffn_act(i, r, a, z):
                n = 2 * i + r
                for m in range(a, z):
                    act.wait_ge(ffn_pe, now(7, n, m + 1))
                    act.wait_ge(h_made, now(6, n, m - 1))
                    act.activation(sg[m % 2], bank(4 + 2 * (m % 2)), ACT.Silu, scale=1.0 / 127.0).then_inc(act_silu, 1)

            def step_act(i, r, ahead=True):
                order = ((pre_act_1, 0, 3), (pre_act_2, 3, 4), (pre_act_3, 4, 5), (pre_act_4, 5, HT), (pre_act_5, HT, HT))
                for part, a, z in order:
                    if ahead:
                        part(i + r, 1 - r)
                    ffn_act(i, r, a, z)

            pre_act_1(0, 0)
            made_act()
            for w, part in enumerate((pre_act_2, pre_act_3, pre_act_4)):
                part(0, 0)
                weight_act(w)
            pre_act_5(0, 0)
            with act.Fori(0, B - 1) as i:
                for r in range(2):
                    step_act(i, r)
            step_act(B - 1, 0)
            step_act(B - 1, 1, ahead=False)
            meet(act, 3)

            act.wait_ge(w5_in, W5_IN)
            act.activation(a_neg, a_neg, ACT.Exp).then_inc(prep5_act, 1)
            act.wait_ge(prep5_act, 1)
            act.activation(a_neg, a_neg, ACT.Copy, scale=-1.0).then_inc(prep5_act, 1)
            act.wait_ge(prep5_pe, 1)
            act.activation(rt_wT, bank(0)[:, 0:KD * E].rearrange("p (k e) -> p k e", e=E), ACT.Copy).then_inc(prep5_act, 1)
            act.wait_ge(prep5_act, 3)
            act.sem_inc(act_a, 15)
            act.sem_inc(act_b, 6)
            flat2 = lambda a: a.rearrange("p k n -> p (k n)")

            def first_act(i, r):
                n = 2 * i + r
                act.wait_ge(pe_a, now(12, n, 1))
                act.activation(flat2(T_a), bank(0, 4), ACT.Copy).then_inc(act_a, 1)
                act.wait_ge(prep5, 3)
                for k in range(KD):
                    act.wait_ge(pe_a, now(12, n, 2 + k))
                    act.activation(xpad[:, k, 1:S + 1], bank(2 * k, 2), ACT.Identity, bias=in_b[:, k:k + 1]).then_inc(act_a, 1)
                for k in range(KD):
                    act.wait_ge(pe_a, now(12, n, 4 + k))
                    act.activation(gate[:, k], bank(2 * k, 2), ACT.Sigmoid, bias=in_b[:, 2 + k:3 + k]).then_inc(act_a, 1)

            def scan_act_1(i, r):
                n = 2 * i + r
                for k in range(KD):
                    act.wait_ge(pe_a, now(12, n, 6 + k))
                    act.activation(z[:, k], bank(2 * k, 2), ACT.Identity, bias=dt_b[:, k:k + 1]).then_inc(act_a, 1)
                for k in range(KD):
                    act.wait_ge(pe_a, now(12, n, 8 + k))
                    act.activation(v[:, k], bank(2 * k, 2), ACT.Tanh, bias=b_b[:, k:k + 1]).then_inc(act_a, 1)

            def steps_act(i, r):
                n = 2 * i + r
                act.preload_act_table_set("natural_log_exp_and_others")
                act.wait_ge(dve_a, now(15, n, 7))
                act.activation(l, l, ACT.Exp).then_inc(act_a, 1)
                act.wait_ge(act_a, now(15, n, 12))
                act.activation(l, l, ACT.Ln, bias=1.0).then_inc(act_a, 1)

            def decay_act(i, r):
                n = 2 * i + r
                act.wait_ge(dve_a, now(15, n, 8))
                for k in range(KD):
                    act.activation(decay[:, k], dt[:, k], ACT.Exp, scale=a_neg[:, k:k + 1]).then_inc(act_a, 1)

            def scan_act_2(i, r):
                n = 2 * i + r
                for k in range(KD):
                    act.wait_ge(pe_a, now(12, n, 10 + k))
                    act.activation(ct[:, k], bank(2 * k, 2), ACT.Tanh, bias=c_b[:, k:k + 1]).then_inc(act_a, 1)

            def turned_act(i, r, k, m):
                act.wait_ge(pe_b, now(8, 2 * i + r, k))
                act.activation(flat2(T_b), bank(4, 4), ACT.Copy).then_inc(act_b, 1)

            def gelu_act(i, r):
                n = 2 * i + r
                for m in range(4):
                    act.wait_ge(pe_b, now(8, n, 2 + m))
                    act.activation(gl[:, m], bank(4 + 2 * (m % 2), 2), ACT.Gelu, bias=f1_b[:, m:m + 1]).then_inc(act_b, 1)

            def step4_act(i, r, scan=True):
                nxt = (i + r, 1 - r)
                if scan:
                    first_act(*nxt)
                turned_act(i, r, 1, 1)
                if scan:
                    scan_act_1(*nxt)
                    scan_act_2(*nxt)
                    steps_act(*nxt)
                gelu_act(i, r)
                if scan:
                    decay_act(*nxt)
                turned_act(i, r, 7, 6)

            first_act(0, 0)
            scan_act_1(0, 0)
            scan_act_2(0, 0)
            steps_act(0, 0)
            decay_act(0, 0)
            for i in range(B // 2 - 1):
                for r in range(2):
                    step4_act(i, r)
            step4_act(B // 2 - 1, 0)
            step4_act(B // 2 - 1, 1, scan=False)
            meet(act, 4)

            act.sem_inc(act6, 6)
            for r in range(2):
                act.sem_inc(y_out[r], 16)
            act.wait_ge(top6, (TOP_A + TOP_B) * (B - 1) + TOP_A)
            act.activation(p2, top2, ACT.Exp).then_inc(exp6, 1)
            act.preload_act_table_set("silu_and_others")
            with act.Fori(0, E // 2) as i:
                for r in range(2):
                    e = 2 * i + r
                    act.wait_ge(pe6, now(6, e, 1))
                    act.wait_ge(pe6, before(6, e, 5))
                    act.activation(XT.rearrange("p k n -> p (k n)"), bank(0, 2), ACT.Copy).then_inc(act6, 1)
                    for m in range(4):
                        act.wait_ge(pe6, now(6, e, 2 + m))
                        act.wait_ge(dve6, now(4, e, m - 1))
                        act.activation(sg6[m % 2], bank(3 + 2 * (m % 2)), ACT.Silu).then_inc(act6, 1)
                    act.wait_ge(pe6, now(6, e, 6))
                    act.wait_ge(y_out[r], 16 * (i + 1))
                    act.activation(ye_s[r].rearrange("p j n -> p (j n)"), bank(6, 2), ACT.Copy).then_inc(act6, 1)
            meet(act, 5)

        @block.vector
        def _(dve):
            dve.memset(fscale[0:64], -FID_SCALE).then_inc(s_fscale, 1)
            dve.memset(fscale[64:128], 1.0).then_inc(s_fscale, 1)
            for one, per in ((s_v, 1), (s_rest, 4), (s_rest_f, 1), (s_lo, 4), (s_lo_f, 1), (s_qkb, 1), (s_sq, 4), (s_qn, 1),
                             (s_rn, 13), (vs_out[0], 64), (vs_out[1], 64), (s_st[0], 96), (s_st[1], 96)):
                dve.sem_inc(one, per)

            def step(done, v):
                def then(ins):
                    v[0] += 1
                    ins.then_inc(done, 1)
                    dve.wait_ge(done, v[0])
                then.count = v
                return then

            def split(n, r, f, hi, mid, done, per, k):
                dve.wait_ge(hi, now(per, n, k))
                dve.wait_ge(mid, before(per, n, k))
                dve.scalar_tensor_tensor(out=rest[:, f, :], in0=feat[:, f, :], scalar=SCORE_SCALE if f < 2 else 1.0,
                                         in1=planes[r][:, f, 0, :], op0=ALU.mult, op1=ALU.subtract).then_inc(done, 1)

            def low(n, r, f, mid, done, per, k):
                dve.wait_ge(mid, now(per, n, k))
                dve.tensor_tensor(planes[r][:, f, 2, :], rest[:, f, :], planes[r][:, f, 1, :],
                                  ALU.subtract).then_inc(done, 1)

            def xT_dve(i, r):
                n = 2 * i + r
                dve.wait_ge(s_xT, now(1, n, 1))
                dve.wait_ge(s_proj, before(5, n, 5))
                dve.tensor_copy(xT[:, 1, :], bank(7)).then_inc(s_xTs, 1)

            def v_dve(i, r):
                dve.wait_ge(s_proj, now(5, 2 * i + r, 1))
                dve.wait_ge(vs_out[r], 64 * (i + 1))
                dve.tensor_tensor(v_out[r], bank(6, 2).rearrange("p (j n) -> p j n", j=TPC),
                                  bvb.unsqueeze(1).to_broadcast([P, TPC, D]), ALU.add).then_inc(s_v, 1)

            def norms_dve(i, r):
                n = 2 * i + r
                dve.wait_ge(s_qq, now(1, n, 1))
                dve.wait_ge(s_fT, before(1, n, 1))
                dve.tensor_tensor(qk, bank(0).rearrange("p (j n) -> p j n", j=TPC),
                                  bcb.unsqueeze(1).to_broadcast([P, TPC, P]), ALU.add).then_inc(s_qkb, 1)
                dve.wait_ge(s_qkb, now(1, n, 1))
                dve.tensor_tensor(qk2, qk, qk, ALU.mult).then_inc(s_sq, 1)
                dve.wait_ge(s_sq, now(4, n, 1))
                dve.tensor_reduce(ss, qk2.rearrange("p j (g q) -> p (j g) q", q=NQ), AX.X, ALU.add).then_inc(s_sq, 1)
                dve.wait_ge(s_sq, now(4, n, 2))
                dve.tensor_scalar(ss, ss, TINY, None, ALU.max).then_inc(s_sq, 1)
                dve.wait_ge(s_sq, now(4, n, 3))
                then = step(s_rn, [now(13, n, 0)])
                then(dve.tensor_scalar(rn.bitcast(I32), ss.bitcast(I32), -0.5, RSQRT_START, ALU.mult, ALU.add))
                for _ in range(4):
                    then(dve.tensor_tensor(rn2, rn, rn, ALU.mult))
                    then(dve.scalar_tensor_tensor(out=rn2, in0=rn2, scalar=-0.5, in1=ss, op0=ALU.mult, op1=ALU.mult))
                    then(dve.scalar_tensor_tensor(out=rn, in0=rn2, scalar=1.5, in1=rn, op0=ALU.add, op1=ALU.mult))
                for at, dst in enumerate((q_norms, k_norms)):
                    part = lambda a: a.rearrange("p (j g) -> p j g", j=TPC)[:, :, at * H:(at + 1) * H]
                    dve.tensor_tensor(dst[:, bass.ds(H * i, H), r * TPC:(r + 1) * TPC].rearrange("p h j -> p j h"),
                                      part(ss), part(rn), ALU.mult).then_inc(norms_made, 1)

            def unit_dve(i, r):
                n = 2 * i + r
                dve.tensor_tensor(qk.rearrange("p j (g q) -> p (j g) q", q=NQ),
                                  qk.rearrange("p j (g q) -> p (j g) q", q=NQ),
                                  rn.unsqueeze(2).to_broadcast([P, TPC * 2 * H, NQ]), ALU.mult).then_inc(s_qn, 1)
                dve.sem_inc(s_sq, 1)

            def step1_dve(i, r, ahead=True):
                nxt = (i + r, 1 - r)
                m = 2 * nxt[0] + nxt[1]
                n = 2 * i + r
                if ahead:
                    xT_dve(*nxt)
                norms_dve(i, r)
                if ahead:
                    v_dve(*nxt)
                unit_dve(i, r)
                if ahead:
                    for f in range(2):
                        split(m, 1 - r, f, s_hi, s_mid, s_rest, 4, f + 1)
                split(n, r, 4, s_hi_f, s_mid_f, s_rest_f, 1, 1)
                if ahead:
                    split(m, 1 - r, 2, s_hi, s_mid, s_rest, 4, 3)
                low(n, r, 4, s_mid_f, s_lo_f, 1, 1)
                if ahead:
                    split(m, 1 - r, 3, s_hi, s_mid, s_rest, 4, 4)
                    for f in range(4):
                        low(m, 1 - r, f, s_mid, s_lo, 4, f + 1)

            xT_dve(0, 0)
            dve.wait_ge(s_w, 16 * W_DMAS)
            v_dve(0, 0)
            for f in range(4):
                split(0, 0, f, s_hi, s_mid, s_rest, 4, f + 1)
            for f in range(4):
                low(0, 0, f, s_mid, s_lo, 4, f + 1)
            with dve.Fori(0, B - 1) as b:
                for r in range(2):
                    step1_dve(b, r)
            step1_dve(B - 1, 0)
            step1_dve(B - 1, 1, ahead=False)
            meet(dve, 1)

            flags = step(flag_made, [0])
            dve.wait_ge(norms_made, 2 * 2 * B)
            flags(dve.tensor_reduce(low_norm, fp(1024, 2 * B * H * ST), AX.X, ALU.min))
            dve.wait_ge(flag_pe, 1)
            flags(dve.tensor_reduce(low_norm[0:1], bank(0)[0:1, 0:P], AX.X, ALU.min))
            flags(dve.tensor_scalar(flag, low_norm[0:1], SMALL_NORM, None, ALU.is_lt))
            small = dve.value_load(flag)
            dve.sem_inc(score_used, 2)

            def evac_dve(g, k, first):
                dve.wait_ge(tr_made, 32 * g + 2 * k + 2)
                if not (first and k < 8):
                    dve.wait_ge(pv_made, 4 * g + k // 4 - 1)
                dve.tensor_copy(pT[k // 4 % 2][:, 4:8, (k % 4) * P:(k % 4 + 1) * P],
                                bank(5).rearrange("p (t n) -> p t n", t=4)).then_inc(ev_d, 1)

            def normalize(g, hh, first):
                dve.wait_ge(folded, 4 * g + 2 * hh + 2)
                dve.wait_ge(rinv_made, g + 1)
                if not first:
                    dve.wait_ge(att_out, 16 * g)
                dve.tensor_tensor(att_s[:, :, hh * HD:(hh + 1) * HD],
                                  bank(7)[:, hh * 256:hh * 256 + 256].rearrange("p (s d) -> p s d", d=HD),
                                  rinv[:, 8 * hh:8 * hh + 8].unsqueeze(2).to_broadcast([P, ST, HD]),
                                  ALU.mult).then_inc(att_made, 1)

            def guard_dve(g, u):
                hh, st = divmod(u, ST)
                if st == 0:
                    dve.wait_ge(norms_in[hh], 32 * (g + 1))
                dve.tensor_scalar(share, key_norm[hh], query_norm[hh][:, st:st + 1], 1.0 / EPS_COS, ALU.mult, ALU.mult).then_inc(share_made, 1)
                dve.wait_ge(share_made, 16 * g + u + 1)
                dve.wait_ge(score_made, 32 * g + u + 1)
                cosines = bank(2 * (u % 2), 2)
                dve.scalar_tensor_tensor(out=cosines, in0=share, scalar=1.0, in1=cosines, op0=ALU.min, op1=ALU.mult).then_inc(guarded, 1)

            def sin_dve(g, prev=True, scores=True, guard=False):
                for u in range(UNITS):
                    if scores:
                        if guard:
                            guard_dve(g, u)
                        dve.wait_ge(sin_made, 16 * g + u + 1)
                        if prev:
                            dve.wait_ge(tr_made, 32 * g - 32 + 2 * u + 2)
                        dve.scalar_tensor_tensor(out=logits[:, u, :], in0=sn[u % 2], scalar=10.0,
                                                 in1=bank(2 * (u % 2), 2), op0=ALU.add, op1=ALU.mult).then_inc(score_used, 1)
                    if prev and u == 1:
                        dve.wait_ge(exp_made, 16 * g)
                        dve.reciprocal(rinv, rsum).then_inc(rinv_made, 1)
                    if prev and u in SIN_TURNS:
                        evac_dve(g - 1, SIN_TURNS[u], False)
                    if prev and u == 8:
                        normalize(g - 1, 0, False)

            def exp_dve(g, first=False):
                for u in range(UNITS):
                    dve.wait_ge(score_made, 32 * g + 16 + u + 1)
                    dve.wait_ge(score_used, 2 + 32 * g + u + 1)
                    dve.sem_inc(passed, 1)
                    dve.tensor_tensor_reduce(out=logits[:, u, :], in0=logits[:, u, :], in1=bank(2 * (u % 2), 2),
                                             scale=1.0, scalar=3.0e38, op0=ALU.add, op1=ALU.min,
                                             accum_out=nmax[:, u:u + 1]).then_inc(score_used, 1)
                    if u in EXP_TURNS:
                        evac_dve(g, EXP_TURNS[u], first)
                    if not first and u == OLD_FOLD + 2:
                        normalize(g - 1, 1, False)

            def sines_dve(g, prev=True):
                with dve.If(small > 0):
                    sin_dve(g, prev, guard=True)
                with dve.If(small < 1):
                    sin_dve(g, prev)

            sines_dve(0, prev=False)
            exp_dve(0, first=True)
            with dve.Fori(1, PAIRS) as g:
                sines_dve(g)
                exp_dve(g)
            sin_dve(PAIRS, scores=False)
            normalize(PAIRS - 1, 1, False)
            meet(dve, 2)

            dve.sem_inc(dve_pre, 23)
            dve.sem_inc(h_made, 6)
            dve.sem_inc(dve_out, 5)
            for r in range(2):
                dve.sem_inc(x_out[r], 16)
            dve.wait_ge(w3_in, W3_IN)
            for w in range(3):
                dve.tensor_copy(floats[w], ints[:, w * HT * D:(w + 1) * HT * D]).then_inc(prep_dve, 1)

            def scaled_normal(then, src, dst, gain, plus, got, v, st, mo, va, rs, tiles_, before_write=None):
                for j in range(tiles_):
                    last = dve.bn_stats(st[:, j, :], src[:, j, :])
                then(last)
                dve.sem_inc(passed, 1)
                for j in range(tiles_):
                    last = dve.bn_aggr(mo[:, j, :], st[:, j, :])
                then(last)
                then(dve.tensor_scalar(va[:, 0:tiles_], mo[:, 0:tiles_, 1], LN_EPS, None, ALU.add))
                if before_write:
                    before_write()
                for j in range(tiles_):
                    last = dve.scalar_tensor_tensor(out=dst[:, j, :], in0=src[:, j, :], scalar=mo[:, j, 0:1], in1=gain,
                                                    op0=ALU.subtract, op1=ALU.mult)
                then(last)
                dve.wait_ge(got, v)
                for j in range(tiles_):
                    last = dve.scalar_tensor_tensor(out=dst[:, j, :], in0=dst[:, j, :], scalar=rs[:, j:j + 1], in1=plus(j),
                                                    op0=ALU.mult, op1=ALU.add)
                then(last)

            def normal(then, src, dst, got, v, st, mo, va, rs, tiles_, before_last=None):
                for j in range(tiles_):
                    last = dve.bn_stats(st[:, j, :], src[:, j, :])
                then(last)
                dve.sem_inc(passed, 1)
                for j in range(tiles_):
                    last = dve.bn_aggr(mo[:, j, :], st[:, j, :])
                then(last)
                then(dve.tensor_scalar(va[:, 0:tiles_], mo[:, 0:tiles_, 1], LN_EPS, None, ALU.add))
                dve.wait_ge(got, v)
                if before_last:
                    before_last()
                for j in range(tiles_):
                    last = dve.tensor_scalar(dst[:, j, :], src[:, j, :], mo[:, j, 0:1], rs[:, j:j + 1], ALU.subtract, ALU.mult)
                then(last)

            flat = lambda a: a.rearrange("p j n -> p (j n)")

            def pre_dve_1(i, r, between=None):
                n = 2 * i + r
                then = step(dve_pre, [now(23, n, 0)])
                dve.wait_ge(pre_pe, now(6, n, 2))
                dve.wait_ge(pool_pre, now(5, n, 1))
                then(dve.tensor_tensor(flat(r1), bank(2, 2), flat(xbo), ALU.add))
                scaled_normal(then, r1, x1, g1_b, lambda j: be1_b, pool_pre, now(5, n, 3), stats, moments, var, rstd, TPC, between)

            def pre_dve_2(i, r):
                n = 2 * i + r
                then = step(dve_pre, [now(23, n, 6)])
                dve.wait_ge(pre_pe, now(6, n, 4))
                then(dve.tensor_scalar(mid_q, bank(2)[0:NQ, :], qm_col[0:NQ], None, ALU.add))
                then(dve.tensor_scalar(turns, mid_q, 0.125, ROUND, ALU.mult, ALU.add))
                then(dve.tensor_scalar(turns, turns, ROUND, -8.0, ALU.subtract, ALU.mult))
                then(dve.tensor_tensor(turns, mid_q, turns, ALU.add))
                then(dve.scalar_tensor_tensor(out=turns, in0=turns, scalar=-1.0, in1=turns, op0=ALU.mult, op1=ALU.max))
                then(dve.tensor_scalar(turns, turns, -PI / 4, PI / 2, ALU.mult, ALU.add))

            def pre_dve_3(i, r):
                n = 2 * i + r
                then = step(dve_pre, [now(23, n, 12)])
                dve.wait_ge(act_pre, now(5, n, 4))
                then(dve.tensor_tensor(qeT[0:NQ], th, cs, ALU.mult))

            def pre_dve_4(i, r):
                n = 2 * i + r
                then = step(dve_pre, [now(23, n, 13)])
                dve.wait_ge(pre_pe, now(6, n, 5))
                then(dve.tensor_tensor(flat(r2), bank(0, 2), flat(x1), ALU.add))
                scaled_normal(then, r2, r3, g2_b, lambda j: xb2[:, j, :], pool_pre, now(5, n, 4), stats, moments, var, rstd, TPC)
                normal(then, r3, xp[r], pool_pre, now(5, n, 5), stats, moments, var, rstd, TPC)

            def ffn_dve(i, r, a, z):
                n = 2 * i + r
                for m in range(a, z):
                    dve.wait_ge(act_silu, now(6, n, m + 1))
                    if m == 0:
                        dve.wait_ge(ffn_pe, before(7, n, 7))
                    dve.scalar_tensor_tensor(out=hT[:, m, :], in0=bank(5 + 2 * (m % 2)), scalar=1.0 / 127.0, in1=sg[m % 2],
                                             op0=ALU.mult, op1=ALU.mult).then_inc(h_made, 1)

            def out_dve(i, r):
                n = 2 * i + r
                then = step(dve_out, [now(5, n, 0)])
                dve.wait_ge(ffn_pe, now(7, n, 7))
                then(dve.scalar_tensor_tensor(out=flat(r4), in0=bank(4, 2), scalar=1.0 / 127.0, in1=flat(xp[r]),
                                              op0=ALU.mult, op1=ALU.add))
                normal(then, r4, xo[r], pool_ffn, now(1, n, 1), stats_f, moments_f, var_f, rstd_f, TPC,
                       lambda: dve.wait_ge(x_out[r], 16 * (i + 1)))

            def step_dve(i, r, ahead=True):
                nxt = (i + r, 1 - r)
                ffn_dve(i, r, 0, 1)
                if ahead:
                    pre_dve_1(*nxt, lambda: ffn_dve(i, r, 1, 2))
                    ffn_dve(i, r, 2, 4)
                    pre_dve_2(*nxt)
                    ffn_dve(i, r, 4, 5)
                    pre_dve_3(*nxt)
                    ffn_dve(i, r, 5, HT)
                    pre_dve_4(*nxt)
                else:
                    ffn_dve(i, r, 1, HT)
                out_dve(i, r)

            dve.memset(qeT[0:NQ + 1], 1.0).then_inc(qe_one, 1)
            dve.wait_ge(qe_one, 1)
            for part in (pre_dve_1, pre_dve_2, pre_dve_3, pre_dve_4):
                part(0, 0)
            with dve.Fori(0, B - 1) as i:
                for r in range(2):
                    step_dve(i, r)
            step_dve(B - 1, 0)
            step_dve(B - 1, 1, ahead=False)
            meet(dve, 3)

            dve.sem_inc(dve_a, 15)
            dve.sem_inc(dve_f, 5)
            dve.sem_inc(dve_b, 11)
            dve.wait_ge(w5_in, W5_IN)

            def first_dve(i, r):
                n = 2 * i + r
                then = step(dve_f, [now(5, n, 0)])
                dve.wait_ge(x5_in[r], 16 * (i + 1))
                scaled_normal(then, xr[r], norm_a, ln1g_b, lambda j: ln1b_b, pool_f, now(1, n, 1), stats5, mom5, var5, rstd5, ST)

            def conv_dve(i, r):
                n = 2 * i + r
                then = step(dve_a, [now(15, n, 0)])
                for k in range(KD):
                    dve.wait_ge(act_a, now(15, n, 2 + k))
                    then(dve.tensor_scalar(mixed[:, k], xpad[:, k, 0:S], taps[:, k, 0:1], tap_b[:, k:k + 1], ALU.mult, ALU.add))
                    for q in (1, 2):
                        then(dve.scalar_tensor_tensor(out=mixed[:, k], in0=xpad[:, k, q:S + q], scalar=taps[:, k, q:q + 1],
                                                      in1=mixed[:, k], op0=ALU.mult, op1=ALU.add))

            def scan_dve(i, r):
                n = 2 * i + r
                then = step(dve_a, [now(15, n, 6)])
                dve.wait_ge(act_a, now(15, n, 7))
                then(dve.scalar_tensor_tensor(out=l, in0=z, scalar=-1.0, in1=z, op0=ALU.mult, op1=ALU.min))
                dve.wait_ge(act_a, now(15, n, 13))
                then(dve.scalar_tensor_tensor(out=dt, in0=z, scalar=0.0, in1=l, op0=ALU.max, op1=ALU.add))
                dve.wait_ge(pool_a, now(4, n, 1))
                then(dve.tensor_tensor(v, v, dt, ALU.mult))

            def states_dve(i, r):
                n = 2 * i + r
                then = step(dve_a, [now(15, n, 9)])
                for k in range(KD):
                    dve.wait_ge(act_a, now(15, n, 15))
                    then(dve.tensor_tensor_scan(state[:, k], decay[:, k], v[:, k], 0.0, ALU.mult, ALU.add))

            def gate_dve(i, r):
                n = 2 * i + r
                then = step(dve_a, [now(15, n, 11)])
                for k in range(KD):
                    dve.wait_ge(pool_a, now(4, n, 3 + k))
                    then(dve.scalar_tensor_tensor(out=ct[:, k], in0=mixed[:, k], scalar=skip[:, k:k + 1], in1=ct[:, k],
                                                  op0=ALU.mult, op1=ALU.add))
                then(dve.tensor_tensor(ct, ct, gate, ALU.mult))

            def mix_dve(i, r):
                n = 2 * i + r
                then = step(dve_a, [now(15, n, 14)])
                dve.wait_ge(pe_a, now(12, n, 12))
                dve.wait_ge(pool_a, now(4, n, 2))
                then(dve.tensor_tensor(flat(x2), bank(0, 4), flat(x2), ALU.add))

            def second_dve_1(i, r):
                n = 2 * i + r
                then = step(dve_b, [now(11, n, 0)])
                scaled_normal(then, x2, norm_b, ln2g_b, lambda j: ln2b_b, pool_b, now(4, n, 1), stats_b, mom_b, var_b, rstd_b, ST,
                       lambda: (dve.wait_ge(pe_b, before(8, n, 7)), dve.wait_ge(x3_out, 16 * (n + 1))))

            def second_dve_2(i, r):
                n = 2 * i + r
                then = step(dve_b, [now(11, n, 5)])
                dve.wait_ge(pe_b, now(8, n, 6))
                dve.wait_ge(pool_b, now(4, n, 3))
                then(dve.tensor_tensor(flat(x3), bank(4, 4), flat(x3), ALU.add))
                normal(then, x3, norm_b, pool_b, now(4, n, 4), stats_b, mom_b, var_b, rstd_b, ST)

            def logits_dve(i, r):
                n = 2 * i + r
                dve.wait_ge(pe_b, now(8, n, 8))
                dve.tensor_copy(lg_all[:, bass.ds(ST * n, ST), :],
                                bank(4)[:, 0:ST * E].rearrange("p (j e) -> p j e", e=E)).then_inc(dve_b, 1)

            def top_first(b):
                top = step(top6, [(TOP_A + TOP_B) * b])
                at = slice(ST * b, ST * (b + 1))
                over_e = lambda a: a[:, at].unsqueeze(2).to_broadcast([P, ST, E])
                dve.wait_ge(dve_b, now(11, b, 11))
                for best, s, mask, src in ((top1, s1, mask1, lg_all[:, at]), (top2, s2, mask2, rest6)):
                    top(dve.tensor_reduce(best[:, at], src, AX.X, ALU.max))
                    top(dve.tensor_tensor(eq, src, over_e(best), ALU.is_equal))
                    top(dve.tensor_tensor(eq, eq, rev[:, at], ALU.mult))
                    top(dve.tensor_reduce(s[:, at], eq, AX.X, ALU.max))
                    top(dve.tensor_tensor(mask[:, at], rev[:, at], over_e(s), ALU.is_equal))
                    if mask is mask1:
                        top(dve.scalar_tensor_tensor(out=rest6, in0=mask[:, at], scalar=-3.0e38, in1=src,
                                                     op0=ALU.mult, op1=ALU.add))
                top(dve.tensor_tensor(both[:, at], mask1[:, at], mask2[:, at], ALU.add))
                top(dve.tensor_tensor(top2[:, at], top2[:, at], top1[:, at], ALU.subtract))
                assert top.count[0] == (TOP_A + TOP_B) * b + TOP_A

            def top_second(b):
                top = step(top6, [(TOP_A + TOP_B) * b + TOP_A])
                at = slice(ST * b, ST * (b + 1))
                counts = lambda q: bank(q)[:, 0:ST * E].rearrange("p (t e) -> p t e", e=E)
                dve.wait_ge(count_pe, b + 1)
                top(dve.tensor_tensor(pos, counts(0), carry[:, b:b + 1, :].to_broadcast([P, ST, E]), ALU.add))
                top(dve.tensor_copy(tot, counts(1)))
                for e in range(E):
                    last = dve.tensor_tensor_scan(eq[:, :, e], ones6[:, 0:ST], tot[:, :, e], 0.0, ALU.mult, ALU.add)
                top(last)
                top(dve.tensor_tensor(carry[:, b + 1:b + 2, :], carry[:, b:b + 1, :], eq[:, ST - 1:ST, :], ALU.add))
                top(dve.tensor_tensor(eq, eq, tot, ALU.subtract))
                top(dve.tensor_tensor(pos, pos, eq, ALU.add))
                for k, (s, mask) in enumerate(((s1, mask1), (s2, mask2))):
                    top(dve.tensor_tensor(eq, pos, mask[:, at], ALU.mult))
                    top(dve.tensor_reduce(slot[:, at], eq, AX.X, ALU.add))
                    top(dve.tensor_scalar(fits[:, at], slot[:, at], float(CAP), None, ALU.is_lt))
                    top(dve.scalar_tensor_tensor(out=slot[:, at], in0=s[:, at], scalar=-float(CAP), in1=slot[:, at], op0=ALU.mult, op1=ALU.add))
                    top(dve.tensor_tensor(slot[:, at], slot[:, at], fits[:, at], ALU.mult))
                    dve.tensor_scalar(idx[k][:, at], slot[:, at], float(E * CAP), None, ALU.add).then_inc(idx6, 1)
                assert top.count[0] == (TOP_A + TOP_B) * (b + 1)

            def step4_dve(i, r, scan=True, first=True):
                nxt = (i + r, 1 - r)
                b = 2 * i + r
                second_dve_1(i, r)
                if b >= 1:
                    top_first(b - 1)
                if scan:
                    conv_dve(*nxt)
                if b >= 1:
                    top_second(b - 1)
                if scan:
                    scan_dve(*nxt)
                if first:
                    first_dve(i + 1, r)
                if scan:
                    states_dve(*nxt)
                    gate_dve(*nxt)
                second_dve_2(i, r)
                if scan:
                    mix_dve(*nxt)
                logits_dve(i, r)

            first_dve(0, 0)
            dve.wait_ge(const6, E + 3)
            conv_dve(0, 0)
            scan_dve(0, 0)
            first_dve(0, 1)
            states_dve(0, 0)
            gate_dve(0, 0)
            mix_dve(0, 0)
            for i in range(B // 2 - 1):
                for r in range(2):
                    step4_dve(i, r)
            step4_dve(B // 2 - 1, 0, first=False)
            step4_dve(B // 2 - 1, 1, scan=False, first=False)
            meet(dve, 4)

            top_first(B - 1)
            top_second(B - 1)
            top = step(top6, [(TOP_A + TOP_B) * B])
            dve.wait_ge(exp6, 1)
            top(dve.tensor_scalar(p1, p2, 1.0, None, ALU.add))
            top(dve.reciprocal(p1, p1))
            top(dve.tensor_tensor(p2, p2, p1, ALU.mult))
            dve.sem_inc(dve6, 4)
            with dve.Fori(0, E // 2) as i:
                for r in range(2):
                    e = 2 * i + r
                    for m in range(4):
                        dve.wait_ge(act6, now(6, e, 2 + m))
                        if m == 0:
                            dve.wait_ge(pe6, before(6, e, 6))
                        dve.tensor_tensor(h6[:, m], bank(2 + 2 * (m % 2)), sg6[m % 2], ALU.mult).then_inc(dve6, 1)
            for c in range(TILES // TPC):
                r = c % 2
                then = step(fin6, [6 * c])
                dve.wait_ge(got6[c], 16 * 2 * TPC)
                for j in range(TPC):
                    q = TPC * c + j
                    last = dve.scalar_tensor_tensor(out=acc[r][:, j, :], in0=y_g[0][:, q, :], scalar=p1[:, q:q + 1],
                                                    in1=x_all[:, q, :], op0=ALU.mult, op1=ALU.add)
                then(last)
                for j in range(TPC):
                    q = TPC * c + j
                    last = dve.scalar_tensor_tensor(out=acc[r][:, j, :], in0=y_g[1][:, q, :], scalar=p2[:, q:q + 1],
                                                    in1=acc[r][:, j, :], op0=ALU.mult, op1=ALU.add)
                then(last)
                normal(then, acc[r], fin[r], pow6, c + 1, stats6, mom6, var6, rstd6, TPC,
                       (lambda: dve.wait_ge(fin_out[r], 16 * (c // 2))) if c >= 2 else None)
            meet(dve, 5)

        @block.tensor
        def _(pe):
            pe.wait_ge(s_const, 4)

            for one, per in ((s_xT, 1), (s_proj, 5), (s_qq, 1), (s_fT, 1)):
                pe.sem_inc(one, per)

            def xT_pe(i, r):
                n = 2 * i + r
                pe.wait_ge(s_x[r], 16 * (i + 1))
                pe.wait_ge(s_v, before(1, n, 1))
                for k in range(KD):
                    for j in range(TPC):
                        last = pe.transpose(bank(6 + k)[:, j * P:(j + 1) * P], xin[r][:, j, k * P:(k + 1) * P], ident)
                last.then_inc(s_xT, 1)

            def values_pe(i, r):
                n = 2 * i + r
                pe.wait_ge(s_xTs, now(2, n, 2))
                for j in range(TPC):
                    for k in range(KD):
                        last = pe.matmul(bank(6, 2)[:, j * D:(j + 1) * D], xT[:, k, j * P:(j + 1) * P], wv[:, k, :],
                                         start=(k == 0), stop=(k == 1))
                last.then_inc(s_proj, 1)

            def project_pe(i, r, f):
                n = 2 * i + r
                pe.wait_ge(s_feat, before(4, n, f + 1))
                c = (f % 2) * P
                for k in range(KD):
                    last = pe.matmul(bank(2 + f), (wq if f < 2 else wk)[:, k, c:c + P], xT[:, k, :], start=(k == 0), stop=(k == 1))
                last.then_inc(s_proj, 1)

            def features_pe(i, r):
                n = 2 * i + r
                pe.wait_ge(s_feat, now(4, n, 4))
                pe.wait_ge(s_qkb, before(1, n, 1))
                for j in range(TPC):
                    for w in range(2):
                        for k in range(KD):
                            last = pe.matmul(bank(0)[:, j * P + w * 64:j * P + w * 64 + 64],
                                             feat[:, 2 * w + k, j * P:(j + 1) * P], wc[:, k, :],
                                             start=(k == 0), stop=(k == 1))
                last.then_inc(s_qq, 1)

            def turn_features_pe(i, r):
                n = 2 * i + r
                pe.wait_ge(s_qn, now(1, n, 1))
                pe.wait_ge(s_feat_f, before(1, n, 1))
                for j in range(TPC):
                    last = pe.transpose(bank(1)[:, j * P:(j + 1) * P], qk[:, j, :], ident)
                last.then_inc(s_fT, 1)

            def step1_pe(i, r, ahead=True):
                nxt = (i + r, 1 - r)
                if ahead:
                    xT_pe(*nxt)
                features_pe(i, r)
                if ahead:
                    values_pe(*nxt)
                    for f in range(2):
                        project_pe(*nxt, f)
                turn_features_pe(i, r)
                if ahead:
                    for f in range(2, 4):
                        project_pe(*nxt, f)

            xT_pe(0, 0)
            pe.wait_ge(s_w, 16 * W_DMAS)
            values_pe(0, 0)
            for f in range(4):
                project_pe(0, 0, f)
            with pe.Fori(0, B - 1) as b:
                for r in range(2):
                    step1_pe(b, r)
            step1_pe(B - 1, 0)
            step1_pe(B - 1, 1, ahead=False)
            meet(pe, 1)

            pe.wait_ge(flag_made, 1)
            pe.transpose(bank(0)[0:1, 0:P], low_norm, ident).then_inc(flag_pe, 1)
            pe.wait_ge(fold_made, 5)

            def turn(g, k):
                pe.wait_ge(exp_made, 16 * g + k + 1)
                for part, ev in ((0, ev_a), (1, ev_d)):
                    pe.wait_ge(ev, 16 * g + k)
                    for j in range(4):
                        c = (4 * part + j) * P
                        last = pe.transpose(bank(4 + part)[:, j * P:(j + 1) * P], logits[:, k, c:c + P], ident)
                    last.then_inc(tr_made, 1)

            def quad(g, q, part, first=False):
                if part == 0:
                    pe.wait_ge(ev_a, 16 * g + 4 * q + 4)
                    pe.wait_ge(ev_d, 16 * g + 4 * q + 4)
                    if q == 0:
                        pe.wait_ge(v_in, 16 * g + 16)
                    if not (first and q == 0):
                        pe.wait_ge(o_kept, 4 * g + q)
                for tt in range(4 * part, 4 * part + 4):
                    j = tt % 4
                    last = pe.matmul(bank(6)[HD * j:HD * (j + 1), :], v_pair[:, tt, HD * (q // 2):HD * (q // 2 + 1)],
                                     pT[q % 2][:, tt, :], start=(tt < 4), stop=(tt >= 4))
                if part == 1:
                    last.then_inc(pv_made, 1)

            def combine(g, q, first=False):
                pe.wait_ge(o_kept, 4 * g + q + 1)
                if not first:
                    pe.wait_ge(att_made, 2 * g - 1 + q // 2)
                for j in range(4):
                    u = 4 * q + j
                    last = pe.matmul(bank(7)[:, u * HD:(u + 1) * HD], o_sum[:, j * P:(j + 1) * P], fold, start=True, stop=True)
                last.then_inc(folded, 1)

            def sin_pe(g, prev=True, scores=True, second=False):
                for u in range(UNITS):
                    hh, st = divmod(u, ST)
                    if scores:
                        if st == 0:
                            pe.wait_ge(f_in[hh], F_IN * (g + 1))
                        pe.wait_ge(score_used, 32 * g + u + 1)
                        for c in range(2):
                            last = pe.matmul(bank(2 * (u % 2) + c), fq[hh][:, st * P:(st + 1) * P],
                                             fk[hh][:, c * 512:(c + 1) * 512], start=True, stop=True)
                        last.then_inc(score_made, 1)
                    if prev:
                        if u in SIN_TURNS:
                            turn(g - 1, SIN_TURNS[u])
                        if u in SIN_QUADS:
                            quad(g - 1, *SIN_QUADS[u])
                        if u in SIN_FOLDS:
                            combine(g - 1, SIN_FOLDS[u], second)

            def exp_pe(g, first=False, second=False):
                for u in range(UNITS):
                    hh, st = divmod(u, ST)
                    if st == 0:
                        pe.wait_ge(c_in[hh], C_IN * (g + 1))
                    pe.wait_ge(score_used, 32 * g + 16 + u + 1)
                    for a in range(2):
                        for c in range(2):
                            last = pe.matmul(bank(2 * (u % 2) + c), qs[hh][:, a, st * P:(st + 1) * P],
                                             ks[hh][:, a, c * 512:(c + 1) * 512], start=(a == 0), stop=(a == 1))
                    last.then_inc(score_made, 1)
                    if not first and u in OLD_QUAD:
                        quad(g - 1, 3, OLD_QUAD.index(u))
                    if not first and u == OLD_FOLD:
                        combine(g - 1, 3, second)
                    if u in EXP_TURNS:
                        turn(g, EXP_TURNS[u])
                    if u in OWN_QUAD:
                        quad(g, 0, OWN_QUAD.index(u), first)
                    if u == OWN_FOLD:
                        combine(g, 0, first)

            sin_pe(0, prev=False)
            exp_pe(0, first=True)
            sin_pe(1, second=True)
            exp_pe(1, second=True)
            with pe.Fori(2, PAIRS) as g:
                sin_pe(g)
                exp_pe(g)
            sin_pe(PAIRS, scores=False)
            for part in range(2):
                quad(PAIRS - 1, 3, part)
            combine(PAIRS - 1, 3)
            meet(pe, 2)

            pe.sem_inc(pre_pe, 6)
            pe.sem_inc(ffn_pe, 7)
            pe.wait_ge(w3_in, W3_IN)
            pe.wait_ge(prep_c, 3)
            for k in range(FK):
                for m in range(KD):
                    pe.transpose(bank(k // 2)[:, (k % 2) * D + m * P:(k % 2) * D + (m + 1) * P], w1[:, m, k * P:(k + 1) * P], ident)
            for k in range(FK):
                last = pe.transpose(bank(4)[:, k * NQ:(k + 1) * NQ], wqo[0:NQ, k * P:(k + 1) * P], ident[0:NQ, 0:NQ])
            last.then_inc(prep_pe, 1)
            def made_pe():
                pe.wait_ge(prep_act, 2)
                for m in range(KD):
                    for k in range(FK):
                        pe.matmul(bank(5)[:, m * NQ:(m + 1) * NQ], w1T[:, k, m * P:(m + 1) * P], wm[:, k, :], start=(k == 0), stop=(k == FK - 1))
                for k in range(FK):
                    pe.matmul(bank(5)[0:NQ, 2 * NQ:2 * NQ + 1], wm[:, k, :], b1c[:, k:k + 1], start=(k == 0), stop=False)
                pe.matmul(bank(5)[0:NQ, 2 * NQ:2 * NQ + 1], bm[0:1], ones[0:1, 0:1], start=False, stop=True)
                for k in range(FK):
                    pe.matmul(bank(6)[0:NQ + 1, 0:D], wqoT[:, k, :], w2[:, k, :], start=(k == 0), stop=False)
                pe.matmul(bank(6)[0:NQ + 1, 0:D], last_row[0:1], b2[0:1], start=False, stop=True).then_inc(prep_pe, 1)

            def weight_pe(w):
                pe.wait_ge(prep_dve, w + 1)
                pe.wait_ge(prep_act, 5 + w)
                f = floats[w]
                for a in range(12):
                    if w < 2:
                        k, m = divmod(a, HT)
                        src = tiles(f)[:, m, k * P:(k + 1) * P]
                    else:
                        k, m = divmod(a, KD)
                        src = f.rearrange("p (k n) -> p k n", k=KD)[:, m, k * P:(k + 1) * P]
                    last = pe.transpose(bank(4, 3)[:, a * P:(a + 1) * P], src, ident)
                last.then_inc(prep_pe, 1)

            def flip(dst, src, done):
                for k in range(KD):
                    for j in range(TPC):
                        last = pe.transpose(dst[:, k * CH + j * P:k * CH + (j + 1) * P], src[:, j, k * P:(k + 1) * P], ident)
                last.then_inc(done, 1)

            def pre_pe_1(i, r):
                n = 2 * i + r
                pe.wait_ge(c3_in[r], C3_IN * (i + 1))
                pe.wait_ge(dve_pre, before(23, n, 14))
                flip(bank(0, 2), attc[r], pre_pe)

            def pre_pe_2(i, r):
                pe.wait_ge(act_pre, now(5, 2 * i + r, 1))
                for j in range(TPC):
                    for k in range(KD):
                        last = pe.matmul(bank(2, 2)[:, j * D:(j + 1) * D], aT[:, k, j * P:(j + 1) * P], wo[:, k, :],
                                         start=(k == 0), stop=(k == KD - 1))
                last.then_inc(pre_pe, 1)

            def pre_pe_3(i, r):
                pe.wait_ge(dve_pre, now(23, 2 * i + r, 6))
                flip(bank(0, 2), x1, pre_pe)

            def pre_pe_4(i, r):
                pe.wait_ge(act_pre, now(5, 2 * i + r, 2))
                for k in range(KD):
                    last = pe.matmul(bank(2)[0:NQ, :], w1m[:, k, :], x1T[:, k, :], start=(k == 0), stop=(k == KD - 1))
                last.then_inc(pre_pe, 1)

            def pre_pe_5(i, r):
                n = 2 * i + r
                pe.wait_ge(dve_pre, now(23, n, 13))
                for j in range(TPC):
                    last = pe.matmul(bank(0, 2)[:, j * D:(j + 1) * D], qeT[0:NQ + 1, j * P:(j + 1) * P], w2q[0:NQ + 1, :],
                                     start=True, stop=True)
                last.then_inc(pre_pe, 1)

            def pre_pe_6(i, r):
                pe.wait_ge(dve_pre, now(23, 2 * i + r, 23))
                flip(bank(2, 2), xp[r], pre_pe)

            def ffn_up(i, r, a, z):
                n = 2 * i + r
                if a == 0:
                    pe.wait_ge(act_pre, now(5, n, 5))
                    pe.wait_ge(dve_out, before(5, n, 1))
                for m in range(a, z):
                    pe.wait_ge(h_made, now(6, n, m - 1))
                    for w, at in ((wgT, 4), (wuT, 5)):
                        for k in range(KD):
                            last = pe.matmul(bank(at + 2 * (m % 2)), w[:, k, m * P:(m + 1) * P], xpT[r][:, k, :],
                                             start=(k == 0), stop=(k == KD - 1))
                    last.then_inc(ffn_pe, 1)

            def ffn_down(i, r, a, z):
                n = 2 * i + r
                if a == 0:
                    pe.wait_ge(h_made, now(6, n, 6))
                for j in range(a, z):
                    for m in range(HT):
                        last = pe.matmul(bank(4, 2)[:, j * D:(j + 1) * D], hT[:, m, j * P:(j + 1) * P], wdT[:, m, :],
                                         start=(m == 0), stop=(m == HT - 1))
                if z == TPC:
                    last.then_inc(ffn_pe, 1)

            def step_pe(i, r, ahead=True):
                nxt = (i + r, 1 - r)
                order = ((pre_pe_1, 0, 1), (pre_pe_2, 1, 3), (pre_pe_3, 3, 4), (pre_pe_4, 4, HT))
                for part, a, z in order:
                    if ahead:
                        part(*nxt)
                    ffn_up(i, r, a, z)
                if ahead:
                    pre_pe_5(*nxt)
                ffn_down(i, r, 0, TPC)
                if ahead:
                    pre_pe_6(*nxt)

            pe.wait_ge(prep_act, 2)
            pre_pe_1(0, 0)
            pre_pe_2(0, 0)
            made_pe()
            pre_pe_3(0, 0)
            weight_pe(0)
            pre_pe_4(0, 0)
            weight_pe(1)
            weight_pe(2)
            pre_pe_5(0, 0)
            pre_pe_6(0, 0)
            pe.wait_ge(prep_act, 8)
            with pe.Fori(0, B - 1) as i:
                for r in range(2):
                    step_pe(i, r)
            step_pe(B - 1, 0)
            step_pe(B - 1, 1, ahead=False)
            meet(pe, 3)

            pe.wait_ge(w5_in, W5_IN)
            for k in range(KD):
                last = pe.transpose(bank(0)[:, k * E:(k + 1) * E], rt_w[0:E, k * P:(k + 1) * P], ident[0:E, 0:E])
            last.then_inc(prep5_pe, 1)
            pe.wait_ge(prep5_act, 3)
            pe.wait_ge(prep5, 3)
            pe.sem_inc(pe_a, 12)
            pe.sem_inc(pe_b, 8)

            def flip8(at, src, done):
                for k in range(KD):
                    for j in range(ST):
                        last = pe.transpose(bank(at, 4)[:, k * S + j * P:k * S + (j + 1) * P], src[:, j, k * P:(k + 1) * P], ident)
                last.then_inc(done, 1)

            def project(at, w, m, src, done):
                for c in range(2):
                    for k in range(KD):
                        last = pe.matmul(bank(at + c), w[:, k, m * P:(m + 1) * P], src[:, k, c * CH:(c + 1) * CH],
                                         start=(k == 0), stop=(k == KD - 1))
                last.then_inc(done, 1)

            def first_pe(i, r):
                n = 2 * i + r
                pe.wait_ge(dve_f, now(5, n, 5))
                pe.wait_ge(dve_a, before(15, n, 15))
                flip8(0, norm_a, pe_a)
                pe.wait_ge(act_a, now(15, n, 1))
                project(0, in_w, 0, T_a, pe_a)
                project(2, in_w, 1, T_a, pe_a)
                for m in range(KD):
                    pe.wait_ge(act_a, now(15, n, 2 + m))
                    project(2 * m, in_w, 2 + m, T_a, pe_a)

            def scan_pe_1(i, r):
                n = 2 * i + r
                pe.wait_ge(dve_a, now(15, n, 6))
                for m in range(KD):
                    pe.wait_ge(act_a, now(15, n, 4 + m))
                    project(2 * m, dt_w, m, mixed, pe_a)
                for m in range(KD):
                    pe.wait_ge(act_a, now(15, n, 6 + m))
                    project(2 * m, b_w, m, mixed, pe_a)

            def scan_pe_2(i, r):
                n = 2 * i + r
                for m in range(KD):
                    pe.wait_ge(act_a, now(15, n, 8 + m))
                    project(2 * m, c_w, m, mixed, pe_a)

            def mix_pe(i, r):
                n = 2 * i + r
                pe.wait_ge(act_a, now(15, n, 15))
                pe.wait_ge(dve_a, now(15, n, 14))
                for j in range(ST):
                    for k in range(KD):
                        last = pe.matmul(bank(0, 4)[:, j * D:(j + 1) * D], ct[:, k, j * P:(j + 1) * P], out_w[:, k, :],
                                         start=(k == 0), stop=(k == KD - 1))
                last.then_inc(pe_a, 1)

            def second_pe(i, r):
                n = 2 * i + r
                pe.wait_ge(dve_b, now(11, n, 5))
                pe.wait_ge(dve_b, before(11, n, 11))
                flip8(4, norm_b, pe_b)

            def up_pe(i, r):
                n = 2 * i + r
                pe.wait_ge(act_b, now(6, n, 1))
                for m in range(4):
                    if m >= 2:
                        pe.wait_ge(act_b, now(6, n, m))
                    project(4 + 2 * (m % 2), f1_w, m, T_b, pe_b)

            def down_pe(i, r):
                n = 2 * i + r
                pe.wait_ge(act_b, now(6, n, 5))
                for j in range(ST):
                    for m in range(4):
                        last = pe.matmul(bank(4, 4)[:, j * D:(j + 1) * D], gl[:, m, j * P:(j + 1) * P], f2_w[:, m, :],
                                         start=(m == 0), stop=(m == 3))
                last.then_inc(pe_b, 1)

            def turn_pe(i, r):
                n = 2 * i + r
                pe.wait_ge(dve_b, now(11, n, 10))
                flip8(4, norm_b, pe_b)

            def logits_pe(i, r):
                n = 2 * i + r
                pe.wait_ge(act_b, now(6, n, 6))
                for j in range(ST):
                    q = bank(4)[:, j * E:(j + 1) * E]
                    for k in range(KD):
                        pe.matmul(q, T_b[:, k, j * P:(j + 1) * P], rt_wT[:, k, :], start=(k == 0), stop=False)
                    last = pe.matmul(q, ones4[0:1], rt_b[0:1], start=False, stop=True)
                last.then_inc(pe_b, 1)

            def count(b):
                pe.wait_ge(top6, (TOP_A + TOP_B) * b + TOP_A)
                chosen = both[:, ST * b:ST * (b + 1)].rearrange("p t e -> p (t e)")
                pe.matmul(bank(0)[:, 0:ST * E], below, chosen, start=True, stop=True)
                pe.matmul(bank(1)[:, 0:ST * E], ones6, chosen, start=True, stop=True).then_inc(count_pe, 1)

            def step4_pe(i, r, scan=True):
                nxt = (i + r, 1 - r)
                b = 2 * i + r
                if scan:
                    first_pe(*nxt)
                if b >= 1:
                    if scan:
                        pe.wait_ge(act_a, now(15, b + 1, 4))
                    else:
                        pe.wait_ge(dve_a, now(15, b, 15))
                    count(b - 1)
                second_pe(i, r)
                if scan:
                    if b >= 1:
                        pe.wait_ge(top6, (TOP_A + TOP_B) * (b - 1) + TOP_A + 2)
                    scan_pe_1(*nxt)
                    scan_pe_2(*nxt)
                up_pe(i, r)
                down_pe(i, r)
                if scan:
                    mix_pe(*nxt)
                turn_pe(i, r)
                logits_pe(i, r)

            first_pe(0, 0)
            scan_pe_1(0, 0)
            scan_pe_2(0, 0)
            mix_pe(0, 0)
            for i in range(B // 2 - 1):
                for r in range(2):
                    step4_pe(i, r)
            step4_pe(B // 2 - 1, 0)
            step4_pe(B // 2 - 1, 1, scan=False)
            meet(pe, 4)

            count(B - 1)
            pe.sem_inc(pe6, 6)
            pe.wait_ge(idx6, 2 * B)
            with pe.Fori(0, E // 2) as i:
                for r in range(2):
                    e = 2 * i + r
                    pe.wait_ge(e_in[r], 64 * (i + 1))
                    pe.wait_ge(act6, before(6, e, 1))
                    flip(bank(0, 2), xe_s[r], pe6)
                    pe.wait_ge(act6, now(6, e, 1))
                    for m in range(4):
                        pe.wait_ge(dve6, now(4, e, m - 1))
                        for w, at in ((we[r], 2), (ve[r], 3)):
                            for k in range(KD):
                                last = pe.matmul(bank(at + 2 * (m % 2)), w[:, k, m * P:(m + 1) * P], XT[:, k, :],
                                                 start=(k == 0), stop=(k == KD - 1))
                        last.then_inc(pe6, 1)
                    pe.wait_ge(dve6, now(4, e, 4))
                    pe.wait_ge(act6, before(6, e, 6))
                    for j in range(TPC):
                        for m in range(4):
                            last = pe.matmul(bank(6, 2)[:, j * D:(j + 1) * D], h6[:, m, j * P:(j + 1) * P], woe[r][:, m, :],
                                             start=(m == 0), stop=(m == 3))
                    last.then_inc(pe6, 1)
            meet(pe, 5)


_OUTS = [((B, S, D), "float32")]


def kernel(**inputs):
    import numpy as _np
    import concourse.bacc as _bacc
    from concourse import mybir as _mybir
    from concourse.bass_utils import run_bass_kernel_spmd as _run

    nc = _bacc.Bacc("TRN2", target_bir_lowering=False, num_devices=1)
    arrays, t = {}, {}
    for name in inputs:
        a = _np.ascontiguousarray(inputs[name])
        arrays["in_" + name] = a
        t[name] = nc.dram_tensor("in_" + name, a.shape, _mybir.dt.from_np(a.dtype), kind="ExternalInput").ap()
    out = nc.dram_tensor("out", (B, S, D), F32, kind="ExternalOutput").ap()
    build_program(nc, t, out)
    r = _run(nc, [arrays], core_ids=[0])
    return r.results[0]["out"]
```
